# Optimizing a Trainium2 kernel written in Bass

```python
import numpy as np
import jax
import jax.numpy as jnp

def _softmax(x, axis=-1):
    return jax.nn.softmax(x, axis=axis)

def _gelu(x):
    return jax.nn.gelu(x, approximate=True)

def _silu(x):
    return jax.nn.silu(x)

def _sigmoid(x):
    return jax.nn.sigmoid(x)

def _layernorm(x, axis=-1, eps=1e-05):
    m = jnp.mean(x, axis=axis, keepdims=True)
    v = jnp.var(x, axis=axis, keepdims=True)
    return (x - m) / jnp.sqrt(v + eps)

def _scatter_add(tgt, idx, src, axis=0):
    return tgt.at[idx].add(src)

def _segment_sum(src, seg, n):
    return jax.ops.segment_sum(src, seg, n)
kernel_name = 'mk_cond_seq_d4_seqx_r8_135526'

def setup_inputs(seed: int=0):
    np.random.seed(seed)
    _w = jnp.asarray

    def _rec_inputs():
        import jax
        import jax.numpy as jnp
        _rk = jax.random.key(seed)
        x = 1.648e-05 + 1 * jax.random.normal(jax.random.fold_in(_rk, 1), (2, 512, 128), jnp.float32)
        _lenS = 512 - jax.random.randint(jax.random.fold_in(_rk, 7), (2,), 0, max(1, 512 // 4) + 1, jnp.int32)
        _lenS2 = 512 - jax.random.randint(jax.random.fold_in(_rk, 8), (2,), 0, max(1, 512 // 4) + 1, jnp.int32)
        cond_1024 = 0.00191187 + 0.999416 * jax.random.normal(jax.random.fold_in(_rk, 11), (2, 128), jnp.float32)
        _validS = jnp.arange(512)[None, :] < _lenS[:, None]
        _validS2 = jnp.arange(512)[None, :] < _lenS2[:, None]
        _causal = jnp.tril(jnp.ones((512, 512), dtype=bool))
        mask_BxSxSx11_ik0 = jnp.where(jnp.ones((2, 512, 512, 11), dtype=bool), 0, 1).astype(jnp.int32)
        return (x, cond_1024, mask_BxSxSx11_ik0)
    x, cond_1024, mask_BxSxSx11_ik0 = _rec_inputs()

    def _L0_cond_setup():
        import jax, jax.numpy as jnp
        import numpy as np
        NONGT = 20
        H = 16
        NEG = -9000000000000000.0

        def _gat_attention(self_feat, cond_adj, label_bias, Wq, bq, Wk, bk, Wout, bout):
            B, N, F = self_feat.shape
            ng = min(NONGT, N)
            dh = F // H
            kv = self_feat[:, :ng]
            qh = (self_feat @ Wq.T + bq).reshape(B, N, H, dh)
            kh = (kv @ Wk.T + bk).reshape(B, ng, H, dh)
            aff = jnp.einsum('bnhd,bmhd->bnhm', qh, kh) * (1.0 / np.sqrt(dh))
            mask = cond_adj[:, :, None, :] > 0
            aff = jnp.where(mask, aff, NEG) + label_bias[:, :, None, :]
            w = jax.nn.softmax(aff, axis=-1)
            out_t = jnp.einsum('bnhm,bmf->bnhf', w, kv)
            out = jnp.einsum('bnhf,hgf->bnhg', out_t, Wout) + bout.reshape(H, F // H)
            return out.reshape(B, N, F)

        def _forward(v, q, adj, W_self, b_self, w_bias, b_bias, Wq, bq, Wk, bk, Wout, bout):
            adj_f = adj.astype(jnp.float32)
            exp_v = v
            row_zero = exp_v.sum(-1) == 0
            q_exp = jnp.where(row_zero[..., None], 0.0, q[:, None, :])
            vcq = jnp.concatenate([exp_v, q_exp], axis=-1)
            self_feat = vcq @ W_self.T + b_self
            output = self_feat
            for d in range(2):
                A = adj_f if d == 0 else jnp.swapaxes(adj_f, 1, 2)
                A = A[:, :, :NONGT, :]
                cond = A.sum(-1)
                vb = A @ w_bias + b_bias
                output = output + _gat_attention(self_feat, cond, vb, Wq[d], bq[d], Wk[d], bk[d], Wout[d], bout[d])
            rel = jax.nn.relu(output)
            return exp_v + rel
        key = jax.random.key(seed)
        ks = jax.random.split(key, 8)
        B, N, L, F, Q = (32, 36, 11, 128, 128)
        IN = F + Q
        s = 0.02
        return {'v': jax.random.normal(ks[0], (B, N, F), jnp.float32), 'q': jax.random.normal(ks[1], (B, Q), jnp.float32), 'adj': jax.random.randint(ks[2], (B, N, N, L), 0, 2, jnp.int32), 'W_self': jax.random.normal(ks[3], (F, IN), jnp.float32) * s, 'b_self': jnp.zeros((F,), jnp.float32), 'w_bias': jax.random.normal(ks[4], (L,), jnp.float32) * s, 'b_bias': jnp.zeros((), jnp.float32), 'Wq': jax.random.normal(ks[5], (2, F, F), jnp.float32) * s, 'bq': jnp.zeros((2, F), jnp.float32), 'Wk': jax.random.normal(ks[6], (2, F, F), jnp.float32) * s, 'bk': jnp.zeros((2, F), jnp.float32), 'Wout': jax.random.normal(ks[7], (2, H, F // H, F), jnp.float32) * s, 'bout': jnp.zeros((2, F), jnp.float32)}
    _L0_cond_all = _L0_cond_setup()
    _L0_cond_in = {k: v for k, v in _L0_cond_all.items() if k in ('W_self', 'b_self', 'w_bias', 'b_bias', 'Wq', 'bq', 'Wk', 'bk', 'Wout', 'bout')}
    del _L0_cond_all

    def _L1_cond_setup():
        import jax, jax.numpy as jnp
        import numpy as np
        D = 128
        H = 8
        WIN = 128
        DH = D // H
        EPS = 1e-05

        def _rmsnorm(x, scale):
            xf = x.astype(jnp.float32)
            var = jnp.mean(jnp.square(xf), axis=-1, keepdims=True)
            return (xf * jax.lax.rsqrt(var + EPS) * scale.astype(jnp.float32)).astype(x.dtype)

        def _rope(x):
            S, Dh = (x.shape[1], x.shape[3])
            freqs = 1.0 / 10000.0 ** (jnp.arange(0, Dh, 2, dtype=jnp.float32) / Dh)
            ang = jnp.arange(S, dtype=jnp.float32)[:, None] * freqs[None, :]
            sin = jnp.repeat(jnp.sin(ang), 2, axis=-1)[None, :, None, :]
            cos = jnp.repeat(jnp.cos(ang), 2, axis=-1)[None, :, None, :]
            x1, x2 = jnp.split(x, 2, axis=-1)
            rot = jnp.concatenate([-x2, x1], axis=-1)
            return x * cos + rot * sin
        key = jax.random.key(seed)
        ks = jax.random.split(key, 16)
        s = 0.02
        return {'group_x': jax.random.normal(ks[0], (8, 512, D), jnp.float32), 'context': jax.random.normal(ks[1], (8, D), jnp.float32), 'W_ada': jax.random.normal(ks[2], (D, 6 * D), jnp.float32) * s, 'b_ada': jnp.zeros((6 * D,), jnp.float32), 'scale1': jnp.ones((D,), jnp.float32), 'W_qkv': jax.random.normal(ks[3], (D, 3 * D), jnp.float32) * s, 'b_qkv': jnp.zeros((3 * D,), jnp.float32), 'W_out': jax.random.normal(ks[4], (D, D), jnp.float32) * s, 'b_out': jnp.zeros((D,), jnp.float32), 'scale2': jnp.ones((D,), jnp.float32), 'W_ff1': jax.random.normal(ks[5], (D, 4 * D), jnp.float32) * s, 'b_ff1': jnp.zeros((4 * D,), jnp.float32), 'W_ff2': jax.random.normal(ks[6], (4 * D, D), jnp.float32) * s, 'b_ff2': jnp.zeros((D,), jnp.float32)}
    _L1_cond_all = _L1_cond_setup()
    _L1_cond_in = {k: v for k, v in _L1_cond_all.items() if k in ('W_ada', 'b_ada', 'scale1', 'W_qkv', 'b_qkv', 'W_out', 'b_out', 'scale2', 'W_ff1', 'b_ff1', 'W_ff2', 'b_ff2')}
    del _L1_cond_all

    def _L2_cond_setup():
        import jax, jax.numpy as jnp
        import numpy as np
        B, L, D, P = (8, 256, 128, 32)

        def _ln(x):
            m = x.mean(-1, keepdims=True)
            v = x.var(-1, keepdims=True)
            return (x - m) * jax.lax.rsqrt(v + 1e-05)

        def _s5(u, Lam_re, Lam_im, B_re, B_im, C_re, C_im, D_diag, log_step):
            Lam = Lam_re + 1j * Lam_im
            dt = jnp.exp(log_step)
            Lam_bar = jnp.exp(Lam * dt)
            Bc = B_re + 1j * B_im
            B_bar = ((Lam_bar - 1.0) / Lam)[:, None] * Bc
            Bu = jnp.einsum('bld,pd->blp', u.astype(B_bar.dtype), B_bar)
            A = jnp.broadcast_to(Lam_bar, Bu.shape)

            def binop(e1, e2):
                a1, b1 = e1
                a2, b2 = e2
                return (a1 * a2, a2 * b1 + b2)
            _, xs = jax.lax.associative_scan(binop, (A, Bu), axis=1)
            Cc = C_re + 1j * C_im
            return 2.0 * jnp.einsum('blp,dp->bld', xs, Cc).real + D_diag * u
        key = jax.random.key(seed)
        ks = jax.random.split(key, 16)
        inp = {'y': jax.random.normal(ks[0], (B, L, D), jnp.float32), 't': jax.random.normal(ks[1], (B, D), jnp.float32), 'Wm': jax.random.normal(ks[2], (D, 6 * D), jnp.float32) * 0.02, 'bm': jax.random.normal(ks[3], (6 * D,), jnp.float32) * 0.02, 'Lam_re': -0.5 * jnp.ones((P,), jnp.float32), 'Lam_im': jnp.pi * jnp.arange(P, dtype=jnp.float32), 'B_re': jax.random.normal(ks[4], (P, D), jnp.float32) / np.sqrt(D), 'B_im': jax.random.normal(ks[5], (P, D), jnp.float32) / np.sqrt(D), 'C_re': jax.random.normal(ks[6], (D, P), jnp.float32) / np.sqrt(P), 'C_im': jax.random.normal(ks[7], (D, P), jnp.float32) / np.sqrt(P), 'D_diag': jax.random.normal(ks[8], (D,), jnp.float32), 'log_step': jax.random.uniform(ks[9], (P,), jnp.float32, np.log(0.001), np.log(0.1)), 'Wc': jax.random.normal(ks[10], (D, 2 * D), jnp.float32) * 0.02, 'bc': jax.random.normal(ks[11], (2 * D,), jnp.float32) * 0.02, 'W1': jax.random.normal(ks[12], (D, 4 * D), jnp.float32) / np.sqrt(D), 'b1': jnp.zeros((4 * D,), jnp.float32), 'W2': jax.random.normal(ks[13], (4 * D, D), jnp.float32) / np.sqrt(4 * D) * 0.1, 'b2': jnp.zeros((D,), jnp.float32)}
        return inp
    _L2_cond_all = _L2_cond_setup()
    _L2_cond_in = {k: v for k, v in _L2_cond_all.items() if k in ('Wm', 'bm', 'Lam_re', 'Lam_im', 'B_re', 'B_im', 'C_re', 'C_im', 'D_diag', 'log_step', 'Wc', 'bc', 'W1', 'b1', 'W2', 'b2')}
    del _L2_cond_all

    def _L3_cond_setup():
        import jax, jax.numpy as jnp
        import numpy as np
        EPS = float(np.finfo(np.float32).eps)

        def _rmsnorm(x, g):
            return x * jax.lax.rsqrt(jnp.mean(x * x, axis=-1, keepdims=True) + EPS) * g

        def _silu(x):
            return x * jax.nn.sigmoid(x)

        def _swiglu(x):
            a, gate = jnp.split(x, 2, axis=-1)
            return a * _silu(gate)

        def _rope(x):
            T, hd = (x.shape[1], x.shape[-1])
            inv_freq = 1.0 / 10000.0 ** (jnp.arange(0, hd, 2, dtype=jnp.float32) / hd)
            ang = jnp.arange(T, dtype=jnp.float32)[:, None] * inv_freq[None, :]
            cos = jnp.cos(ang)[None, :, None, :]
            sin = jnp.sin(ang)[None, :, None, :]
            x0, x1 = (x[..., 0::2], x[..., 1::2])
            o0 = x0 * cos - x1 * sin
            o1 = x1 * cos + x0 * sin
            return jnp.stack([o0, o1], axis=-1).reshape(x.shape)

        def _mha(x, w_qkv, b_qkv, w_ao, b_ao, n_head):
            B, T, C = x.shape
            hd = C // n_head
            qkv = x @ w_qkv + b_qkv
            q, k, v = jnp.split(qkv, 3, axis=-1)
            q = _rope(q.reshape(B, T, n_head, hd)).transpose(0, 2, 1, 3)
            k = _rope(k.reshape(B, T, n_head, hd)).transpose(0, 2, 1, 3)
            v = v.reshape(B, T, n_head, hd).transpose(0, 2, 1, 3)
            attn = jnp.einsum('bhqd,bhkd->bhqk', q, k) * (1.0 / np.sqrt(hd))
            attn = jax.nn.softmax(attn, axis=-1)
            out = jnp.einsum('bhqk,bhkd->bhqd', attn, v)
            out = out.transpose(0, 2, 1, 3).reshape(B, T, C)
            return out @ w_ao + b_ao

        def _ffn(x, w_fc, b_fc, w_fo, b_fo):
            return _swiglu(x @ w_fc + b_fc) @ w_fo + b_fo
        key = jax.random.key(seed)
        ks = jax.random.split(key, 10)
        B, T, D, H = (2, 256, 128, 16)
        s = 0.02
        return {'x': jax.random.normal(ks[0], (B, T, D), jnp.float32), 'time_emb': jax.random.normal(ks[1], (B, D), jnp.float32), 'g1': jnp.ones((D,), jnp.float32), 'g2': jnp.ones((D,), jnp.float32), 'w_qkv': jax.random.normal(ks[2], (D, 3 * D), jnp.float32) * s, 'b_qkv': jnp.zeros((3 * D,), jnp.float32), 'w_ao': jax.random.normal(ks[3], (D, D), jnp.float32) * s, 'b_ao': jnp.zeros((D,), jnp.float32), 'w_fc': jax.random.normal(ks[4], (D, 8 * D), jnp.float32) * s, 'b_fc': jnp.zeros((8 * D,), jnp.float32), 'w_fo': jax.random.normal(ks[5], (4 * D, D), jnp.float32) * s, 'b_fo': jnp.zeros((D,), jnp.float32), 'w_t1': jax.random.normal(ks[6], (D, 2 * D), jnp.float32) * s, 'b_t1': jnp.zeros((2 * D,), jnp.float32), 'w_t2': jax.random.normal(ks[7], (D, 4 * D), jnp.float32) * s, 'b_t2': jnp.zeros((4 * D,), jnp.float32)}
    _L3_cond_all = _L3_cond_setup()
    _L3_cond_in = {k: v for k, v in _L3_cond_all.items() if k in ('g1', 'g2', 'w_qkv', 'b_qkv', 'w_ao', 'b_ao', 'w_fc', 'b_fc', 'w_fo', 'b_fo', 'w_t1', 'b_t1', 'w_t2', 'b_t2')}
    del _L3_cond_all
    return {'x': x, 'cond_1024': cond_1024, 'mask_BxSxSx11_ik0': mask_BxSxSx11_ik0, 'L0_cond_W_self': _L0_cond_in['W_self'], 'L0_cond_b_self': _L0_cond_in['b_self'], 'L0_cond_w_bias': _L0_cond_in['w_bias'], 'L0_cond_b_bias': _L0_cond_in['b_bias'], 'L0_cond_Wq': _L0_cond_in['Wq'], 'L0_cond_bq': _L0_cond_in['bq'], 'L0_cond_Wk': _L0_cond_in['Wk'], 'L0_cond_bk': _L0_cond_in['bk'], 'L0_cond_Wout': _L0_cond_in['Wout'], 'L0_cond_bout': _L0_cond_in['bout'], 'L1_cond_W_ada': _L1_cond_in['W_ada'], 'L1_cond_b_ada': _L1_cond_in['b_ada'], 'L1_cond_scale1': _L1_cond_in['scale1'], 'L1_cond_W_qkv': _L1_cond_in['W_qkv'], 'L1_cond_b_qkv': _L1_cond_in['b_qkv'], 'L1_cond_W_out': _L1_cond_in['W_out'], 'L1_cond_b_out': _L1_cond_in['b_out'], 'L1_cond_scale2': _L1_cond_in['scale2'], 'L1_cond_W_ff1': _L1_cond_in['W_ff1'], 'L1_cond_b_ff1': _L1_cond_in['b_ff1'], 'L1_cond_W_ff2': _L1_cond_in['W_ff2'], 'L1_cond_b_ff2': _L1_cond_in['b_ff2'], 'L2_cond_Wm': _L2_cond_in['Wm'], 'L2_cond_bm': _L2_cond_in['bm'], 'L2_cond_Lam_re': _L2_cond_in['Lam_re'], 'L2_cond_Lam_im': _L2_cond_in['Lam_im'], 'L2_cond_B_re': _L2_cond_in['B_re'], 'L2_cond_B_im': _L2_cond_in['B_im'], 'L2_cond_C_re': _L2_cond_in['C_re'], 'L2_cond_C_im': _L2_cond_in['C_im'], 'L2_cond_D_diag': _L2_cond_in['D_diag'], 'L2_cond_log_step': _L2_cond_in['log_step'], 'L2_cond_Wc': _L2_cond_in['Wc'], 'L2_cond_bc': _L2_cond_in['bc'], 'L2_cond_W1': _L2_cond_in['W1'], 'L2_cond_b1': _L2_cond_in['b1'], 'L2_cond_W2': _L2_cond_in['W2'], 'L2_cond_b2': _L2_cond_in['b2'], 'L3_cond_g1': _L3_cond_in['g1'], 'L3_cond_g2': _L3_cond_in['g2'], 'L3_cond_w_qkv': _L3_cond_in['w_qkv'], 'L3_cond_b_qkv': _L3_cond_in['b_qkv'], 'L3_cond_w_ao': _L3_cond_in['w_ao'], 'L3_cond_b_ao': _L3_cond_in['b_ao'], 'L3_cond_w_fc': _L3_cond_in['w_fc'], 'L3_cond_b_fc': _L3_cond_in['b_fc'], 'L3_cond_w_fo': _L3_cond_in['w_fo'], 'L3_cond_b_fo': _L3_cond_in['b_fo'], 'L3_cond_w_t1': _L3_cond_in['w_t1'], 'L3_cond_b_t1': _L3_cond_in['b_t1'], 'L3_cond_w_t2': _L3_cond_in['w_t2'], 'L3_cond_b_t2': _L3_cond_in['b_t2']}

def reference(x, cond_1024, mask_BxSxSx11_ik0, L0_cond_W_self, L0_cond_b_self, L0_cond_w_bias, L0_cond_b_bias, L0_cond_Wq, L0_cond_bq, L0_cond_Wk, L0_cond_bk, L0_cond_Wout, L0_cond_bout, L1_cond_W_ada, L1_cond_b_ada, L1_cond_scale1, L1_cond_W_qkv, L1_cond_b_qkv, L1_cond_W_out, L1_cond_b_out, L1_cond_scale2, L1_cond_W_ff1, L1_cond_b_ff1, L1_cond_W_ff2, L1_cond_b_ff2, L2_cond_Wm, L2_cond_bm, L2_cond_Lam_re, L2_cond_Lam_im, L2_cond_B_re, L2_cond_B_im, L2_cond_C_re, L2_cond_C_im, L2_cond_D_diag, L2_cond_log_step, L2_cond_Wc, L2_cond_bc, L2_cond_W1, L2_cond_b1, L2_cond_W2, L2_cond_b2, L3_cond_g1, L3_cond_g2, L3_cond_w_qkv, L3_cond_b_qkv, L3_cond_w_ao, L3_cond_b_ao, L3_cond_w_fc, L3_cond_b_fc, L3_cond_w_fo, L3_cond_b_fo, L3_cond_w_t1, L3_cond_b_t1, L3_cond_w_t2, L3_cond_b_t2):
    import jax
    import jax.numpy as jnp

    def _L0_cond_ref(v, q, adj, W_self, b_self, w_bias, b_bias, Wq, bq, Wk, bk, Wout, bout):
        import jax, jax.numpy as jnp
        import numpy as np
        NONGT = 20
        H = 16
        NEG = -9000000000000000.0

        def _gat_attention(self_feat, cond_adj, label_bias, Wq, bq, Wk, bk, Wout, bout):
            B, N, F = self_feat.shape
            ng = min(NONGT, N)
            dh = F // H
            kv = self_feat[:, :ng]
            qh = (self_feat @ Wq.T + bq).reshape(B, N, H, dh)
            kh = (kv @ Wk.T + bk).reshape(B, ng, H, dh)
            aff = jnp.einsum('bnhd,bmhd->bnhm', qh, kh) * (1.0 / np.sqrt(dh))
            mask = cond_adj[:, :, None, :] > 0
            aff = jnp.where(mask, aff, NEG) + label_bias[:, :, None, :]
            w = jax.nn.softmax(aff, axis=-1)
            out_t = jnp.einsum('bnhm,bmf->bnhf', w, kv)
            out = jnp.einsum('bnhf,hgf->bnhg', out_t, Wout) + bout.reshape(H, F // H)
            return out.reshape(B, N, F)

        def _forward(v, q, adj, W_self, b_self, w_bias, b_bias, Wq, bq, Wk, bk, Wout, bout):
            adj_f = adj.astype(jnp.float32)
            exp_v = v
            row_zero = exp_v.sum(-1) == 0
            q_exp = jnp.where(row_zero[..., None], 0.0, q[:, None, :])
            vcq = jnp.concatenate([exp_v, q_exp], axis=-1)
            self_feat = vcq @ W_self.T + b_self
            output = self_feat
            for d in range(2):
                A = adj_f if d == 0 else jnp.swapaxes(adj_f, 1, 2)
                A = A[:, :, :NONGT, :]
                cond = A.sum(-1)
                vb = A @ w_bias + b_bias
                output = output + _gat_attention(self_feat, cond, vb, Wq[d], bq[d], Wk[d], bk[d], Wout[d], bout[d])
            rel = jax.nn.relu(output)
            return exp_v + rel
        return _forward(v, q, adj, W_self, b_self, w_bias, b_bias, Wq, bq, Wk, bk, Wout, bout)

    def _L1_cond_ref(group_x, context, W_ada, b_ada, scale1, W_qkv, b_qkv, W_out, b_out, scale2, W_ff1, b_ff1, W_ff2, b_ff2):
        import jax, jax.numpy as jnp
        import numpy as np
        D = 128
        H = 8
        WIN = 128
        DH = D // H
        EPS = 1e-05

        def _rmsnorm(x, scale):
            xf = x.astype(jnp.float32)
            var = jnp.mean(jnp.square(xf), axis=-1, keepdims=True)
            return (xf * jax.lax.rsqrt(var + EPS) * scale.astype(jnp.float32)).astype(x.dtype)

        def _rope(x):
            S, Dh = (x.shape[1], x.shape[3])
            freqs = 1.0 / 10000.0 ** (jnp.arange(0, Dh, 2, dtype=jnp.float32) / Dh)
            ang = jnp.arange(S, dtype=jnp.float32)[:, None] * freqs[None, :]
            sin = jnp.repeat(jnp.sin(ang), 2, axis=-1)[None, :, None, :]
            cos = jnp.repeat(jnp.cos(ang), 2, axis=-1)[None, :, None, :]
            x1, x2 = jnp.split(x, 2, axis=-1)
            rot = jnp.concatenate([-x2, x1], axis=-1)
            return x * cos + rot * sin
        B, L, _ = group_x.shape
        nw = L // WIN
        ada = jax.nn.silu(context) @ W_ada + b_ada
        sh_msa, sc_msa, g_msa, sh_mlp, sc_mlp, g_mlp = jnp.split(ada, 6, axis=-1)
        sh_msa, sc_msa, g_msa = (sh_msa[:, None], sc_msa[:, None], g_msa[:, None])
        sh_mlp, sc_mlp, g_mlp = (sh_mlp[:, None], sc_mlp[:, None], g_mlp[:, None])
        res = group_x
        x = _rmsnorm(group_x, scale1)
        x = x * (1 + sc_msa) + sh_msa
        xw = x.reshape(B * nw, WIN, D)
        qkv = xw @ W_qkv + b_qkv
        q, k, v = jnp.split(qkv, 3, axis=-1)
        q = _rope(q.reshape(B * nw, WIN, H, DH))
        k = _rope(k.reshape(B * nw, WIN, H, DH))
        v = v.reshape(B * nw, WIN, H, DH)
        scores = jnp.einsum('bqhd,bkhd->bhqk', q, k) / jnp.sqrt(jnp.float32(DH))
        attn = jax.nn.softmax(scores, axis=-1)
        o = jnp.einsum('bhqk,bkhd->bqhd', attn, v).reshape(B, L, D)
        o = o @ W_out + b_out
        x = res + g_msa * o
        res = x
        h = _rmsnorm(x, scale2)
        h = h * (1 + sc_mlp) + sh_mlp
        h = jax.nn.gelu(h @ W_ff1 + b_ff1)
        h = h @ W_ff2 + b_ff2
        return res + g_mlp * h

    def _L2_cond_ref(y, t, Wm, bm, Lam_re, Lam_im, B_re, B_im, C_re, C_im, D_diag, log_step, Wc, bc, W1, b1, W2, b2):
        import jax, jax.numpy as jnp
        import numpy as np
        B, L, D, P = (8, 256, 128, 32)

        def _ln(x):
            m = x.mean(-1, keepdims=True)
            v = x.var(-1, keepdims=True)
            return (x - m) * jax.lax.rsqrt(v + 1e-05)

        def _s5(u, Lam_re, Lam_im, B_re, B_im, C_re, C_im, D_diag, log_step):
            Lam = Lam_re + 1j * Lam_im
            dt = jnp.exp(log_step)
            Lam_bar = jnp.exp(Lam * dt)
            Bc = B_re + 1j * B_im
            B_bar = ((Lam_bar - 1.0) / Lam)[:, None] * Bc
            Bu = jnp.einsum('bld,pd->blp', u.astype(B_bar.dtype), B_bar)
            A = jnp.broadcast_to(Lam_bar, Bu.shape)

            def binop(e1, e2):
                a1, b1 = e1
                a2, b2 = e2
                return (a1 * a2, a2 * b1 + b2)
            _, xs = jax.lax.associative_scan(binop, (A, Bu), axis=1)
            Cc = C_re + 1j * C_im
            return 2.0 * jnp.einsum('blp,dp->bld', xs, Cc).real + D_diag * u
        mod = t @ Wm + bm
        shift_a, scale_a, gate_a, shift_ff, scale_ff, gate_ff = jnp.split(mod, 6, axis=-1)
        y_mod = _ln(y) * (1 + scale_a[:, None]) + shift_a[:, None]
        a_y = _s5(y_mod, Lam_re, Lam_im, B_re, B_im, C_re, C_im, D_diag, log_step)
        y = y + gate_a[:, None] * a_y
        cond = t @ Wc + bc
        scale_c, shift_c = jnp.split(cond, 2, axis=-1)
        y_norm = _ln(y) * (1 + scale_c[:, None]) + shift_c[:, None]
        y_mod = y_norm * (1 + scale_ff[:, None]) + shift_ff[:, None]
        h = jax.nn.gelu(y_mod @ W1 + b1)
        ff_y = h @ W2 + b2
        return y + gate_ff[:, None] * ff_y

    def _L3_cond_ref(x, time_emb, g1, g2, w_qkv, b_qkv, w_ao, b_ao, w_fc, b_fc, w_fo, b_fo, w_t1, b_t1, w_t2, b_t2):
        import jax, jax.numpy as jnp
        import numpy as np
        EPS = float(np.finfo(np.float32).eps)

        def _rmsnorm(x, g):
            return x * jax.lax.rsqrt(jnp.mean(x * x, axis=-1, keepdims=True) + EPS) * g

        def _silu(x):
            return x * jax.nn.sigmoid(x)

        def _swiglu(x):
            a, gate = jnp.split(x, 2, axis=-1)
            return a * _silu(gate)

        def _rope(x):
            T, hd = (x.shape[1], x.shape[-1])
            inv_freq = 1.0 / 10000.0 ** (jnp.arange(0, hd, 2, dtype=jnp.float32) / hd)
            ang = jnp.arange(T, dtype=jnp.float32)[:, None] * inv_freq[None, :]
            cos = jnp.cos(ang)[None, :, None, :]
            sin = jnp.sin(ang)[None, :, None, :]
            x0, x1 = (x[..., 0::2], x[..., 1::2])
            o0 = x0 * cos - x1 * sin
            o1 = x1 * cos + x0 * sin
            return jnp.stack([o0, o1], axis=-1).reshape(x.shape)

        def _mha(x, w_qkv, b_qkv, w_ao, b_ao, n_head):
            B, T, C = x.shape
            hd = C // n_head
            qkv = x @ w_qkv + b_qkv
            q, k, v = jnp.split(qkv, 3, axis=-1)
            q = _rope(q.reshape(B, T, n_head, hd)).transpose(0, 2, 1, 3)
            k = _rope(k.reshape(B, T, n_head, hd)).transpose(0, 2, 1, 3)
            v = v.reshape(B, T, n_head, hd).transpose(0, 2, 1, 3)
            attn = jnp.einsum('bhqd,bhkd->bhqk', q, k) * (1.0 / np.sqrt(hd))
            attn = jax.nn.softmax(attn, axis=-1)
            out = jnp.einsum('bhqk,bhkd->bhqd', attn, v)
            out = out.transpose(0, 2, 1, 3).reshape(B, T, C)
            return out @ w_ao + b_ao

        def _ffn(x, w_fc, b_fc, w_fo, b_fo):
            return _swiglu(x @ w_fc + b_fc) @ w_fo + b_fo
        n_head = 16
        tp = _swiglu(time_emb @ w_t1 + b_t1) @ w_t2 + b_t2
        shift1, scale1, shift2, scale2 = jnp.split(tp, 4, axis=-1)
        h = _rmsnorm(x, g1) * (1.0 + scale1[:, None, :]) + shift1[:, None, :]
        x = x + _mha(h, w_qkv, b_qkv, w_ao, b_ao, n_head)
        h = _rmsnorm(x, g2) * (1.0 + scale2[:, None, :]) + shift2[:, None, :]
        x = x + _ffn(h, w_fc, b_fc, w_fo, b_fo)
        return x
    x = _L0_cond_ref(x, cond_1024, mask_BxSxSx11_ik0, L0_cond_W_self, L0_cond_b_self, L0_cond_w_bias, L0_cond_b_bias, L0_cond_Wq, L0_cond_bq, L0_cond_Wk, L0_cond_bk, L0_cond_Wout, L0_cond_bout)
    x = _L1_cond_ref(x, cond_1024, L1_cond_W_ada, L1_cond_b_ada, L1_cond_scale1, L1_cond_W_qkv, L1_cond_b_qkv, L1_cond_W_out, L1_cond_b_out, L1_cond_scale2, L1_cond_W_ff1, L1_cond_b_ff1, L1_cond_W_ff2, L1_cond_b_ff2)
    x = _L2_cond_ref(x, cond_1024, L2_cond_Wm, L2_cond_bm, L2_cond_Lam_re, L2_cond_Lam_im, L2_cond_B_re, L2_cond_B_im, L2_cond_C_re, L2_cond_C_im, L2_cond_D_diag, L2_cond_log_step, L2_cond_Wc, L2_cond_bc, L2_cond_W1, L2_cond_b1, L2_cond_W2, L2_cond_b2)
    x = _L3_cond_ref(x, cond_1024, L3_cond_g1, L3_cond_g2, L3_cond_w_qkv, L3_cond_b_qkv, L3_cond_w_ao, L3_cond_b_ao, L3_cond_w_fc, L3_cond_b_fc, L3_cond_w_fo, L3_cond_b_fo, L3_cond_w_t1, L3_cond_b_t1, L3_cond_w_t2, L3_cond_b_t2)
    return x

_drawn_inputs = setup_inputs


def setup_inputs(seed=0):
    import zlib

    import numpy as np

    out = dict(_drawn_inputs(seed))
    spreads = {'L0_cond_b_self': (0.0, 0.1),
     'L0_cond_bq': (0.0, 0.1),
     'L0_cond_bk': (0.0, 0.1),
     'L0_cond_bout': (0.0, 0.1),
     'L1_cond_b_ada': (0.0, 0.545),
     'L1_cond_scale1': (1.0, 0.6),
     'L1_cond_b_qkv': (0.0, 0.8),
     'L1_cond_b_out': (0.0, 0.583),
     'L1_cond_scale2': (1.0, 0.6),
     'L1_cond_b_ff1': (0.0, 0.8),
     'L1_cond_b_ff2': (0.0, 0.528),
     'L2_cond_Lam_re': (-0.5, 0.6),
     'L2_cond_b1': (0.0, 0.8),
     'L2_cond_b2': (0.0, 0.376),
     'L3_cond_g1': (1.0, 0.6),
     'L3_cond_g2': (1.0, 0.6),
     'L3_cond_b_qkv': (0.0, 0.386),
     'L3_cond_b_ao': (0.0, 0.384),
     'L3_cond_b_fc': (0.0, 0.8),
     'L3_cond_b_fo': (0.0, 2.0),
     'L3_cond_b_t1': (0.0, 0.8),
     'L3_cond_b_t2': (0.0, 0.8)}
    factors = {'L1_cond_W_ada': 2.944,
     'L1_cond_W_qkv': 8.0,
     'L1_cond_W_out': 8.0,
     'L1_cond_W_ff1': 6.13,
     'L1_cond_W_ff2': 5.535,
     'L2_cond_Wc': 8.0,
     'L2_cond_bc': 8.0,
     'L2_cond_W1': 4.339,
     'L2_cond_W2': 4.056,
     'L3_cond_w_qkv': 5.313,
     'L3_cond_w_fc': 4.071,
     'L3_cond_w_fo': 4.044,
     'L3_cond_w_t1': 8.0,
     'L3_cond_w_t2': 8.0}
    for name, (base, spread) in spreads.items():
        noise = np.random.default_rng([zlib.crc32(name.encode()), seed]).standard_normal(out[name].shape)
        drawn = base * np.exp(spread * noise) if base else spread * noise
        out[name] = jnp.asarray(drawn.astype(out[name].dtype))
    for name, factor in factors.items():
        out[name] = (out[name] * factor).astype(out[name].dtype)
    return out
```

```python
from contextlib import ExitStack

import concourse.bass as bass
from concourse import mybir

F32 = mybir.dt.float32
BF16 = mybir.dt.bfloat16
I32 = mybir.dt.int32
ALU = mybir.AluOpType
ACT = mybir.ActivationFunctionType
X_AXIS = mybir.AxisListType.X

P = 128
B, T, D = 2, 512, 128
NB = T // P
NT = B * NB
L, M0 = 11, 20
H0, H1, H3 = 16, 8, 16
HC = 6
NC0 = 3
RC = HC * M0
RLAST = H0 * M0 - 2 * RC
D1 = D // H1
D3 = D // H3
PAD = 32
G3 = 4
NG3 = H3 // G3
NIT = B * NG3
AUG = 96
NEG = -9000000000000000.0
ROUND = 1.5 * 2.0 ** 23
ROUND12 = 1.5 * 2.0 ** 11
TWO_PI = 6.283185307179586
TURN = (6.28125, 0.0019350051879882812, 3.0199159819e-07)

W0 = dict(ident=P, ones=P, wsv=P, wsq=P, wq=2 * P, wk=2 * P, wo=2 * P, kmask0=H0 * M0, vmask0=NC0 * P,
          bself=1, bq0=2, bk0=2, bout0=2, cond=2)
W1 = dict(wcol1=4 * P, wgate1=2 * P, wt1=2 * P, wqkv1=3 * P, wout1=P, wff1_1=4 * P, wff2_1=4 * P,
          kmask1=H1, cos1=D1, sin1=D1, bff1_1=4, bmod=12, bmodd=4, s1a=1, s1b=1, g3a=1, g3b=1)
W2 = dict(wcol2=6 * P, wgate2=2 * P, wff1_2=4 * P, wff2_2=4 * P, bx=P, by=P, cta=P, ctb=P, steps=T,
          lam_re=1, lam_im=1, log_step=1, sa=1, sb=1, sign1=2, sign2=2, dcol=1, bff1_2=4, halfpi=1)
W3 = dict(wcol3=4 * P, wqkv3=3 * P, wao=P, wfc=8 * P, wfo=4 * P, cos3=NB * 64, sin3=NB * 64, bfc=8)
ROWS = dict(wbias0=L, bbias0=1, rgate=4 * P, rqkv1=3 * P, rout1=P, rff2_1=P, rff2_2=P, rqkv3=3 * P,
            rao=P, rfo=P)


def build_program(nc, w0, w1, w2, w3, rows, xt_in, adj_in, out, q_scr, k_scr):
    with ExitStack() as ctx:
        sems = {}

        def sem(name):
            if name not in sems:
                sems[name] = ctx.enter_context(nc.semaphore(name))
            return sems[name]

        def sb(name, shape, dt=F32):
            return ctx.enter_context(nc.sbuf_tensor(name, shape, dt))

        def arena(name, words):
            return [sb(name, [P, words]), 0]

        def carve(a, shape, dt=F32):
            n = 1
            for k in shape[1:]:
                n *= k
            words = n if dt in (F32, I32) else n // 2
            v = a[0][0:shape[0], a[1]:a[1] + words]
            a[1] += words
            if dt is not F32:
                v = v.bitcast(dt)
            names = "abcd"[:len(shape) - 1]
            if len(names) > 1:
                v = v.rearrange(f"p ({' '.join(names)}) -> p {' '.join(names)}",
                                **{c: k for c, k in zip(names, shape[1:])})
            return v

        packed = {}
        tiles = {}
        for tag, spec in (("w0", W0), ("w1", W1), ("w2", W2), ("w3", W3), ("rw", ROWS)):
            n = sum(spec.values())
            tiles[tag] = sb(tag + "_sb", [P, n])
            at = 0
            for name, width in spec.items():
                packed[name] = tiles[tag][:, at:at + width]
                at += width

        def W(name):
            return packed[name]

        ident, ones = W("ident"), W("ones")
        attn = arena("attn", 23 * 1024)
        early = arena("early", 4 * 1024)
        mlp = arena("mlp", 4 * B * T)
        gT = carve(mlp, [P, 4, B * T])

        adj = [carve(attn, [P, NT * M0 * L], I32) for d in range(2)]
        adj_w = carve(attn, [P, NT * M0, L])
        msum = carve(attn, [P, 2, NT * M0])
        mbias = carve(attn, [P, 2, NT * M0])
        mask = carve(attn, [P, 2, NT * M0])
        mpen = carve(attn, [P, 2, NT * M0])
        mtb = carve(attn, [P, 2, NT * M0])
        qhT = [carve(attn, [P, B * T]) for d in range(2)]
        kblk = [carve(attn, [P, H0, M0]) for j in range(4)]
        kvrep = [carve(attn, [P, NC0 * HC, M0]) for b in range(B)]
        vblk = [carve(attn, [RC, NC0, P]) for j in range(4)]
        w0p = carve(attn, [P, 4, 2, H0 * M0])
        w0T = [carve(attn, [RC, NC0, T]) for j in range(4)]
        l0sum = carve(attn, [P, B, T])
        xoT = carve(attn, [P, B * T])
        xT = carve(early, [P, B * T])
        sfT = carve(early, [P, B * T])
        keep = carve(early, [1, B * T])
        qrow = carve(early, [1, B * P])
        bc_cond = carve(early, [P, B, P])
        bc_silu = carve(early, [P, B, P])
        col = sb("col", [P, 24])
        mx0 = sb("mx0", [P, 4, 2 * H0])
        sm0 = sb("sm0", [P, 4, 2 * H0])
        rs0 = sb("rs0", [P, 4, 2 * H0])
        bout_sum = sb("bout_sum", [P, 1])

        silu_c = sb("silu_c", [P, B])
        modc = sb("modc", [P, 12, B])
        modp = sb("modp", [P, 12, B])
        modd = sb("modd", [P, 4, B])
        modq = sb("modq", [P, 4, B])
        sgt = sb("sgt", [P, B])
        tpe = sb("tpe", [P, B])
        scl = sb("scl", [P, 6, B])
        shf = sb("shf", [P, 6, B])
        shtmp = sb("shtmp", [P, B])
        gate = sb("gate", [P, B, 4 * P])
        wout1g = sb("wout1g", [P, B, P])
        wff2g = [sb(f"wff2g{n}", [P, B, 4, P]) for n in range(2)]
        bres = sb("bres", [P, 3, B, P])

        X = sb("X", [P, NT, P])
        Xb = sb("Xb", [P, NT, P])
        st = sb("st", [P, NT, 6])
        mv = sb("mv", [P, NT, 2])
        msq = sb("msq", [P, NT])
        var = sb("var", [P, NT])
        rstd = sb("rstd", [P, NT])
        mhalf = sb("mhalf", [P, NT])
        xn = sb("xn", [P, NT, P])
        early[1] = 0
        qk = carve(early, [P, NT, 2 * P])
        hT = carve(early, [P, B * T])
        oT = carve(early, [P, B * T])

        attn[1] = 0
        v1 = carve(attn, [P, NT, H1, PAD])
        qkT1 = carve(attn, [P, 2, 2 * P])
        kb1 = carve(attn, [P, 2, H1, P])
        p1 = carve(attn, [P, 2, H1, P])
        pT1 = carve(attn, [P, 2, H1, P])
        os1 = carve(attn, [P, 2, 2, P])
        otok = carve(attn, [P, NT, P])
        mx1 = sb("mx1", [P, 2, H1])
        rc1 = sb("rc1", [P, 2, H1])

        attn[1] = 0
        v3 = carve(attn, [P, NIT, NB, G3, PAD])
        qa = [carve(attn, [P, G3, T], BF16) for j in range(2)]
        ka = [carve(attn, [P, G3, T], BF16) for j in range(2)]
        split = carve(attn, [P, 2 * B, 3, T], BF16)
        res3 = carve(attn, [P, 2 * B, T])
        tail = attn[1]
        p3 = carve(attn, [P, 2, G3, 2, T])
        o3 = carve(attn, [P, NB, NIT, G3 * D3])
        mlp[1] = 0
        vg = [carve(mlp, [P, NB, G3, PAD]) for j in range(2)]
        os3 = carve(mlp, [P, T])
        nm3 = sb("nm3", [P, G3 * NB])
        nr3 = sb("nr3", [P, G3 * NB])
        ms3 = sb("ms3", [P, P // (G3 * NB), G3 * NB], BF16)
        mT3 = sb("mT3", [3 * G3 * NB, P], BF16)
        identb = sb("identb", [P, P], BF16)
        rc3 = sb("rc3", [P, NB, G3])

        attn[1] = tail
        rt1 = carve(attn, [P, NT, 2 * P])
        rt2 = carve(attn, [P, NT, 2 * P])
        er = carve(attn, [P, T])
        ei = carve(attn, [P, T])
        tA = carve(attn, [P, T])
        tB = carve(attn, [P, T])
        uw = carve(attn, [P, T])
        uw2 = carve(attn, [P, T])
        xs = carve(attn, [P, T])
        bbar = carve(attn, [P, P])
        bbT = carve(attn, [P, P])
        cga = carve(attn, [P, B, P])
        cgb = carve(attn, [P, B, P])
        dg = carve(attn, [P, B, P])
        attn[1] = tail
        sg3 = carve(attn, [P, 2, T])

        PP = [ctx.enter_context(nc.psum_tensor(f"pp{j}", [P, 2, 512], F32)) for j in range(4)]

        def bank(k):
            return PP[k // 2][:, k % 2, :]

        block = ctx.enter_context(nc.Block())
        pe, dve, act, pool = nc.tensor, nc.vector, nc.scalar, nc.gpsimd

        def tile_cols(i):
            return slice(i * P, (i + 1) * P)

        def half(b):
            return slice(b * T, (b + 1) * T)

        def btiles(b):
            return slice(b * NB, (b + 1) * NB)

        @block.sync
        def _(sp):
            sp.dma_start(tiles["w0"][:, :], w0).then_inc(sem("ld_w0"), 16)
            sp.dma_start(adj[1][:, :], adj_in[1]).then_inc(sem("ld_adj1"), 16)
            sp.dma_start(tiles["w2"][:, :], w2).then_inc(sem("ld_w2"), 16)
            sp.dma_start(tiles["w3"][:, :], w3).then_inc(sem("ld_w3"), 16)

            for b in range(B):
                sp.wait_ge(sem("split3"), 2 * b + 1)
                for g in range(NG3):
                    sp.dma_start(q_scr[b * NG3 + g].rearrange("i p t -> p i t"),
                                 split[32 * g:32 * g + 32, 2 * b, :, :]).then_inc(sem("st_q"), 16)
                sp.wait_ge(sem("split3"), 2 * b + 2)
                for g in range(NG3):
                    it = b * NG3 + g
                    sp.dma_start(k_scr[it, 0:3].rearrange("i p t -> p i t"),
                                 split[32 * g:32 * g + 32, 2 * b + 1, :, :]).then_inc(sem("st_q"), 16)
                    sp.dma_start(k_scr[it, 3:5].rearrange("i p t -> p i t"),
                                 split[32 * g:32 * g + 32, 2 * b + 1, 0:2, :]).then_inc(sem("st_q"), 16)

            def load(it, par):
                for s in range(3):
                    qsrc = q_scr[bass.ds(it, 1)].rearrange("a i (d c) t -> (a i d) (c t)", c=G3)
                    ksrc = k_scr[bass.ds(it, 1), s:s + 3].rearrange("a i (d c) t -> (a i d) (c t)", c=G3)
                    r = slice(24 * s, 24 * s + 24)
                    sp.dma_start(qa[par][r, :, :].rearrange("p c t -> p (c t)"), qsrc).then_inc(sem(f"ld_qa{par}"), 16)
                    sp.dma_start(ka[par][r, :, :].rearrange("p c t -> p (c t)"), ksrc).then_inc(sem(f"ld_qa{par}"), 16)

            def maxima(it, par):
                sp.wait_ge(sem("mT3"), it + 1)
                for i in range(3):
                    sp.dma_start(qa[par][AUG + i:AUG + i + 1, :, :].rearrange("p c (w t) -> p (c w) t", w=NB),
                                 mT3[16 * i:16 * i + 16, :]).then_inc(sem(f"ld_m{par}"), 16)

            sp.wait_ge(sem("zero3"), 4)
            sp.wait_ge(sem("st_q"), 16 * 3 * NG3 * 1 + 16 * 3 * NG3)
            load(0, 0)
            maxima(0, 0)
            load(1, 1)
            with sp.Fori(0, NIT // 2 - 1) as pair:
                it = pair * 2
                maxima(it + 1, 1)
                sp.wait_ge(sem("st3"), it * 16 + 16)
                load(it + 2, 0)
                maxima(it + 2, 0)
                sp.wait_ge(sem("st3"), it * 16 + 32)
                load(it + 3, 1)
            maxima(NIT - 1, 1)

            for b in range(B):
                sp.wait_ge(sem("xr"), 2 * 5 + b + 1)
                sp.dma_start(out[:, b * T:(b + 1) * T], X[:, btiles(b), :].rearrange("p w f -> p (w f)"))\
                  .then_inc(sem("st_out"), 16)
            sp.wait_ge(sem("st_out"), 32)

        freed = {}

        def claim(eng, k, name, value):
            if k in freed:
                eng.wait_ge(sem(freed[k][0]), freed[k][1])
            freed[k] = (name, value)

        @block.tensor
        def _(eng):
            def mm(o, l, r, start=True, stop=True):
                return pe.matmul(o, l, r, start=start, stop=stop)

            eng.wait_ge(sem("ld_w0"), 16)
            eng.wait_ge(sem("ld_xT"), 16)
            for b in range(B):
                claim(eng, 6 + b, "keep", b + 1)
                mm(bank(6 + b)[0:1, :], ones[:, 0:1], xT[:, half(b)]).then_inc(sem("rowsum"), 1)
            claim(eng, 5, "qrow", 1)
            for b in range(B):
                last = mm(bank(5)[0:1, b * P:(b + 1) * P], W("cond")[:, b:b + 1], W("wsq"))
            last.then_inc(sem("qrow_mm"), 1)
            for b in range(B):
                claim(eng, b, "sfT", b + 1)
                mm(bank(b), W("wsv"), xT[:, half(b)], True, False)
                eng.wait_ge(sem("keep"), b + 1)
                eng.wait_ge(sem("qrow"), 1)
                mm(bank(b), qrow[:, b * P:(b + 1) * P], keep[:, half(b)], False, True).then_inc(sem("sf_mm"), 1)
            for b in range(B):
                eng.wait_ge(sem("sfT"), b + 1)
                for d in range(2):
                    n = 2 * b + d
                    claim(eng, 2 + n, "qhT", n + 1)
                    mm(bank(2 + n), W("wq")[:, tile_cols(d)], sfT[:, half(b)]).then_inc(sem("qh_mm"), 1)
            claim(eng, 6, "kblk", 4)
            for b in range(B):
                for d in range(2):
                    n = 2 * b + d
                    mm(bank(6)[:, 32 * n:32 * n + M0], W("wk")[:, tile_cols(d)], sfT[:, b * T:b * T + M0])\
                        .then_inc(sem("kh_mm"), 1)
            for b in range(B):
                eng.wait_ge(sem("kvrep"), b + 1)
                for d in range(2):
                    n = 2 * b + d
                    claim(eng, 4 + n, "vblk", n + 1)
                    for c in range(NC0):
                        last = mm(bank(4 + n)[0:RC, c * P:(c + 1) * P],
                                  kvrep[b][:, HC * c:HC * c + HC, :].rearrange("p h m -> p (h m)"),
                                  W("wo")[:, tile_cols(d)])
                    last.then_inc(sem("vf_mm"), 1)

            def l0_scores(g):
                b, d, h = g // 4, (g // 2) % 2, g % 2
                pr = PP[g % 2]
                claim(eng, 2 * (g % 2), "s0_m", g + 1)
                claim(eng, 2 * (g % 2) + 1, "s0_m", g + 1)
                eng.wait_ge(sem("kblk"), 2 * b + d + 1)
                eng.wait_ge(sem("qhT"), 2 * b + d + 1)
                for t in range(2):
                    i = b * NB + 2 * h + t
                    last = mm(pr[:, t, 0:H0 * M0], qhT[d][:, tile_cols(i)],
                              kblk[2 * b + d][:, :, :].rearrange("p h m -> p (h m)"))
                last.then_inc(sem("s0_mm"), 1)

            def l0_turn(g):
                pr = PP[2 + g % 2]
                claim(eng, 4 + 2 * (g % 2), "w0T", 2 * g + 2)
                claim(eng, 5 + 2 * (g % 2), "w0T", 2 * g + 2)
                eng.wait_ge(sem("w0n"), g + 1)
                for t in range(2):
                    for c in range(NC0):
                        n = RC if c < 2 else RLAST
                        last = pe.transpose(pr[0:n, t, c * P:(c + 1) * P],
                                            w0p[:, g % 4, t, c * RC:c * RC + n], ident)
                last.then_inc(sem("w0_tr"), 1)

            def l0_out(b):
                k = 4 + 2 * b
                claim(eng, k, "l0sum", b + 1)
                eng.wait_ge(sem("w0T"), 8 * b + 8)
                for d in range(2):
                    eng.wait_ge(sem("vblk"), 2 * b + d + 1)
                    for c in range(NC0):
                        n = RC if c < 2 else RLAST
                        last = mm(bank(k), vblk[2 * b + d][0:n, c, :], w0T[2 * b + d][0:n, c, :],
                                  d == 0 and c == 0, d == 1 and c == NC0 - 1)
                last.then_inc(sem("o0_mm"), 1)

            def l0_back(b):
                k = 5 + 2 * b
                claim(eng, k, "x0", b + 1)
                eng.wait_ge(sem("l0x"), b + 1)
                for w in range(NB):
                    last = pe.transpose(bank(k)[:, tile_cols(w)], xoT[:, tile_cols(b * NB + w)], ident)
                last.then_inc(sem("l0_back"), 1)

            l0_scores(0)
            l0_scores(1)

            claim(eng, 4, "modc", 1)
            eng.wait_ge(sem("ld_w1"), 16)
            eng.wait_ge(sem("ld_w2"), 16)
            eng.wait_ge(sem("ld_w3"), 16)
            eng.wait_ge(sem("silu_c"), 1)
            eng.wait_ge(sem("bcast"), 2)
            cond = W("cond")
            for j in range(12):
                lhs, rhs = ((W("wcol1"), silu_c[:, :]) if j < 4 else
                            (W("wcol2"), cond) if j < 10 else (W("wt1"), cond))
                at = j if j < 4 else j - 4 if j < 10 else j - 10
                last = mm(bank(4)[:, 2 * j:2 * j + 2], lhs[:, tile_cols(at)], rhs)
            last.then_inc(sem("mod_mm"), 1)
            for b in range(B):
                claim(eng, 5 + b, "gate", b + 1)
                mm(bank(5 + b)[:, 0:2 * P], bc_silu[:, b, :], W("wgate1"))
                mm(bank(5 + b)[:, 2 * P:4 * P], bc_cond[:, b, :], W("wgate2")).then_inc(sem("gate_mm"), 1)
            claim(eng, 7, "modd", 1)
            eng.wait_ge(sem("tpe"), 1)
            for j in range(4):
                last = mm(bank(7)[:, 2 * j:2 * j + 2], W("wcol3")[:, tile_cols(j)], tpe[:, :])
            last.then_inc(sem("modd_mm"), 1)

            for g in range(8):
                if g + 2 < 8:
                    l0_scores(g + 2)
                l0_turn(g)
                if g == 5:
                    l0_out(0)
                    l0_back(0)
            l0_out(1)
            l0_back(1)

            def norm_turn(n):
                for b in range(B):
                    claim(eng, 4 + b, "hT", 2 * n + b + 1)
                    eng.wait_ge(sem("xn"), NT * n + NB * (b + 1))
                    for w in range(NB):
                        last = pe.transpose(bank(4 + b)[:, tile_cols(w)], xn[:, b * NB + w, :], ident)
                    last.then_inc(sem("norm_tr"), 1)

            def mlp_up(n, w):
                for b in range(B):
                    eng.wait_ge(sem("hT"), 2 * (3 if n else 1) + b + 1)
                    for c in range(4):
                        k = 4 * b + c
                        claim(eng, k % 4, "gT", 8 * n + k + 1)
                        mm(bank(k % 4), w[:, tile_cols(c)], hT[:, half(b)]).then_inc(sem("up_mm"), 1)

            def mlp_down(n, w):
                for b in range(B):
                    claim(eng, 6 + b, "xr", 2 * {0: 1, 1: 3, 2: 5}[n] + b + 1)
                    eng.wait_ge(sem("gT"), 8 * n + 4 * b + 4)
                    for wt in range(NB):
                        for c in range(4):
                            last = mm(bank(6 + b)[:, tile_cols(wt)], gT[:, c, tile_cols(b * NB + wt)], w(b, c),
                                      c == 0, c == 3)
                    last.then_inc(sem("down_mm"), 1)

            def qkv(n, w):
                for i in range(NT):
                    b = i // NB
                    claim(eng, 6 + i % 2, "vv", NT * n + i + 1)
                    eng.wait_ge(sem("hT"), 2 * (4 if n else 0) + b + 1)
                    mm(bank(6 + i % 2)[:, 0:3 * P], hT[:, tile_cols(i)], w).then_inc(sem("qkv_mm"), 1)

            norm_turn(0)
            qkv(0, W("wqkv1"))

            def l1_qkT(w):
                claim(eng, 6, "qkT1", w + 1)
                eng.wait_ge(sem("rope"), w // NB + 1)
                for j in range(2):
                    last = pe.transpose(bank(6)[:, tile_cols(j)], qk[:, w, j * P:(j + 1) * P], ident)
                last.then_inc(sem("qkT_mm"), 1)

            def l1_scores(w):
                claim(eng, 2 * (w % 2), "sub1", w + 1)
                claim(eng, 2 * (w % 2) + 1, "sub1", w + 1)
                eng.wait_ge(sem("kb1"), w + 1)
                for j in range(2):
                    last = mm(PP[w % 2][:, j, :], qkT1[:, w % 2, 0:P],
                              kb1[:, w % 2, 4 * j:4 * j + 4, :].rearrange("p h k -> p (h k)"))
                last.then_inc(sem("s1_mm"), 1)

            def l1_turn(w):
                claim(eng, 4, "pT1", w + 1)
                claim(eng, 5, "pT1", w + 1)
                eng.wait_ge(sem("exp1"), w + 1)
                for h in range(H1):
                    last = pe.transpose(PP[2][:, h // 4, tile_cols(h % 4)], p1[:, w % 2, h, :], ident)
                last.then_inc(sem("p1_tr"), 1)

            def l1_values(w):
                claim(eng, 6, "os1", w + 1)
                eng.wait_ge(sem("pT1"), w + 1)
                eng.wait_ge(sem("vv"), w + 1)
                eng.wait_ge(sem("ones_v"), 2)
                for h in range(H1):
                    g = h % 4
                    last = mm(bank(6)[PAD * g:PAD * g + PAD, tile_cols(h // 4)], v1[:, w, h, :], pT1[:, w % 2, h, :])
                last.then_inc(sem("pv1_mm"), 1)

            def l1_tokens(w):
                claim(eng, 7, "otok1", w + 1)
                eng.wait_ge(sem("os1"), w + 1)
                for j in range(2):
                    last = pe.transpose(bank(7)[:, tile_cols(j)], os1[:, w % 2, j, :], ident)
                last.then_inc(sem("ot1_mm"), 1)

            for k in range(NT + 4):
                if k < NT:
                    l1_qkT(k)
                if 0 <= k - 1 < NT:
                    l1_scores(k - 1)
                if 0 <= k - 2 < NT:
                    l1_turn(k - 2)
                if 0 <= k - 3 < NT:
                    l1_values(k - 3)
                if 0 <= k - 4 < NT:
                    l1_tokens(k - 4)

            def out_proj(n, src, w):
                for b in range(B):
                    claim(eng, b, "oT", 2 * n + b + 1)
                    eng.wait_ge(sem("otok1" if n == 0 else "otok3"), NB * (b + 1))
                    for wt in range(NB):
                        last = pe.transpose(bank(b)[:, tile_cols(wt)], src(b, wt), ident)
                    last.then_inc(sem("oT_mm"), 1)
                for b in range(B):
                    claim(eng, 2 + b, "xr", 2 * (4 if n else 0) + b + 1)
                    eng.wait_ge(sem("oT"), 2 * n + b + 1)
                    for wt in range(NB):
                        last = mm(bank(2 + b)[:, tile_cols(wt)], oT[:, tile_cols(b * NB + wt)], w(b))
                    last.then_inc(sem("proj_mm"), 1)

            eng.wait_ge(sem("gated_w"), 2)
            out_proj(0, lambda b, wt: otok[:, b * NB + wt, :], lambda b: wout1g[:, b, :])

            norm_turn(1)
            mlp_up(0, W("wff1_1"))
            eng.wait_ge(sem("gated_w"), 4)
            mlp_down(0, lambda b, c: wff2g[0][:, b, c, :])

            claim(eng, 0, "bbT", 1)
            eng.wait_ge(sem("bbar"), 1)
            pe.transpose(bank(0)[:, 0:P], bbar[:, :], ident).then_inc(sem("bbar_tr"), 1)
            norm_turn(2)
            eng.wait_ge(sem("bbT"), 1)
            claim(eng, 2, "rotin", 1)
            claim(eng, 3, "rotin", 2)
            for b in range(B):
                eng.wait_ge(sem("hT"), 2 * 2 + b + 1)
                for j in range(2):
                    last = mm(bank(2 + j)[64 * b:64 * b + 64, :], bbT[:, 64 * j:64 * j + 64], hT[:, half(b)])
            last.then_inc(sem("u_mm"), 1)
            eng.wait_ge(sem("cg"), 3 * B)
            eng.wait_ge(sem("rotout"), 2)
            for b in range(B):
                claim(eng, 6 + b, "xr", 2 * 2 + b + 1)
                for wt in range(NB):
                    o = bank(6 + b)[:, tile_cols(wt)]
                    mm(o, uw[:, tile_cols(wt)], cga[:, b, :], True, False)
                    mm(o, uw2[:, tile_cols(wt)], cgb[:, b, :], False, False)
                    last = mm(o, hT[:, tile_cols(b * NB + wt)], dg[:, b, :], False, True)
                last.then_inc(sem("y_mm"), 1)
            norm_turn(3)
            mlp_up(1, W("wff1_2"))
            eng.wait_ge(sem("gated_w"), 6)
            mlp_down(1, lambda b, c: wff2g[1][:, b, c, :])

            norm_turn(4)
            qkv(1, W("wqkv3"))
            for b in range(B):
                for j in range(2):
                    n = 2 * b + j
                    claim(eng, n, "res3", n + 1)
                    eng.wait_ge(sem("rope3"), b + 1)
                    for wt in range(NB):
                        last = pe.transpose(bank(n)[:, tile_cols(wt)], qk[:, b * NB + wt, j * P:(j + 1) * P], ident)
                    last.then_inc(sem("qkT3_mm"), 1)
            eng.wait_ge(sem("res3"), 4)
            eng.wait_ge(sem("vv"), 2 * NT)
            eng.wait_ge(sem("hT"), 2 * 4 + 2)

            def l3_score(it, par, s):
                h, w = s // NB, s % NB
                eng.wait_ge(sem("max3"), it * 16 + (s - 1)) if not (isinstance(it, int) and it * 16 + s - 1 <= 0) else None
                mm(bank(s % 2), qa[par][0:AUG, h, tile_cols(w)], ka[par][0:AUG, h, :]).then_inc(sem("s3_mm"), 1)

            def l3_pair(it, par, s):
                p, h = s // G3, s % G3
                if s >= 2:
                    eng.wait_ge(sem("exp3"), it * 8 + (s - 1))
                for t in range(2):
                    last = mm(PP[1 + s % 2][:, t, :], ka[par][:, h, tile_cols(2 * p + t)], qa[par][:, h, :])
                    if t == 0:
                        last.then_inc(sem("st3"), 1)
                last.then_inc(sem("st3"), 1)

            def l3_values(it, par, p):
                eng.wait_ge(sem("exp3"), it * 8 + 4 * p + 4)
                if p == 0:
                    eng.wait_ge(sem("vg"), it + 1)
                for t in range(2):
                    for h in range(G3):
                        last = mm(bank(6)[PAD * h:PAD * h + PAD, :], vg[par][:, 2 * p + t, h, :], p3[:, p, h, t, :],
                                  p == 0 and t == 0, p == 1 and t == 1)
                last.then_inc(sem("pv3_mm"), 1)

            def l3_turn_max(it):
                eng.wait_ge(sem("ms3"), it + 1)
                if not (isinstance(it, int) and it == 0):
                    eng.wait_ge(sem("otok3"), it)
                pe.transpose(bank(7)[:, 0:P // 2].bitcast(BF16), ms3[:, :, :].rearrange("p i n -> p (i n)"),
                             identb[:, :]).then_inc(sem("m3_tr"), 1)

            def l3_tokens(it):
                eng.wait_ge(sem("os3"), it + 1)
                for w in range(NB):
                    last = pe.transpose(bank(7)[:, tile_cols(w)], os3[:, tile_cols(w)], ident)
                last.then_inc(sem("ot3_mm"), 1)

            def l3_step(it, par, ahead):
                eng.wait_ge(sem(f"ld_m{par}"), (it // 2 if isinstance(it, int) else it_half(it)) * 48 + 48)
                if ahead:
                    eng.wait_ge(sem(f"ld_qa{1 - par}"), nxt_loads(it, par))
                for s in range(8):
                    l3_pair(it, par, s)
                    if ahead:
                        l3_score(it + 1, 1 - par, 2 * s)
                        l3_score(it + 1, 1 - par, 2 * s + 1)
                    if s == 5:
                        l3_values(it, par, 0)
                l3_values(it, par, 1)
                l3_tokens(it)
                if ahead:
                    eng.wait_ge(sem("mT3"), it + 1)
                    l3_turn_max(it + 1)

            pair_of = {}

            def it_half(it):
                return pair_of["now"]

            def nxt_loads(it, par):
                if isinstance(it, int):
                    return ((it + 1) // 2 + 1) * 96
                return (pair_of["now"] + (2 if par else 1)) * 96

            eng.wait_ge(sem("identb"), 1)
            eng.wait_ge(sem("ms3_pad"), 1)
            eng.wait_ge(sem("ld_qa0"), 96)
            for s in range(16):
                l3_score(0, 0, s)
            l3_turn_max(0)
            with eng.Fori(0, NIT // 2 - 1) as pair:
                pair_of["now"] = pair
                l3_step(pair * 2, 0, True)
                l3_step(pair * 2 + 1, 1, True)
            l3_step(NIT - 2, 0, True)
            l3_step(NIT - 1, 1, False)
            eng.wait_ge(sem("max3"), 16 * NIT)
            eng.wait_ge(sem("exp3"), 8 * NIT)
            freed.clear()
            out_proj(1, lambda b, wt: o3[:, wt, b * NG3:(b + 1) * NG3, :].rearrange("p g f -> p (g f)"), lambda b: W("wao"))

            norm_turn(5)
            for b in range(B):
                eng.wait_ge(sem("hT"), 2 * 5 + b + 1)
                for c in range(4):
                    k = 4 * b + c
                    claim(eng, 2 * (k % 2), "gT", 16 + k + 1)
                    claim(eng, 2 * (k % 2) + 1, "sg3", k + 1)
                    mm(bank(2 * (k % 2) + 1), W("wfc")[:, tile_cols(4 + c)], hT[:, half(b)]).then_inc(sem("fc_mm"), 1)
                    mm(bank(2 * (k % 2)), W("wfc")[:, tile_cols(c)], hT[:, half(b)]).then_inc(sem("fc_mm"), 1)
            mlp_down(2, lambda b, c: W("wfo")[:, tile_cols(c)])

        @block.scalar
        def _(eng):
            eng.dma_start(xT[:, :], xt_in).then_inc(sem("ld_xT"), 16)
            eng.dma_start(adj[0][:, :], adj_in[0]).then_inc(sem("ld_adj0"), 16)
            eng.dma_start(tiles["rw"][:, :], rows.to_broadcast([P, sum(ROWS.values())])).then_inc(sem("ld_rows"), 16)
            eng.dma_start(tiles["w1"][:, :], w1).then_inc(sem("ld_w1"), 16)

            def ident_act(o, i, bias=None, scale=None):
                kw = {}
                if bias is not None:
                    kw["bias"] = bias
                if scale is not None:
                    kw["scale"] = scale
                return act.activation(o, i, ACT.Identity, **kw)

            eng.wait_ge(sem("ld_w0"), 16)
            act.activation(silu_c[:, :], W("cond"), ACT.Silu).then_inc(sem("silu_c"), 1)
            eng.wait_ge(sem("qrow_mm"), 1)
            act.copy(qrow[:, :], bank(5)[0:1, 0:2 * P]).then_inc(sem("qrow"), 1)
            for b in range(B):
                eng.wait_ge(sem("sf_mm"), b + 1)
                ident_act(sfT[:, half(b)], bank(b), W("bself")).then_inc(sem("sfT"), 1)
            for b in range(B):
                for d in range(2):
                    n = 2 * b + d
                    eng.wait_ge(sem("qh_mm"), n + 1)
                    ident_act(qhT[d][:, half(b)], bank(2 + n), W("bq0")[:, d:d + 1]).then_inc(sem("qhT"), 1)
            eng.wait_ge(sem("modc"), 1)
            act.activation(sgt[:, :], modc[:, 11, :], ACT.Silu).then_inc(sem("sgt"), 1)

            def l0_exp(g):
                eng.wait_ge(sem("sub0"), g + 1)
                act.activation(w0p[:, g % 4, :, :], w0p[:, g % 4, :, :], ACT.Exp).then_inc(sem("exp0"), 1)

            def l0_evac(g):
                b, d, h = g // 4, (g // 2) % 2, g % 2
                dst = w0T[2 * b + d]
                cols = slice(2 * h * P, 2 * h * P + 2 * P)
                pr = PP[2 + g % 2]
                eng.wait_ge(sem("w0_tr"), g + 1)
                act.copy(dst[:, 0:2, cols].rearrange("r c (t q) -> r t c q", t=2),
                         pr[0:RC, :, 0:2 * P].rearrange("r t (c q) -> r t c q", c=2)).then_inc(sem("w0T"), 1)
                act.copy(dst[0:RLAST, 2, cols].rearrange("r (t q) -> r t q", t=2),
                         pr[0:RLAST, :, 2 * P:3 * P]).then_inc(sem("w0T"), 1)

            def x0_evac(b):
                eng.wait_ge(sem("l0_back"), b + 1)
                act.copy(X[:, btiles(b), :].rearrange("p w f -> p (w f)"), bank(5 + 2 * b)).then_inc(sem("x0"), 1)

            for k in range(8 + 2):
                if k < 8:
                    l0_exp(k)
                if k >= 2:
                    l0_evac(k - 2)
                if k - 2 == 5:
                    x0_evac(0)
            x0_evac(1)

            def norm_evac(n):
                for b in range(B):
                    eng.wait_ge(sem("norm_tr"), 2 * n + b + 1)
                    eng.wait_ge(sem("scl"), 1)
                    ident_act(hT[:, half(b)], bank(4 + b), shf[:, n, b:b + 1], scl[:, n, b:b + 1])\
                        .then_inc(sem("hT"), 1)

            def mlp_act(n, bias):
                for k in range(8):
                    b, c = k // 4, k % 4
                    eng.wait_ge(sem("up_mm"), 8 * n + k + 1)
                    act.activation(gT[:, c, half(b)], bank(k % 4), ACT.Gelu_apprx_tanh, bias=bias[:, c:c + 1])\
                       .then_inc(sem("gT"), 1)

            def oT_evac(n):
                for b in range(B):
                    eng.wait_ge(sem("oT_mm"), 2 * n + b + 1)
                    act.copy(oT[:, half(b)], bank(b)).then_inc(sem("oT"), 1)

            norm_evac(0)
            for k in range(NT + 3):
                w = k
                if w < NT:
                    eng.wait_ge(sem("qkT_mm"), w + 1)
                    if w >= 2:
                        eng.wait_ge(sem("kb1"), w - 1)
                        eng.wait_ge(sem("s1_mm"), w - 1)
                    act.copy(qkT1[:, w % 2, :], bank(6)[:, 0:2 * P]).then_inc(sem("qkT1"), 1)
                w = k - 2
                if 0 <= w < NT:
                    eng.wait_ge(sem("p1_tr"), w + 1)
                    if w >= 2:
                        eng.wait_ge(sem("pv1_mm"), w - 1)
                    act.copy(pT1[:, w % 2, :, :].rearrange("p h q -> p (h q)"),
                             PP[2][:, :, :].rearrange("p a q -> p (a q)")).then_inc(sem("pT1"), 1)
                w = k - 3
                if 0 <= w < NT:
                    eng.wait_ge(sem("pv1_mm"), w + 1)
                    if w >= 2:
                        eng.wait_ge(sem("ot1_mm"), w - 1)
                    act.copy(os1[:, w % 2, :, :].rearrange("p a q -> p (a q)"), bank(6)[:, 0:2 * P])\
                       .then_inc(sem("os1"), 1)
                w = k - 1
                if 0 <= w < NT:
                    eng.wait_ge(sem("sub1"), w + 1)
                    act.activation(p1[:, w % 2, :, :], p1[:, w % 2, :, :], ACT.Exp, scale=float(D1) ** -0.5)\
                       .then_inc(sem("exp1"), 1)
            oT_evac(0)
            norm_evac(1)
            mlp_act(0, W("bff1_1"))

            act.activation(col[:, 0:1], W("log_step"), ACT.Exp).then_inc(sem("dt"), 1)
            eng.wait_ge(sem("rho_in"), 1)
            act.activation(col[:, 2:3], col[:, 1:2], ACT.Exp).then_inc(sem("rho"), 1)
            eng.wait_ge(sem("turns"), 1)
            act.activation(ei[:, :], tA[:, :], ACT.Sin, scale=TWO_PI).then_inc(sem("rot"), 1)
            eng.wait_ge(sem("turns"), 2)
            act.activation(er[:, :], tB[:, :], ACT.Sin, scale=-TWO_PI, bias=W("halfpi")).then_inc(sem("rot"), 1)
            eng.wait_ge(sem("bbar_tr"), 1)
            act.copy(bbT[:, :], bank(0)[:, 0:P]).then_inc(sem("bbT"), 1)
            norm_evac(2)
            norm_evac(3)
            mlp_act(1, W("bff1_2"))

            norm_evac(4)
            for n in range(2 * B):
                eng.wait_ge(sem("qkT3_mm"), n + 1)
                act.copy(split[:, n, 0, :], bank(n)).then_inc(sem("split1"), 1)
                eng.wait_ge(sem("res3"), n + 1)
                act.copy(split[:, n, 1, :], res3[:, n, :]).then_inc(sem("split2"), 1)

            def l3_exp(it, s):
                p, h = s // G3, s % G3
                eng.wait_ge(sem("st3"), it * 16 + 2 * s + 2)
                act.activation(p3[:, p, h, :, :], PP[1 + s % 2][:, :, :], ACT.Exp, scale=float(D3) ** -0.5)\
                   .then_inc(sem("exp3"), 1)

            def l3_mT(it):
                eng.wait_ge(sem("m3_tr"), it + 1)
                if not (isinstance(it, int) and it == 0):
                    eng.wait_ge(sem("st3"), it * 16)
                act.copy(mT3[:, :], bank(7)[0:3 * 16, 0:P // 2].bitcast(BF16)).then_inc(sem("mT3"), 1)

            def l3_step(it, ahead):
                for s in range(8):
                    l3_exp(it, s)
                eng.wait_ge(sem("pv3_mm"), it * 2 + 2)
                act.copy(os3[:, :], bank(6)).then_inc(sem("os3"), 1)
                if ahead:
                    l3_mT(it + 1)

            l3_mT(0)
            with eng.Fori(0, NIT - 1) as it:
                l3_step(it, True)
            l3_step(NIT - 1, False)
            oT_evac(1)
            norm_evac(5)
            for k in range(8):
                c = k % 4
                eng.wait_ge(sem("fc_mm"), 2 * k + 1)
                if k >= 2:
                    eng.wait_ge(sem("gT"), 16 + k - 1)
                act.activation(sg3[:, k % 2, :], bank(2 * (k % 2) + 1), ACT.Silu, bias=W("bfc")[:, 4 + c:5 + c])\
                   .then_inc(sem("sg3"), 1)

        @block.gpsimd
        def _(eng):
            def tt(o, a, b, op):
                return pool.tensor_tensor(o, a, b, op)

            pool.memset(ms3[:, 3:, :], 0.0).then_inc(sem("ms3_pad"), 1)
            pool.memset(mhalf[:, :], -0.5).then_inc(sem("mhalf"), 1)
            eng.wait_ge(sem("ld_w0"), 16)
            pool.tensor_copy(bc_cond[:, :, :], W("cond").unsqueeze(2).to_broadcast([P, B, P])).then_inc(sem("bcast"), 1)
            eng.wait_ge(sem("silu_c"), 1)
            pool.tensor_copy(bc_silu[:, :, :], silu_c[:, :].unsqueeze(2).to_broadcast([P, B, P])).then_inc(sem("bcast"), 1)
            for b in range(B):
                eng.wait_ge(sem("sfT"), b + 1)
                pool.tensor_copy(kvrep[b][:, :, :],
                                 sfT[:, b * T:b * T + M0].unsqueeze(1).to_broadcast([P, NC0 * HC, M0]))\
                    .then_inc(sem("kvrep"), 1)

            def l0_tiles(src, g):
                b, d, h = g // 4, (g // 2) % 2, g % 2
                i = b * NB + 2 * h
                return src[:, d, i * M0:(i + 2) * M0].rearrange("p (t m) -> p t m", t=2).unsqueeze(2)\
                    .to_broadcast([P, 2, H0, M0])

            def l0_view(g):
                return w0p[:, g % 4, :, :].rearrange("p t (h m) -> p t h m", m=M0)

            def l0_bias(g):
                eng.wait_ge(sem("s0_m"), g + 1)
                eng.wait_ge(sem("mtb"), (g // 2) % 2 + 1)
                tt(l0_view(g), l0_view(g), l0_tiles(mtb, g), ALU.add).then_inc(sem("add0"), 1)

            def l0_norm(g):
                eng.wait_ge(sem("rs0"), g + 1)
                v = w0p[:, g % 4, :, :].rearrange("p t (h m) -> p (t h) m", m=M0)
                tt(v, v, rs0[:, g % 4, :].unsqueeze(2).to_broadcast([P, 2 * H0, M0]), ALU.mult)\
                    .then_inc(sem("w0n"), 1)

            for k in range(8 + 2):
                if k < 8:
                    l0_bias(k)
                if k >= 2:
                    l0_norm(k - 2)

            pool.memset(v1[:, :, :, D1:PAD], 0.0).then_inc(sem("ones_v"), 1)
            eng.wait_ge(sem("ones_v"), 1)
            pool.memset(v1[:, :, :, D1:D1 + 1], 1.0).then_inc(sem("ones_v"), 1)

            eng.wait_ge(sem("ld_w1"), 16)
            eng.wait_ge(sem("ld_w2"), 16)
            eng.wait_ge(sem("ld_rows"), 16)
            eng.wait_ge(sem("gate"), B)

            def gcols(b, j, n=None):
                g = gate[:, b, j * P:(j + 1) * P]
                return g if n is None else g.unsqueeze(1).to_broadcast([P, n, P])

            for b in range(B):
                tt(wout1g[:, b, :], W("wout1"), gcols(b, 0), ALU.mult).then_inc(sem("gated_w"), 1)
            for b in range(B):
                tt(bres[:, 0, b, :], W("rout1"), gcols(b, 0), ALU.mult).then_inc(sem("gated_b"), 1)

            def residual(n, bias):
                use = {0: 0, 1: 1, 2: 3, 3: 4, 4: 5}[n]
                for b in range(B):
                    if use == 0:
                        eng.wait_ge(sem("x0"), b + 1)
                    else:
                        eng.wait_ge(sem("xr"), 2 * (use - 1) + b + 1)
                    tt(Xb[:, btiles(b), :], X[:, btiles(b), :], bias(b).unsqueeze(1).to_broadcast([P, NB, P]), ALU.add)\
                        .then_inc(sem("xb"), 1)

            def norm_pow(n):
                for b in range(B):
                    eng.wait_ge(sem("var"), 2 * n + b + 1)
                    if n == 0 and b == 0:
                        eng.wait_ge(sem("mhalf"), 1)
                    tt(rstd[:, btiles(b)], var[:, btiles(b)], mhalf[:, btiles(b)], ALU.pow).then_inc(sem("rstd"), 1)

            norm_pow(0)
            eng.wait_ge(sem("gated_b"), 2)
            residual(0, lambda b: bres[:, 0, b, :])
            for w in range(NT):
                eng.wait_ge(sem("qkT1"), w + 1)
                if w >= 2:
                    eng.wait_ge(sem("s1_mm"), w - 1)
                tt(kb1[:, w % 2, :, :], qkT1[:, w % 2, P:2 * P].unsqueeze(1).to_broadcast([P, H1, P]),
                   W("kmask1").unsqueeze(2).to_broadcast([P, H1, P]), ALU.mult).then_inc(sem("kb1"), 1)
            for b in range(B):
                tt(wff2g[0][:, b, :, :], W("wff2_1").rearrange("p (c f) -> p c f", c=4), gcols(b, 1, 4), ALU.mult)\
                    .then_inc(sem("gated_w"), 1)
            for b in range(B):
                tt(bres[:, 1, b, :], W("rff2_1"), gcols(b, 1), ALU.mult).then_inc(sem("gated_b"), 1)
            norm_pow(1)
            eng.wait_ge(sem("gated_b"), 4)
            residual(1, lambda b: bres[:, 1, b, :])
            for b in range(B):
                tt(wff2g[1][:, b, :, :], W("wff2_2").rearrange("p (c f) -> p c f", c=4), gcols(b, 3, 4), ALU.mult)\
                    .then_inc(sem("gated_w"), 1)
            for b in range(B):
                tt(bres[:, 2, b, :], W("rff2_2"), gcols(b, 3), ALU.mult).then_inc(sem("gated_b"), 1)
            pool.memset(v3[:, :, :, :, D3:PAD], 0.0).then_inc(sem("ones_v"), 1)
            eng.wait_ge(sem("ones_v"), 3)
            pool.memset(v3[:, :, :, :, D3:D3 + 1], 1.0).then_inc(sem("ones_v"), 1)
            eng.wait_ge(sem("ones_v"), 4)
            for j in range(2):
                pool.memset(qa[j][64:P, :, :], 0.0).then_inc(sem("zero3"), 1)
                pool.memset(ka[j][64:P, :, :], 0.0).then_inc(sem("zero3a"), 1)
            eng.wait_ge(sem("zero3a"), 2)
            for j in range(2):
                pool.memset(ka[j][AUG:AUG + 3, :, :], 1.0).then_inc(sem("zero3"), 1)
            eng.wait_ge(sem("zero3"), 4)
            pool.tensor_copy(identb[:, :], ident).then_inc(sem("identb"), 1)
            norm_pow(2)
            norm_pow(3)
            eng.wait_ge(sem("gated_b"), 6)
            residual(2, lambda b: bres[:, 2, b, :])
            norm_pow(4)
            residual(3, lambda b: W("rao"))

            for n in range(2 * B):
                eng.wait_ge(sem("split2"), n + 1)
                tt(split[:, n, 2, :], res3[:, n, :], split[:, n, 1, :], ALU.subtract).then_inc(sem("split3"), 1)

            def values(it, par):
                if not (isinstance(it, int) and it < 2):
                    eng.wait_ge(sem("pv3_mm"), it * 2 - 2)
                pool.tensor_copy(vg[par][:, :, :, :].rearrange("p w h c -> p (w h c)"),
                                 v3[:, :, :, :, :].rearrange("p i w h c -> p (i w h c)")[:, bass.ds(it * 512, 512)])\
                    .then_inc(sem("vg"), 1)

            eng.wait_ge(sem("vv"), 2 * NT)
            eng.wait_ge(sem("ones_v"), 4)
            values(0, 0)
            values(1, 1)
            with eng.Fori(1, NIT // 2) as pair:
                values(pair * 2, 0)
                values(pair * 2 + 1, 1)
            norm_pow(5)
            residual(4, lambda b: W("rfo"))

        @block.vector
        def _(eng):
            def tt(o, a, b, op):
                return dve.tensor_tensor(o, a, b, op)

            for b in range(B):
                eng.wait_ge(sem("rowsum"), b + 1)
                dve.tensor_scalar(keep[:, half(b)], bank(6 + b)[0:1, :], 0.0, None, ALU.not_equal)\
                   .then_inc(sem("keep"), 1)
            eng.wait_ge(sem("ld_rows"), 16)
            for d in range(2):
                a = adj[d][:, :].rearrange("p (n l) -> p n l", l=L)
                eng.wait_ge(sem(f"ld_adj{d}"), 16)
                dve.tensor_reduce(msum[:, d, :], a, X_AXIS, ALU.add).then_inc(sem("msum"), 1)
                if d:
                    eng.wait_ge(sem("mbias"), 1)
                tt(adj_w[:, :, :], a, W("wbias0").unsqueeze(1).to_broadcast([P, NT * M0, L]), ALU.mult)\
                    .then_inc(sem("mprod"), 1)
                eng.wait_ge(sem("msum"), d + 1)
                dve.tensor_scalar(mask[:, d, :], msum[:, d, :], 0.0, None, ALU.is_gt).then_inc(sem("mask"), 1)
                eng.wait_ge(sem("mprod"), d + 1)
                dve.tensor_reduce(mbias[:, d, :], adj_w[:, :, :], X_AXIS, ALU.add).then_inc(sem("mbias"), 1)
                eng.wait_ge(sem("mask"), d + 1)
                dve.tensor_scalar(mpen[:, d, :], mask[:, d, :], -1.0, -NEG, ALU.add, ALU.mult).then_inc(sem("mpen"), 1)
                eng.wait_ge(sem("mbias"), d + 1)
                eng.wait_ge(sem("mpen"), d + 1)
                dve.scalar_tensor_tensor(out=mtb[:, d, :], in0=mbias[:, d, :], scalar=W("bbias0"), in1=mpen[:, d, :],
                                         op0=ALU.add, op1=ALU.add).then_inc(sem("mtb"), 1)
            tt(bout_sum[:, :], W("bout0")[:, 0:1], W("bout0")[:, 1:2], ALU.add).then_inc(sem("bout_sum"), 1)
            eng.wait_ge(sem("kh_mm"), 4)
            for n in range(4):
                d = n % 2
                dve.scalar_tensor_tensor(
                    out=kblk[n][:, :, :], in0=bank(6)[:, 32 * n:32 * n + M0].unsqueeze(1).to_broadcast([P, H0, M0]),
                    scalar=W("bk0")[:, d:d + 1], in1=W("kmask0").rearrange("p (h m) -> p h m", m=M0),
                    op0=ALU.add, op1=ALU.mult).then_inc(sem("kblk"), 1)
            for n in range(4):
                eng.wait_ge(sem("vf_mm"), n + 1)
                tt(vblk[n][:, :, :].rearrange("r c f -> r (c f)"), bank(4 + n)[0:RC, 0:NC0 * P], W("vmask0")[0:RC, :],
                   ALU.mult).then_inc(sem("vblk"), 1)

            def l0_tiles(src, g):
                b, d, h = g // 4, (g // 2) % 2, g % 2
                i = b * NB + 2 * h
                return src[:, d, i * M0:(i + 2) * M0].rearrange("p (t m) -> p t m", t=2).unsqueeze(2)\
                    .to_broadcast([P, 2, H0, M0])

            def flat(g):
                return w0p[:, g % 4, :, :].rearrange("p t (h m) -> p (t h) m", m=M0)

            def l0_mask(g):
                eng.wait_ge(sem("s0_mm"), g + 1)
                if g >= 4:
                    eng.wait_ge(sem("w0_tr"), g - 3)
                tt(w0p[:, g % 4, :, :].rearrange("p t (h m) -> p t h m", m=M0),
                   PP[g % 2][:, :, 0:H0 * M0].rearrange("p t (h m) -> p t h m", m=M0),
                   l0_tiles(mask, g), ALU.mult).then_inc(sem("s0_m"), 1)

            def l0_max(g):
                eng.wait_ge(sem("add0"), g + 1)
                dve.tensor_reduce(mx0[:, g % 4, :], flat(g), X_AXIS, ALU.max).then_inc(sem("mx0"), 1)
                eng.wait_ge(sem("mx0"), g + 1)
                tt(flat(g), flat(g), mx0[:, g % 4, :].unsqueeze(2).to_broadcast([P, 2 * H0, M0]), ALU.subtract)\
                    .then_inc(sem("sub0"), 1)

            def l0_sum(g):
                eng.wait_ge(sem("exp0"), g + 1)
                dve.tensor_reduce(sm0[:, g % 4, :], flat(g), X_AXIS, ALU.add).then_inc(sem("sm0"), 1)
                eng.wait_ge(sem("sm0"), g + 1)
                dve.reciprocal(rs0[:, g % 4, :], sm0[:, g % 4, :]).then_inc(sem("rs0"), 1)

            def l0_final(b):
                k = 4 + 2 * b
                eng.wait_ge(sem("o0_mm"), b + 1)
                eng.wait_ge(sem("bout_sum"), 1)
                dve.scalar_tensor_tensor(out=l0sum[:, b, :], in0=bank(k), scalar=bout_sum[:, :], in1=sfT[:, half(b)],
                                         op0=ALU.add, op1=ALU.add).then_inc(sem("l0sum"), 1)
                eng.wait_ge(sem("l0sum"), b + 1)
                dve.scalar_tensor_tensor(out=xoT[:, half(b)], in0=l0sum[:, b, :], scalar=0.0, in1=xT[:, half(b)],
                                         op0=ALU.max, op1=ALU.add).then_inc(sem("l0x"), 1)

            def modulation():
                steps = [0]

                def did(ins):
                    steps[0] += 1
                    ins.then_inc(sem("mod_step"), 1)
                    eng.wait_ge(sem("mod_step"), steps[0])

                eng.wait_ge(sem("mod_mm"), 1)
                tt(modc[:, :, :], bank(4)[:, 0:24].rearrange("p (j b) -> p j b", b=B),
                   W("bmod").unsqueeze(2).to_broadcast([P, 12, B]), ALU.add).then_inc(sem("modc"), 1)
                eng.wait_ge(sem("sgt"), 1)
                eng.wait_ge(sem("modc"), 1)
                tt(tpe[:, :], modc[:, 10, :], sgt[:, :], ALU.mult).then_inc(sem("tpe"), 1)
                for b in range(B):
                    eng.wait_ge(sem("gate_mm"), b + 1)
                    tt(gate[:, b, :], bank(5 + b), W("rgate"), ALU.add).then_inc(sem("gate"), 1)
                eng.wait_ge(sem("modd_mm"), 1)
                tt(modd[:, :, :], bank(7)[:, 0:8].rearrange("p (j b) -> p j b", b=B),
                   W("bmodd").unsqueeze(2).to_broadcast([P, 4, B]), ALU.add).then_inc(sem("modd"), 1)
                eng.wait_ge(sem("modd"), 1)
                did(dve.tensor_scalar(modp[:, :, :], modc[:, :, :], 1.0, None, ALU.add))
                did(dve.tensor_scalar(modq[:, :, :], modd[:, :, :], 1.0, None, ALU.add))
                did(dve.tensor_scalar(scl[:, 0, :], modp[:, 1, :], W("s1a"), None, ALU.mult))
                did(dve.tensor_scalar(scl[:, 1, :], modp[:, 3, :], W("s1b"), None, ALU.mult))
                did(dve.tensor_copy(scl[:, 2, :], modp[:, 5, :]))
                did(tt(scl[:, 3, :], modp[:, 8, :], modp[:, 7, :], ALU.mult))
                did(dve.tensor_scalar(scl[:, 4, :], modq[:, 1, :], W("g3a"), None, ALU.mult))
                did(dve.tensor_scalar(scl[:, 5, :], modq[:, 3, :], W("g3b"), None, ALU.mult))
                did(dve.tensor_copy(shf[:, 0, :], modc[:, 0, :]))
                did(dve.tensor_copy(shf[:, 1, :], modc[:, 2, :]))
                did(dve.tensor_copy(shf[:, 2, :], modc[:, 4, :]))
                did(tt(shtmp[:, :], modc[:, 9, :], modp[:, 7, :], ALU.mult))
                did(tt(shf[:, 3, :], shtmp[:, :], modc[:, 6, :], ALU.add))
                did(dve.tensor_copy(shf[:, 4, :], modd[:, 0, :]))
                dve.tensor_copy(shf[:, 5, :], modd[:, 2, :]).then_inc(sem("scl"), 1)

            for k in range(8 + 2):
                if k < 8:
                    l0_mask(k)
                if k == 1:
                    modulation()
                if 1 <= k <= 8:
                    l0_max(k - 1)
                if k >= 2:
                    l0_sum(k - 2)
                if k == 7:
                    l0_final(0)
            l0_final(1)

            def ssm_tables():
                steps = [0]

                def did(ins):
                    steps[0] += 1
                    ins.then_inc(sem("ssm_step"), 1)
                    eng.wait_ge(sem("ssm_step"), steps[0])

                def c(j):
                    return col[:, j:j + 1]

                def ts(o, i, s1, s2, op0, op1=None):
                    return dve.tensor_scalar(o, i, s1, s2, op0) if op1 is None else dve.tensor_scalar(o, i, s1, s2, op0, op1)

                def stt(o, i, s, j, op0, op1):
                    return dve.scalar_tensor_tensor(out=o, in0=i, scalar=s, in1=j, op0=op0, op1=op1)

                eng.wait_ge(sem("ld_w2"), 16)
                eng.wait_ge(sem("dt"), 1)
                tt(c(1), W("lam_re"), c(0), ALU.mult).then_inc(sem("rho_in"), 1)
                did(tt(c(3), W("lam_im"), c(0), ALU.mult))
                did(ts(c(4), c(3), 1.0 / TWO_PI, ROUND, ALU.mult, ALU.add))
                did(ts(c(4), c(4), -ROUND, None, ALU.add))
                did(stt(c(5), c(4), -TURN[0], c(3), ALU.mult, ALU.add))
                did(stt(c(5), c(4), -TURN[1], c(5), ALU.mult, ALU.add))
                did(stt(c(5), c(4), -TURN[2], c(5), ALU.mult, ALU.add))
                did(ts(c(6), c(5), 1.0 / TWO_PI, None, ALU.mult))
                did(ts(c(7), c(6), ROUND12, ROUND12, ALU.add, ALU.subtract))
                did(tt(c(8), c(6), c(7), ALU.subtract))
                t = W("steps")
                did(ts(tA[:, :], t, c(7), None, ALU.mult))
                did(ts(tB[:, :], tA[:, :], ROUND, ROUND, ALU.add, ALU.subtract))
                did(tt(tA[:, :], tA[:, :], tB[:, :], ALU.subtract))
                did(stt(tA[:, :], t, c(8), tA[:, :], ALU.mult, ALU.add))
                did(ts(tB[:, :], tA[:, :], ROUND, ROUND, ALU.add, ALU.subtract))
                did(tt(tA[:, :], tA[:, :], tB[:, :], ALU.subtract))
                ts(tA[:, :], tA[:, :], 0.4999999, -0.4999999, ALU.min, ALU.max).then_inc(sem("turns"), 1)
                eng.wait_ge(sem("turns"), 1)
                stt(tB[:, :], tA[:, :], -1.0, tA[:, :], ALU.mult, ALU.max).then_inc(sem("turns"), 1)
                lre, lim = W("lam_re"), W("lam_im")
                eng.wait_ge(sem("rho"), 1)
                eng.wait_ge(sem("rot"), 2)
                did(ts(c(9), er[:, 1:2], c(2), -1.0, ALU.mult, ALU.add))
                did(tt(c(10), ei[:, 1:2], c(2), ALU.mult))
                did(tt(c(11), lre, lre, ALU.mult))
                did(stt(c(12), lim, lim, c(11), ALU.mult, ALU.add))
                did(dve.reciprocal(c(13), c(12)))
                did(tt(c(14), c(9), lre, ALU.mult))
                did(stt(c(15), c(10), lim, c(14), ALU.mult, ALU.add))
                did(tt(c(16), c(15), c(13), ALU.mult))
                did(tt(c(17), c(9), lim, ALU.mult))
                did(stt(c(18), c(10), lre, c(17), ALU.mult, ALU.subtract))
                did(tt(c(19), c(18), c(13), ALU.mult))
                did(tt(c(20), c(16), W("sa"), ALU.mult))
                did(tt(c(21), c(19), W("sb"), ALU.mult))
                did(ts(bbar[:, :], W("bx"), c(20), None, ALU.mult))
                stt(bbar[:, :], W("by"), c(21), bbar[:, :], ALU.mult, ALU.add).then_inc(sem("bbar"), 1)
                for b in range(B):
                    g = gate[:, b, 2 * P:3 * P]
                    stt(cga[:, b, :], W("cta"), W("sign1")[:, b:b + 1], g, ALU.mult, ALU.mult).then_inc(sem("cg"), 1)
                    stt(cgb[:, b, :], W("ctb"), W("sign2")[:, b:b + 1], g, ALU.mult, ALU.mult).then_inc(sem("cg"), 1)
                    stt(dg[:, b, :], ident, W("dcol"), g, ALU.mult, ALU.mult).then_inc(sem("cg"), 1)

            def norm(n, centred):
                for b in range(B):
                    if n == 0:
                        eng.wait_ge(sem("x0"), b + 1)
                    else:
                        eng.wait_ge(sem("xr"), 2 * (n - 1) + b + 1)
                    for w in range(NB):
                        i = b * NB + w
                        dve.bn_stats(st[:, i, :], X[:, i, :]).then_inc(sem("stats"), 1)
                    for w in range(NB):
                        i = b * NB + w
                        eng.wait_ge(sem("stats"), NT * n + i + 1)
                        dve.bn_aggr(mv[:, i, :], st[:, i, :]).then_inc(sem("aggr"), 1)
                    eng.wait_ge(sem("aggr"), NT * n + NB * (b + 1))
                    bt = btiles(b)
                    eps = {True: 1e-5, False: 1e-5 if n < 2 else 1.1920928955078125e-07}[centred]
                    if centred:
                        dve.tensor_scalar(var[:, bt], mv[:, bt, 1], eps, None, ALU.add).then_inc(sem("var"), 1)
                    else:
                        tt(msq[:, bt], mv[:, bt, 0], mv[:, bt, 0], ALU.mult).then_inc(sem("msq"), 1)
                        m = 2 * {0: 0, 1: 1, 4: 2, 5: 3}[n] + b + 1
                        eng.wait_ge(sem("msq"), m)
                        dve.scalar_tensor_tensor(out=var[:, bt], in0=msq[:, bt], scalar=eps, in1=mv[:, bt, 1],
                                                 op0=ALU.add, op1=ALU.add).then_inc(sem("var"), 1)
                for b in range(B):
                    eng.wait_ge(sem("rstd"), 2 * n + b + 1)
                    if n:
                        eng.wait_ge(sem("norm_tr"), 2 * (n - 1) + b + 1)
                    for w in range(NB):
                        i = b * NB + w
                        if centred:
                            ins = dve.tensor_scalar(xn[:, i, :], X[:, i, :], mv[:, i, 0:1], rstd[:, i:i + 1],
                                                    ALU.subtract, ALU.mult)
                        else:
                            ins = dve.tensor_scalar(xn[:, i, :], X[:, i, :], rstd[:, i:i + 1], None, ALU.mult)
                        ins.then_inc(sem("xn"), 1)

            def add_residual(u, done, src, base=Xb):
                for b in range(B):
                    eng.wait_ge(sem(done[0]), done[1] + b + 1)
                    if base is Xb:
                        eng.wait_ge(sem("xb"), 2 * {0: 0, 1: 1, 3: 2, 4: 3, 5: 4}[u] + b + 1)
                    if u == 2:
                        eng.wait_ge(sem("xn"), NT * 3)
                    tt(X[:, btiles(b), :].rearrange("p w f -> p (w f)"), bank(src + b),
                       base[:, btiles(b), :].rearrange("p w f -> p (w f)"), ALU.add).then_inc(sem("xr"), 1)

            norm(0, False)
            for i in range(NT):
                eng.wait_ge(sem("qkv_mm"), i + 1)
                tt(qk[:, i, :], bank(6 + i % 2)[:, 0:2 * P], W("rqkv1")[:, 0:2 * P], ALU.add).then_inc(sem("qk"), 1)
                tt(v1[:, i, :, 0:D1], bank(6 + i % 2)[:, 2 * P:3 * P].rearrange("p (h c) -> p h c", h=H1),
                   W("rqkv1")[:, 2 * P:3 * P].rearrange("p (h c) -> p h c", h=H1), ALU.add).then_inc(sem("vv"), 1)
            for b in range(B):
                eng.wait_ge(sem("qk"), NB * (b + 1))
                v = qk[:, btiles(b), :].rearrange("p w (h c) -> p (w h) c", c=D1)
                r1 = rt1[:, btiles(b), :].rearrange("p w (h c) -> p (w h) c", c=D1)
                r2 = rt2[:, btiles(b), :].rearrange("p w (h c) -> p (w h) c", c=D1)
                n, hd = NB * 2 * H1, D1 // 2
                tt(r1, v, W("cos1").unsqueeze(1).to_broadcast([P, n, D1]), ALU.mult).then_inc(sem("rope_t"), 1)
                tt(r2[:, :, 0:hd], v[:, :, hd:D1], W("sin1")[:, 0:hd].unsqueeze(1).to_broadcast([P, n, hd]), ALU.mult)\
                    .then_inc(sem("rope_t"), 1)
                tt(r2[:, :, hd:D1], v[:, :, 0:hd], W("sin1")[:, hd:D1].unsqueeze(1).to_broadcast([P, n, hd]), ALU.mult)\
                    .then_inc(sem("rope_t"), 1)
                eng.wait_ge(sem("rope_t"), 3 * (b + 1))
                tt(v, r1, r2, ALU.add).then_inc(sem("rope"), 1)

            for k in range(NT + 3):
                w = k
                if w < NT:
                    eng.wait_ge(sem("s1_mm"), w + 1)
                    s = PP[w % 2][:, :, :].rearrange("p a (h k) -> p (a h) k", k=P)
                    dve.tensor_reduce(mx1[:, w % 2, :], s, X_AXIS, ALU.max).then_inc(sem("mx1"), 1)
                    eng.wait_ge(sem("mx1"), w + 1)
                    if w >= 2:
                        eng.wait_ge(sem("p1_tr"), w - 1)
                    tt(p1[:, w % 2, :, :], s, mx1[:, w % 2, :].unsqueeze(2).to_broadcast([P, H1, P]), ALU.subtract)\
                        .then_inc(sem("sub1"), 1)
                w = k - 3
                if 0 <= w < NT:
                    eng.wait_ge(sem("ot1_mm"), w + 1)
                    o = bank(7)[:, 0:2 * P].rearrange("p (h c) -> p h c", c=PAD)
                    dve.reciprocal(rc1[:, w % 2, :], o[:, :, D1]).then_inc(sem("rc1"), 1)
                    eng.wait_ge(sem("rc1"), w + 1)
                    tt(otok[:, w, :].rearrange("p (h c) -> p h c", c=D1), o[:, :, 0:D1],
                       rc1[:, w % 2, :].unsqueeze(2).to_broadcast([P, H1, D1]), ALU.mult).then_inc(sem("otok1"), 1)
            add_residual(0, ("proj_mm", 0), 2)
            norm(1, False)
            ssm_tables()
            add_residual(1, ("down_mm", 0), 6)

            norm(2, True)
            eng.wait_ge(sem("u_mm"), 1)
            eng.wait_ge(sem("rot"), 2)
            tt(tA[:, :], bank(2), er[:, :], ALU.mult).then_inc(sem("rotin"), 1)
            tt(tB[:, :], bank(3), ei[:, :], ALU.mult).then_inc(sem("rotin"), 1)
            eng.wait_ge(sem("rotin"), 2)
            tt(uw[:, :], tA[:, :], tB[:, :], ALU.add).then_inc(sem("scan_in"), 1)
            eng.wait_ge(sem("scan_in"), 1)
            eng.wait_ge(sem("rho"), 1)
            dve.tensor_tensor_scan(xs[:, :], col[:, 2:3].to_broadcast([P, T]), uw[:, :], 0.0, ALU.mult, ALU.add)\
               .then_inc(sem("scan"), 1)
            eng.wait_ge(sem("scan"), 1)
            tt(uw[:, :], xs[:, :], er[:, :], ALU.mult).then_inc(sem("rotout"), 1)
            tt(uw2[:, :], xs[:, :], ei[:, :], ALU.mult).then_inc(sem("rotout"), 1)
            add_residual(2, ("y_mm", 0), 6, X)
            norm(3, True)
            add_residual(3, ("down_mm", 2), 6)

            norm(4, False)
            for i in range(NT):
                b, w = i // NB, i % NB
                eng.wait_ge(sem("qkv_mm"), NT + i + 1)
                tt(qk[:, i, :], bank(6 + i % 2)[:, 0:2 * P], W("rqkv3")[:, 0:2 * P], ALU.add).then_inc(sem("qk"), 1)
                tt(v3[:, btiles(b), w, :, 0:D3],
                   bank(6 + i % 2)[:, 2 * P:3 * P].rearrange("p (g h c) -> p g h c", g=NG3, h=G3),
                   W("rqkv3")[:, 2 * P:3 * P].rearrange("p (g h c) -> p g h c", g=NG3, h=G3), ALU.add)\
                    .then_inc(sem("vv"), 1)
            for b in range(B):
                eng.wait_ge(sem("qk"), NT + NB * (b + 1))
                v = qk[:, btiles(b), :].rearrange("p w (r c) -> p (w r) c", c=G3)
                r1 = rt1[:, btiles(b), :].rearrange("p w (r c) -> p (w r) c", c=G3)
                r2 = rt2[:, btiles(b), :].rearrange("p w (r c) -> p (w r) c", c=G3)
                n = NB * 64
                tt(r1, v, W("cos3").unsqueeze(2).to_broadcast([P, n, G3]), ALU.mult).then_inc(sem("rope_t3"), 1)
                for e in range(2):
                    tt(r2[:, e:n:2, :], v[:, 1 - e:n:2, :],
                       W("sin3")[:, e:n:2].unsqueeze(2).to_broadcast([P, n // 2, G3]), ALU.mult)\
                        .then_inc(sem("rope_t3"), 1)
                eng.wait_ge(sem("rope_t3"), 3 * (b + 1))
                tt(v, r1, r2, ALU.add).then_inc(sem("rope3"), 1)
            for n in range(2 * B):
                eng.wait_ge(sem("split1"), n + 1)
                tt(res3[:, n, :], bank(n), split[:, n, 0, :], ALU.subtract).then_inc(sem("res3"), 1)

            def l3_maxima(it, s):
                h, w = s // NB, s % NB
                eng.wait_ge(sem("s3_mm"), it * 16 + s + 1)
                dve.tensor_reduce(nm3[:, s:s + 1], bank(s % 2), X_AXIS, ALU.max, negate=True).then_inc(sem("max3"), 1)

            def l3_split_max(it):
                eng.wait_ge(sem("max3"), it * 16 + 16)
                if not (isinstance(it, int) and it == 0):
                    eng.wait_ge(sem("m3_tr"), it)
                dve.tensor_copy(ms3[:, 0, :], nm3[:, :]).then_inc(sem("ms3_t"), 1)
                eng.wait_ge(sem("ms3_t"), it * 3 + 1)
                tt(nr3[:, :], nm3[:, :], ms3[:, 0, :], ALU.subtract).then_inc(sem("ms3_t"), 1)
                eng.wait_ge(sem("ms3_t"), it * 3 + 2)
                dve.tensor_copy(ms3[:, 1, :], nr3[:, :]).then_inc(sem("ms3_t"), 1)
                eng.wait_ge(sem("ms3_t"), it * 3 + 3)
                tt(ms3[:, 2, :], nr3[:, :], ms3[:, 1, :], ALU.subtract).then_inc(sem("ms3"), 1)

            def l3_tokens(it):
                eng.wait_ge(sem("ot3_mm"), it + 1)
                o = bank(7).rearrange("p (w h c) -> p w h c", w=NB, h=G3)
                dve.reciprocal(rc3[:, :, :], o[:, :, :, D3]).then_inc(sem("rc3"), 1)
                eng.wait_ge(sem("rc3"), it + 1)
                tt(o3[:, :, :, :].rearrange("p w i f -> p w (i f)")[:, :, bass.ds(it * (G3 * D3), G3 * D3)]
                   .rearrange("p w (h c) -> p w h c", h=G3),
                   o[:, :, :, 0:D3], rc3[:, :, :].unsqueeze(3).to_broadcast([P, NB, G3, D3]), ALU.mult)\
                    .then_inc(sem("otok3"), 1)

            for s in range(16):
                l3_maxima(0, s)
            l3_split_max(0)
            with eng.Fori(0, NIT - 1) as it:
                for s in range(16):
                    l3_maxima(it + 1, s)
                l3_split_max(it + 1)
                l3_tokens(it)
            l3_tokens(NIT - 1)
            add_residual(4, ("proj_mm", 2), 2)
            norm(5, False)
            for k in range(8):
                b, c = k // 4, k % 4
                eng.wait_ge(sem("fc_mm"), 2 * k + 2)
                eng.wait_ge(sem("sg3"), k + 1)
                dve.scalar_tensor_tensor(out=gT[:, c, half(b)], in0=bank(2 * (k % 2)), scalar=W("bfc")[:, c:c + 1],
                                         in1=sg3[:, k % 2, :], op0=ALU.add, op1=ALU.mult).then_inc(sem("gT"), 1)
            add_residual(5, ("down_mm", 4), 6)


def _pack(spec, parts):
    import numpy as np
    cols = []
    for name, width in spec.items():
        a = parts[name]
        a = np.asarray(a, np.float32).reshape(a.shape[0], -1)
        assert a.shape[1] == width, name
        if a.shape[0] < P:
            a = np.concatenate([a, np.zeros((P - a.shape[0], width), np.float32)])
        cols.append(a)
    return np.ascontiguousarray(np.concatenate(cols, 1))


def _rope_angles(n, dim):
    import numpy as np
    inv = np.float32(1.0) / np.float32(10000.0) ** (np.arange(0, dim, 2, dtype=np.float32) / np.float32(dim))
    return np.arange(n, dtype=np.float32)[:, None] * inv[None, :].astype(np.float32)


def _layout(inp):
    import numpy as np
    f = {k: np.asarray(v) for k, v in inp.items()}
    z = {}

    def chunks(w, ids):
        return np.concatenate([w[:, P * j:P * (j + 1)] for j in ids], 1)

    def rows_to_cols(v, ids=None):
        v = v.reshape(-1, P)
        return (v if ids is None else v[list(ids)]).T

    def stacked(w):
        return w.reshape(4, P, P).transpose(1, 0, 2)

    p = np.arange(P)
    z["ident"], z["ones"] = np.eye(P), np.ones((P, P))
    ws = f["L0_cond_W_self"]
    z["wsv"], z["wsq"] = ws[:, :D].T, ws[:, D:].T
    z["wq"] = f["L0_cond_Wq"].transpose(2, 0, 1)
    z["wk"] = f["L0_cond_Wk"].transpose(2, 0, 1)
    z["wo"] = f["L0_cond_Wout"].reshape(2, P, D).transpose(2, 0, 1)
    z["kmask0"] = np.repeat((p[:, None] // 8 == np.arange(H0)) * np.float32(1 / np.sqrt(8)), M0, 1)
    r = np.arange(RC)
    z["vmask0"] = np.stack([HC * c + r[:, None] // M0 == p[None, :] // 8 for c in range(NC0)], 1)
    z["bself"] = rows_to_cols(f["L0_cond_b_self"])
    z["bq0"], z["bk0"], z["bout0"] = f["L0_cond_bq"].T, f["L0_cond_bk"].T, f["L0_cond_bout"].T
    z["cond"] = f["cond_1024"].T

    ada, bada = f["L1_cond_W_ada"], f["L1_cond_b_ada"]
    wm, bm = f["L2_cond_Wm"], f["L2_cond_bm"]
    wc, bc = f["L2_cond_Wc"], f["L2_cond_bc"]
    z["wcol1"], z["wgate1"] = chunks(ada, (0, 1, 3, 4)), chunks(ada, (2, 5))
    z["wt1"] = f["L3_cond_w_t1"]
    z["wqkv1"], z["wout1"], z["wff1_1"] = f["L1_cond_W_qkv"], f["L1_cond_W_out"], f["L1_cond_W_ff1"]
    z["wff2_1"] = stacked(f["L1_cond_W_ff2"])
    z["kmask1"] = p[:, None] // D1 == np.arange(H1)
    ang = _rope_angles(P, D1)
    z["cos1"] = np.repeat(np.cos(ang), 2, 1)
    z["sin1"] = np.repeat(np.sin(ang), 2, 1) * np.where(np.arange(D1) < D1 // 2, -1.0, 1.0)
    z["bff1_1"] = rows_to_cols(f["L1_cond_b_ff1"])
    z["bmod"] = np.concatenate([rows_to_cols(bada, (0, 1, 3, 4)), rows_to_cols(bm, (0, 1, 3, 4)),
                                rows_to_cols(bc), rows_to_cols(f["L3_cond_b_t1"])], 1)
    z["bmodd"] = rows_to_cols(f["L3_cond_b_t2"])
    z["s1a"], z["s1b"] = rows_to_cols(f["L1_cond_scale1"]), rows_to_cols(f["L1_cond_scale2"])
    z["g3a"], z["g3b"] = rows_to_cols(f["L3_cond_g1"]), rows_to_cols(f["L3_cond_g2"])

    z["wcol2"] = np.concatenate([chunks(wm, (0, 1, 3, 4)), wc], 1)
    z["wgate2"] = chunks(wm, (2, 5))
    z["wff1_2"], z["wff2_2"] = f["L2_cond_W1"], stacked(f["L2_cond_W2"])
    bre, bim, cre, cim = (f["L2_cond_" + n] for n in ("B_re", "B_im", "C_re", "C_im"))
    z["bx"] = np.concatenate([bre, bim, bim, bre])
    z["by"] = np.concatenate([bim, bre, bre, bim])
    z["cta"] = np.concatenate([cre.T, cim.T] * 2)
    z["ctb"] = np.concatenate([cim.T, cre.T] * 2)
    z["steps"] = np.tile(np.arange(T), (P, 1))
    for n in ("lam_re", "lam_im", "log_step"):
        src = f["L2_cond_" + {"lam_re": "Lam_re", "lam_im": "Lam_im", "log_step": "log_step"}[n]]
        z[n] = np.tile(src, 4)[:, None]
    q = p // 32
    z["sa"] = np.where(q == 3, -1.0, 1.0)[:, None]
    z["sb"] = np.where(q == 0, -1.0, 1.0)[:, None]
    own = (p[:, None] // 64 == np.arange(B)[None, :])
    z["sign1"] = own * np.where(q % 2 == 0, 2.0, -2.0)[:, None]
    z["sign2"] = own * -2.0
    z["dcol"] = rows_to_cols(f["L2_cond_D_diag"])
    z["bff1_2"] = rows_to_cols(f["L2_cond_b1"])
    z["halfpi"] = np.full((P, 1), np.pi / 2)

    hd, g, c = np.meshgrid(np.arange(D3), np.arange(NG3), np.arange(G3), indexing="ij")
    perm = np.empty(P, int)
    perm[(g * 32 + hd * G3 + c).ravel()] = ((g * G3 + c) * D3 + hd).ravel()
    wqkv, bqkv = f["L3_cond_w_qkv"], f["L3_cond_b_qkv"]
    order = np.concatenate([perm, P + perm, 2 * P + np.arange(P)])
    z["wcol3"], z["wqkv3"], z["wao"] = f["L3_cond_w_t2"], wqkv[:, order], f["L3_cond_w_ao"]
    z["wfc"], z["wfo"] = f["L3_cond_w_fc"], stacked(f["L3_cond_w_fo"])
    ang = _rope_angles(T, D3).reshape(NB, P, D3 // 2).transpose(1, 0, 2)
    sign = np.where(np.arange(D3) % 2 == 0, -1.0, 1.0)
    z["cos3"] = np.tile(np.repeat(np.cos(ang), 2, 2), (1, 1, 2 * NG3))
    z["sin3"] = np.tile(np.repeat(np.sin(ang), 2, 2) * sign, (1, 1, 2 * NG3))
    z["bfc"] = rows_to_cols(f["L3_cond_b_fc"])

    z["wbias0"], z["bbias0"] = f["L0_cond_w_bias"][None], f["L0_cond_b_bias"].reshape(1, 1)
    z["rgate"] = np.concatenate([bada.reshape(6, P)[[2, 5]].ravel(), bm.reshape(6, P)[[2, 5]].ravel()])[None]
    z["rqkv1"], z["rout1"], z["rff2_1"] = (f["L1_cond_" + n][None] for n in ("b_qkv", "b_out", "b_ff2"))
    z["rff2_2"] = f["L2_cond_b2"][None]
    z["rqkv3"], z["rao"], z["rfo"] = bqkv[order][None], f["L3_cond_b_ao"][None], f["L3_cond_b_fo"][None]

    adj = f["mask_BxSxSx11_ik0"]
    adj = [adj[:, :, :M0, :], adj[:, :M0, :, :].transpose(0, 2, 1, 3)]
    adj = np.stack([a.reshape(NT, P, M0 * L).transpose(1, 0, 2).reshape(P, NT * M0 * L) for a in adj])
    return {
        "w0": _pack(W0, z), "w1": _pack(W1, z), "w2": _pack(W2, z), "w3": _pack(W3, z),
        "rows": np.concatenate([z[n].reshape(1, -1) for n in ROWS], 1).astype(np.float32),
        "xt": np.ascontiguousarray(f["x"].reshape(B * T, D).T),
        "adj": np.ascontiguousarray(adj),
    }


def kernel(**inputs):
    import numpy as np
    import concourse.bacc as bacc
    from concourse.bass_utils import run_bass_kernel_spmd

    nc = bacc.Bacc("TRN2", target_bir_lowering=False, num_devices=1)
    arrays = _layout(inputs)
    args = [nc.dram_tensor(n, arrays[n].shape, mybir.dt.from_np(arrays[n].dtype), kind="ExternalInput").ap()
            for n in ("w0", "w1", "w2", "w3", "rows", "xt", "adj")]
    out = nc.dram_tensor("out", (P, B * T), F32, kind="ExternalOutput").ap()
    q_scr = nc.dram_tensor("q_scr", (NIT, 3, 32, T), BF16, kind="Internal").ap()
    k_scr = nc.dram_tensor("k_scr", (NIT, 5, 32, T), BF16, kind="Internal").ap()
    build_program(nc, *args, out, q_scr, k_scr)
    r = run_bass_kernel_spmd(nc, [arrays], core_ids=[0])
    y = np.asarray(r.results[0]["out"]).reshape(P, NT, D)
    return np.ascontiguousarray(y.transpose(1, 0, 2)).reshape(B, T, D)
```

```python
from contextlib import ExitStack

import concourse.bass as bass
from concourse import mybir

F32 = mybir.dt.float32
BF16 = mybir.dt.bfloat16
I32 = mybir.dt.int32
ALU = mybir.AluOpType
ACT = mybir.ActivationFunctionType
X_AXIS = mybir.AxisListType.X

P = 128
B, T, D = 2, 512, 128
NB = T // P
NT = B * NB
L, M0 = 11, 20
H0, H1, H3 = 16, 8, 16
HC = 6
NC0 = 3
RC = HC * M0
RLAST = H0 * M0 - 2 * RC
D1 = D // H1
D3 = D // H3
PAD = 32
G3 = 4
NG3 = H3 // G3
NIT = B * NG3
UNITS = 2 * NIT
NROW = 9 * D3
AUG = 96
NEG = -9000000000000000.0
ROUND = 1.5 * 2.0 ** 23
ROUND12 = 1.5 * 2.0 ** 11
TWO_PI = 6.283185307179586
TURN = (6.28125, 0.0019350051879882812, 3.0199159819e-07)

W0 = dict(ident=P, wsv=P, wsq=P, wq=2 * P, wk=2 * P, wo=2 * P, kmask0=H0, vmask0=NC0 * H0,
          bself=1, bq0=2, bk0=2, bout0=2, cond=2, steps_hi=T // 16, steps_lo=16,
          lam_re=1, lam_im=1, log_step=1, sa=1, sb=1, sign1=2, sign2=2, dcol=1, halfpi=1)
WM = dict(wcol1=4 * P, wgate1=2 * P, wcol2=6 * P, wgate2=2 * P, wt1=2 * P, wcol3=4 * P,
          bmod=12, bmodd=4, s1a=1, s1b=1, g3a=1, g3b=1)
W1 = dict(wqkv1=3 * P, wout1=P, wff1_1=4 * P, wff2_1=4 * P, kmask1=H1, cos1=D1, sin1=D1, bff1_1=4)
W2 = dict(wff1_2=4 * P, wff2_2=4 * P, bx=P, by=P, cta=P, ctb=P, bff1_2=4)
W3 = dict(wqkv3=3 * P, wao=P, wfc=8 * P, wfo=4 * P, cos3=NB * D3, sin3=NB * D3, bfc=8)
NROWS = 4
ROWS = dict(wbias0=L, bbias0=1, rgate=4 * P, rqkv1=3 * P, rout1=P, rff2_1=P, rff2_2=P, rqkv3=3 * P,
            rao=P, rfo=P)


def build_program(nc, w0, wm, w1, w2, w3, rows, xt_in, adj_in, out, q_scr, k_scr):
    with ExitStack() as ctx:
        sems = {}

        def sem(name):
            if name not in sems:
                sems[name] = ctx.enter_context(nc.semaphore(name))
            return sems[name]

        def sb(name, shape, dt=F32):
            return ctx.enter_context(nc.sbuf_tensor(name, shape, dt))

        def arena(name, words):
            return [sb(name, [P, words]), 0]

        def carve(a, shape, dt=F32):
            n = 1
            for k in shape[1:]:
                n *= k
            words = n if dt in (F32, I32) else n // 2
            v = a[0][0:shape[0], a[1]:a[1] + words]
            a[1] += words
            if dt is not F32:
                v = v.bitcast(dt)
            names = "abcd"[:len(shape) - 1]
            if len(names) > 1:
                v = v.rearrange(f"p ({' '.join(names)}) -> p {' '.join(names)}",
                                **{c: k for c, k in zip(names, shape[1:])})
            return v

        packed = {}
        tiles = {}
        for tag, spec in (("w0", W0), ("wm", WM), ("w1", W1), ("w2", W2), ("w3", W3), ("rw", ROWS)):
            n = sum(spec.values())
            tiles[tag] = sb(tag + "_sb", [P, n])
            at = 0
            for name, width in spec.items():
                packed[name] = tiles[tag][:, at:at + width]
                at += width

        def W(name):
            return packed[name]

        ident = W("ident")
        attn = arena("attn", 23 * 1024)
        early = arena("early", 4 * 1024)
        mlp = arena("mlp", 4 * B * T)
        gT = carve(mlp, [P, 4, B * T])
        mlp[1] = 0
        rows_in = carve(mlp, [1, sum(ROWS.values())])

        adj = [carve(attn, [P, NT * M0 * L], I32) for d in range(2)]
        adj_w = [carve(attn, [P, NT * M0, L]), carve(mlp, [P, NT * M0, L])]
        msum = carve(attn, [P, 2, NT * M0])
        mbias = carve(attn, [P, 2, NT * M0])
        mask = carve(attn, [P, 2, NT * M0])
        mpen = carve(attn, [P, 2, NT * M0])
        mtb = carve(attn, [P, 2, NT * M0])
        qhT = [carve(attn, [P, B * T]) for d in range(2)]
        kblk = [carve(attn, [P, H0, M0]) for j in range(4)]
        kvrep = [carve(attn, [P, NC0 * HC, M0]) for b in range(B)]
        vblk = [carve(attn, [RC, NC0, P]) for j in range(4)]
        w0p = carve(attn, [P, 4, 2, H0 * M0])
        w0T_at = attn[1]
        w0T = [carve(attn, [RC, NC0, T]) for j in range(4)]
        l0sum = carve(attn, [P, B, T])
        xoT = carve(attn, [P, B * T])
        attn[1] = w0T_at
        tA, tB, steps = (carve(attn, [P, T]) for j in range(3))
        xT = carve(early, [P, B * T])
        sfT = carve(early, [P, B * T])
        keep = carve(early, [1, B * T])
        qrow = carve(early, [1, B * P])
        bc_cond = carve(early, [P, B, P])
        bc_silu = carve(early, [P, B, P])
        col = sb("col", [P, 24])
        er, ei = sb("er", [P, T]), sb("ei", [P, T])
        ones = sb("ones", [P, P])
        mx0 = sb("mx0", [P, 4, 2 * H0])
        sm0 = sb("sm0", [P, 4, 2 * H0])
        rs0 = sb("rs0", [P, 4, 2 * H0])
        bout_sum = sb("bout_sum", [P, 1])

        silu_c = sb("silu_c", [P, B])
        modc = sb("modc", [P, 12, B])
        modp = sb("modp", [P, 12, B])
        modd = sb("modd", [P, 4, B])
        modq = sb("modq", [P, 4, B])
        sgt = sb("sgt", [P, B])
        tpe = sb("tpe", [P, B])
        scl = sb("scl", [P, 6, B])
        shf = sb("shf", [P, 6, B])
        shtmp = sb("shtmp", [P, B])
        gate = sb("gate", [P, B, 4 * P])
        wout1g = sb("wout1g", [P, B, P])
        wff2g = [sb(f"wff2g{n}", [P, B, 4, P]) for n in range(2)]
        bres = sb("bres", [P, 3, B, P])

        X = sb("X", [P, NT, P])
        Xb = sb("Xb", [P, NT, P])
        st = sb("st", [P, NT, 6])
        mv = sb("mv", [P, NT, 2])
        msq = sb("msq", [P, NT])
        var = sb("var", [P, NT])
        rstd = sb("rstd", [P, NT])
        mhalf = sb("mhalf", [P, NT])
        xn = sb("xn", [P, NT, P])
        early[1] = 0
        qk = carve(early, [P, NT, 2 * P])
        hT = carve(early, [P, B * T])
        oT = carve(early, [P, B * T])

        attn[1] = 0
        v1 = carve(attn, [P, NT, H1, PAD])
        qT1 = carve(attn, [P, B * T])
        kT1 = carve(attn, [P, B * T])
        kb1 = carve(attn, [P, 2, H1, P])
        p1 = carve(attn, [P, 2, H1, P])
        pT1 = carve(attn, [P, 2, H1, P])
        os1 = carve(attn, [P, 2, 2, P])
        otok = carve(attn, [P, NT, P])
        mx1 = sb("mx1", [P, 2, H1])
        rc1 = sb("rc1", [P, 2, H1])

        attn[1] = 0
        v3 = carve(attn, [P, NIT, NB, G3, PAD])
        qa = [carve(attn, [P, G3, T], BF16) for j in range(2)]
        ka = [carve(attn, [P, G3, T], BF16) for j in range(2)]
        split = carve(attn, [P, 2 * B, 3, T], BF16)
        res3 = carve(attn, [P, 2 * B, T])
        tail = attn[1]
        p3 = carve(attn, [P, 2, 2, NB, T])
        o3 = carve(attn, [P, NB, NIT, G3 * D3])
        mlp[1] = 0
        vg = [carve(mlp, [P, NB, G3, PAD]) for j in range(2)]
        os3 = carve(mlp, [P, 2, T // 2])
        nm3 = sb("nm3", [P, 2, 2 * NB])
        zeros = sb("zeros", [P, 2 * NB])
        nr3 = sb("nr3", [P, 2 * NB])
        ms3 = sb("ms3", [P, P // (2 * NB), 2 * NB], BF16)
        mT3 = sb("mT3", [3 * 2 * NB, 2, P], BF16)
        identb = sb("identb", [P, P], BF16)
        rc3 = sb("rc3", [P, NB, 2])

        attn[1] = tail
        rt1 = carve(attn, [P, NT, 2 * P])
        rt2 = carve(attn, [P, NT, 2 * P])
        cos3 = carve(attn, [P, NB, 2 * NG3, D3])
        sin3 = carve(attn, [P, NB, 2 * NG3, D3])
        ua = carve(attn, [P, T])
        ub = carve(attn, [P, T])
        uw = carve(attn, [P, T])
        uw2 = carve(attn, [P, T])
        xs = carve(attn, [P, T])
        bbar = carve(attn, [P, P])
        bbT = carve(attn, [P, P])
        cga = carve(attn, [P, B, P])
        cgb = carve(attn, [P, B, P])
        dg = carve(attn, [P, B, P])
        attn[1] = tail
        sg3 = carve(attn, [P, 2, T])

        PP = [ctx.enter_context(nc.psum_tensor(f"pp{j}", [P, 2, 512], F32)) for j in range(4)]

        def bank(k):
            return PP[k // 2][:, k % 2, :]

        block = ctx.enter_context(nc.Block())
        pe, dve, act, pool = nc.tensor, nc.vector, nc.scalar, nc.gpsimd

        def qkv_bank(i):
            return (6 + i) % 8 if i < 6 else i

        def tile_cols(i):
            return slice(i * P, (i + 1) * P)

        def half(b):
            return slice(b * T, (b + 1) * T)

        def btiles(b):
            return slice(b * NB, (b + 1) * NB)

        @block.sync
        def _(sp):
            sp.dma_start(tiles["w0"][:, :], w0).then_inc(sem("ld_w0"), 16)
            sp.dma_start(adj[0][:, :], adj_in[0]).then_inc(sem("ld_adj0"), 16)
            sp.dma_start(tiles["wm"][:, :], wm).then_inc(sem("ld_wm"), 16)
            sp.dma_start(tiles["w2"][:, :], w2).then_inc(sem("ld_w2"), 16)
            sp.dma_start(tiles["w3"][:, :], w3).then_inc(sem("ld_w3"), 16)

            def store(n):
                b, scr = n // 2, k_scr if n % 2 else q_scr
                for part in range(5 if n % 2 else 3):
                    sp.wait_ge(sem(f"split{part % 3 + 1}"), n + 1)
                    sp.dma_start(scr[b * NG3:(b + 1) * NG3, part, :, :], split[:, n, part % 3, :])\
                      .then_inc(sem(f"st_qk{b}"), 16)

            def load(u, par, hp):
                step_q = q_scr.rearrange("n i (d c) t -> (n i d) (c t)", c=G3)
                step_k = k_scr.rearrange("n i (d c) t -> (n i d) (c t)", c=G3)
                half_row = slice(hp * 2 * T, (hp + 1) * 2 * T)
                heads = slice(2 * hp, 2 * hp + 2)
                it = (u - hp) // 2 if isinstance(u, int) else u
                qs = step_q[bass.ds(it * (3 * D3), 3 * D3), half_row]
                ks = step_k[bass.ds(it * (5 * D3), 3 * D3), half_row]
                row = G3 * T
                sp.dma_start(qa[par][0:NROW, heads, :].rearrange("p c t -> p (c t)"),
                             qs.unsqueeze(0).to_broadcast([3, 3 * D3, 2 * T])).then_inc(sem(f"ld_q{par}{hp}"), 16)
                sp.dma_start(ka[par][0:NROW, heads, :].rearrange("p c t -> p (c t)"),
                             bass.AP(ks.tensor, ks.offset, [[D3 * row, 3], [row, 3 * D3], [1, 2 * T]]))\
                  .then_inc(sem(f"ld_q{par}{hp}"), 16)

            def maxima(u, par, hp):
                sp.wait_ge(sem("mT3"), u + 1)
                sp.dma_start(qa[par][AUG:AUG + 3, 2 * hp:2 * hp + 2, :].rearrange("p c t -> p (c t)"), mT3[:, hp, :])\
                  .then_inc(sem(f"ld_m{par}{hp}"), 16)

            sp.wait_ge(sem("zero3"), 4)
            store(0)
            store(1)
            sp.wait_ge(sem("st_qk0"), 16 * 8)
            for u in range(4):
                load(u, u // 2, u % 2)
            store(2)
            store(3)
            maxima(0, 0, 0)
            maxima(1, 0, 1)

            def slot(u, it, par, hp):
                sp.wait_ge(sem("st3"), u * 4 + 4)
                load(it + 2, par, hp)
                maxima(u + 2, 1 - par, hp)

            sp.wait_ge(sem("st_qk1"), 16 * 8)
            with sp.Fori(0, NIT // 2 - 1) as pair:
                for j in range(4):
                    slot(pair * 4 + j, pair * 2 + j // 2, j // 2, j % 2)
            maxima(UNITS - 2, 1, 0)
            maxima(UNITS - 1, 1, 1)

            for b in range(B):
                sp.wait_ge(sem("xr"), 2 * 5 + b + 1)
                sp.dma_start(out[:, b * T:(b + 1) * T], X[:, btiles(b), :].rearrange("p w f -> p (w f)"))\
                  .then_inc(sem("st_out"), 16)
            sp.wait_ge(sem("st_out"), 32)

        freed = {}

        def claim(eng, k, name, value):
            if k in freed:
                eng.wait_ge(sem(freed[k][0]), freed[k][1])
            freed[k] = (name, value)

        @block.tensor
        def _(eng):
            def mm(o, l, r, start=True, stop=True):
                return pe.matmul(o, l, r, start=start, stop=stop)

            def bias_rows(j, k):
                lo, hi = 512 * j, min(512 * (j + 1), sum(ROWS.values()))
                claim(eng, k, "rows", j + 1)
                mm(bank(k)[:, 0:hi - lo], ones[0:1, :], rows_in[:, lo:hi]).then_inc(sem("rows_mm"), 1)

            eng.wait_ge(sem("ld_xT"), 16)
            eng.wait_ge(sem("consts"), 1)
            for b in range(B):
                claim(eng, 6 + b, "keep", b + 1)
                mm(bank(6 + b)[0:1, :], ones[:, 0:1], xT[:, half(b)]).then_inc(sem("rowsum"), 1)
            eng.wait_ge(sem("ld_w0"), 16)
            claim(eng, 5, "qrow", 1)
            for b in range(B):
                last = mm(bank(5)[0:1, b * P:(b + 1) * P], W("cond")[:, b:b + 1], W("wsq"))
            last.then_inc(sem("qrow_mm"), 1)
            eng.wait_ge(sem("ld_rows"), 16)
            bias_rows(0, 4)
            for b in range(B):
                claim(eng, b, "sfT", b + 1)
                mm(bank(b), W("wsv"), xT[:, half(b)], True, False)
                eng.wait_ge(sem("keep"), b + 1)
                eng.wait_ge(sem("qrow"), 1)
                mm(bank(b), qrow[:, b * P:(b + 1) * P], keep[:, half(b)], False, True).then_inc(sem("sf_mm"), 1)
            for b in range(B):
                eng.wait_ge(sem("sfT"), b + 1)
                for d in range(2):
                    n = 2 * b + d
                    claim(eng, 2 + n, "qhT", n + 1)
                    mm(bank(2 + n), W("wq")[:, tile_cols(d)], sfT[:, half(b)]).then_inc(sem("qh_mm"), 1)
            claim(eng, 6, "kblk", 4)
            for b in range(B):
                for d in range(2):
                    n = 2 * b + d
                    mm(bank(6)[:, 32 * n:32 * n + M0], W("wk")[:, tile_cols(d)], sfT[:, b * T:b * T + M0])\
                        .then_inc(sem("kh_mm"), 1)
            for j in range(1, NROWS):
                bias_rows(j, (7, 0, 1)[j - 1])
            def l0_scores(g):
                b, d, h = g // 4, (g // 2) % 2, g % 2
                pr = PP[g % 2]
                claim(eng, 2 * (g % 2), "s0_m", g + 1)
                claim(eng, 2 * (g % 2) + 1, "s0_m", g + 1)
                eng.wait_ge(sem("kblk"), 2 * b + d + 1)
                eng.wait_ge(sem("qhT"), 2 * b + d + 1)
                for t in range(2):
                    i = b * NB + 2 * h + t
                    last = mm(pr[:, t, 0:H0 * M0], qhT[d][:, tile_cols(i)],
                              kblk[2 * b + d][:, :, :].rearrange("p h m -> p (h m)"))
                last.then_inc(sem("s0_mm"), 1)

            def l0_turn(g):
                pr = PP[2 + g % 2]
                claim(eng, 4 + 2 * (g % 2), "w0T", 2 * g + 2)
                claim(eng, 5 + 2 * (g % 2), "w0T", 2 * g + 2)
                eng.wait_ge(sem("w0n"), g + 1)
                for t in range(2):
                    for c in range(NC0):
                        n = RC if c < 2 else RLAST
                        last = pe.transpose(pr[0:n, t, c * P:(c + 1) * P],
                                            w0p[:, g % 4, t, c * RC:c * RC + n], ident)
                last.then_inc(sem("w0_tr"), 1)

            def l0_out(b, d):
                if d == 0:
                    claim(eng, 2 * b, "l0sum", b + 1)
                eng.wait_ge(sem("w0T"), 8 * b + 4 * d + 4)
                eng.wait_ge(sem("vblk"), 2 * b + d + 1)
                for c in range(NC0):
                    n = RC if c < 2 else RLAST
                    last = mm(bank(2 * b), vblk[2 * b + d][0:n, c, :], w0T[2 * b + d][0:n, c, :],
                              d == 0 and c == 0, d == 1 and c == NC0 - 1)
                if d:
                    last.then_inc(sem("o0_mm"), 1)

            def l0_back(b):
                k = 1 + 2 * b
                claim(eng, k, "x0", b + 1)
                eng.wait_ge(sem("l0x"), b + 1)
                for w in range(NB):
                    last = pe.transpose(bank(k)[:, tile_cols(w)], xoT[:, tile_cols(b * NB + w)], ident)
                last.then_inc(sem("l0_back"), 1)

            for g in range(4):
                l0_scores(g)

            claim(eng, 4, "modc", 1)
            eng.wait_ge(sem("ld_wm"), 16)
            eng.wait_ge(sem("silu_c"), 1)
            eng.wait_ge(sem("bcast"), 2)
            cond = W("cond")
            for j in range(12):
                lhs, rhs = ((W("wcol1"), silu_c[:, :]) if j < 4 else
                            (W("wcol2"), cond) if j < 10 else (W("wt1"), cond))
                at = j if j < 4 else j - 4 if j < 10 else j - 10
                last = mm(bank(4)[:, 2 * j:2 * j + 2], lhs[:, tile_cols(at)], rhs)
            last.then_inc(sem("mod_mm"), 1)
            for b in range(B):
                claim(eng, 5 + b, "gate", b + 1)
                mm(bank(5 + b)[:, 0:2 * P], bc_silu[:, b, :], W("wgate1"))
                mm(bank(5 + b)[:, 2 * P:4 * P], bc_cond[:, b, :], W("wgate2")).then_inc(sem("gate_mm"), 1)
            claim(eng, 7, "modd", 1)
            eng.wait_ge(sem("tpe"), 1)
            for j in range(4):
                last = mm(bank(7)[:, 2 * j:2 * j + 2], W("wcol3")[:, tile_cols(j)], tpe[:, :])
            last.then_inc(sem("modd_mm"), 1)

            for b in range(B):
                eng.wait_ge(sem("kvrep"), b + 1)
                for d in range(2):
                    n = 2 * b + d
                    claim(eng, 4 + n, "vblk", n + 1)
                    for c in range(NC0):
                        last = mm(bank(4 + n)[0:RC, c * P:(c + 1) * P],
                                  kvrep[b][:, HC * c:HC * c + HC, :].rearrange("p h m -> p (h m)"),
                                  W("wo")[:, tile_cols(d)])
                    last.then_inc(sem("vf_mm"), 1)

            for g in range(8):
                if g + 4 < 8:
                    l0_scores(g + 4)
                l0_turn(g)
                if g == 4:
                    l0_out(0, 0)
                if g == 5:
                    l0_out(0, 1)
            l0_out(1, 0)
            l0_out(1, 1)
            l0_back(0)
            l0_back(1)

            def norm_turn(n, b):
                claim(eng, 4 + b, "hT", 2 * n + b + 1)
                eng.wait_ge(sem("xn"), NT * n + NB * (b + 1))
                for w in range(NB):
                    last = pe.transpose(bank(4 + b)[:, tile_cols(w)], xn[:, b * NB + w, :], ident)
                last.then_inc(sem("norm_tr"), 1)

            def mlp_up(n, w):
                m = 3 if n else 1
                norm_turn(m, 0)
                for b in range(B):
                    eng.wait_ge(sem("hT"), 2 * m + b + 1)
                    for c in range(4):
                        if b == 0 and c == 2:
                            norm_turn(m, 1)
                        k = 4 * b + c
                        claim(eng, k % 4, "gT", 8 * n + k + 1)
                        mm(bank(k % 4), w[:, tile_cols(c)], hT[:, half(b)]).then_inc(sem("up_mm"), 1)

            def mlp_down(n, w):
                for b in range(B):
                    claim(eng, 6 + b, "xr", 2 * {0: 1, 1: 3, 2: 5}[n] + b + 1)
                    eng.wait_ge(sem("gT"), 8 * n + 4 * b + 4)
                    for wt in range(NB):
                        for c in range(4):
                            last = mm(bank(6 + b)[:, tile_cols(wt)], gT[:, c, tile_cols(b * NB + wt)], w(b, c),
                                      c == 0, c == 3)
                    last.then_inc(sem("down_mm"), 1)

            def qkv(n, w):
                for i in range(NT):
                    b = i // NB
                    if n == 0 and i == 0:
                        norm_turn(0, 0)
                        norm_turn(0, 1)
                    if n == 1 and i % NB == 0:
                        norm_turn(4, b)
                    claim(eng, qkv_bank(i), "vv", NT * n + i + 1)
                    eng.wait_ge(sem("hT"), 2 * (4 if n else 0) + b + 1)
                    mm(bank(qkv_bank(i))[:, 0:3 * P], hT[:, tile_cols(i)], w).then_inc(sem("qkv_mm"), 1)

            qkv(0, W("wqkv1"))

            def l1_qkT(b):
                eng.wait_ge(sem("rope"), b + 1)
                for j in range(2):
                    claim(eng, 6 + j, "qkT1", 2 * b + j + 1)
                    for wt in range(NB):
                        last = pe.transpose(bank(6 + j)[:, tile_cols(wt)], qk[:, b * NB + wt, j * P:(j + 1) * P], ident)
                    last.then_inc(sem("qkT_mm"), 1)

            def l1_scores(w):
                claim(eng, 2 * (w % 2), "sub1", w + 1)
                claim(eng, 2 * (w % 2) + 1, "sub1", w + 1)
                eng.wait_ge(sem("kb1"), w + 1)
                for j in range(2):
                    last = mm(PP[w % 2][:, j, :], qT1[:, tile_cols(w)],
                              kb1[:, w % 2, 4 * j:4 * j + 4, :].rearrange("p h k -> p (h k)"))
                last.then_inc(sem("s1_mm"), 1)

            def l1_turn(w):
                claim(eng, 4, "pT1", w + 1)
                claim(eng, 5, "pT1", w + 1)
                eng.wait_ge(sem("exp1"), w + 1)
                for h in range(H1):
                    last = pe.transpose(PP[2][:, h // 4, tile_cols(h % 4)], p1[:, w % 2, h, :], ident)
                last.then_inc(sem("p1_tr"), 1)

            def l1_values(w):
                claim(eng, 6, "os1", w + 1)
                eng.wait_ge(sem("pT1"), w + 1)
                eng.wait_ge(sem("vv"), w + 1)
                eng.wait_ge(sem("ones_v"), 2)
                for h in range(H1):
                    g = h % 4
                    last = mm(bank(6)[PAD * g:PAD * g + PAD, tile_cols(h // 4)], v1[:, w, h, :], pT1[:, w % 2, h, :])
                last.then_inc(sem("pv1_mm"), 1)

            def l1_tokens(w):
                claim(eng, 7, "otok1", w + 1)
                eng.wait_ge(sem("os1"), w + 1)
                for j in range(2):
                    last = pe.transpose(bank(7)[:, tile_cols(j)], os1[:, w % 2, j, :], ident)
                last.then_inc(sem("ot1_mm"), 1)

            l1_qkT(0)
            for k in range(NT + 3):
                if k < NT:
                    l1_scores(k)
                if k == 2:
                    l1_qkT(1)
                if 0 <= k - 1 < NT:
                    l1_turn(k - 1)
                if 0 <= k - 2 < NT:
                    l1_values(k - 2)
                if 0 <= k - 3 < NT:
                    l1_tokens(k - 3)

            def out_proj(n, src, w):
                for b in range(B):
                    claim(eng, b, "oT", 2 * n + b + 1)
                    eng.wait_ge(sem("otok1" if n == 0 else "otok3"), NB * (b + 1) if n == 0 else NIT * (b + 1))
                    for wt in range(NB):
                        last = pe.transpose(bank(b)[:, tile_cols(wt)], src(b, wt), ident)
                    last.then_inc(sem("oT_mm"), 1)
                for b in range(B):
                    claim(eng, 2 + b, "xr", 2 * (4 if n else 0) + b + 1)
                    eng.wait_ge(sem("oT"), 2 * n + b + 1)
                    for wt in range(NB):
                        last = mm(bank(2 + b)[:, tile_cols(wt)], oT[:, tile_cols(b * NB + wt)], w(b))
                    last.then_inc(sem("proj_mm"), 1)

            eng.wait_ge(sem("gated_w"), 2)
            out_proj(0, lambda b, wt: otok[:, b * NB + wt, :], lambda b: wout1g[:, b, :])

            mlp_up(0, W("wff1_1"))
            eng.wait_ge(sem("gated_w"), 4)
            mlp_down(0, lambda b, c: wff2g[0][:, b, c, :])

            claim(eng, 0, "bbT", 1)
            eng.wait_ge(sem("bbar"), 1)
            pe.transpose(bank(0)[:, 0:P], bbar[:, :], ident).then_inc(sem("bbar_tr"), 1)
            eng.wait_ge(sem("bbT"), 1)
            claim(eng, 2, "rotin", 1)
            claim(eng, 3, "rotin", 2)
            for b in range(B):
                norm_turn(2, b)
                eng.wait_ge(sem("hT"), 2 * 2 + b + 1)
                for j in range(2):
                    last = mm(bank(2 + j)[64 * b:64 * b + 64, :], bbT[:, 64 * j:64 * j + 64], hT[:, half(b)])
            last.then_inc(sem("u_mm"), 1)
            eng.wait_ge(sem("cg"), 3 * B)
            for b in range(B):
                claim(eng, 6 + b, "xr", 2 * 2 + b + 1)
                for wt in range(NB):
                    mm(bank(6 + b)[:, tile_cols(wt)], hT[:, tile_cols(b * NB + wt)], dg[:, b, :], wt == 0, False)
            eng.wait_ge(sem("rotout"), 2)
            for b in range(B):
                for wt in range(NB):
                    o = bank(6 + b)[:, tile_cols(wt)]
                    mm(o, uw[:, tile_cols(wt)], cga[:, b, :], False, False)
                    last = mm(o, uw2[:, tile_cols(wt)], cgb[:, b, :], False, wt == NB - 1)
                last.then_inc(sem("y_mm"), 1)
            mlp_up(1, W("wff1_2"))
            eng.wait_ge(sem("gated_w"), 6)
            mlp_down(1, lambda b, c: wff2g[1][:, b, c, :])

            qkv(1, W("wqkv3"))
            for b in range(B):
                for j in range(2):
                    n = 2 * b + j
                    claim(eng, n, "res3", n + 1)
                    eng.wait_ge(sem("rope3"), b + 1)
                    for wt in range(NB):
                        last = pe.transpose(bank(n)[:, tile_cols(wt)], qk[:, b * NB + wt, j * P:(j + 1) * P], ident)
                    last.then_inc(sem("qkT3_mm"), 1)
            eng.wait_ge(sem("res3"), 4)
            eng.wait_ge(sem("vv"), 2 * NT)
            eng.wait_ge(sem("hT"), 2 * 4 + 2)

            def l3_score(u, par, hp, j):
                h, w = 2 * hp + j // NB, j % NB
                if not (isinstance(u, int) and u * 8 + j < 2):
                    eng.wait_ge(sem("max3"), u * 8 + (j - 1))
                mm(bank(j % 2), qa[par][0:AUG, h, tile_cols(w)], ka[par][0:AUG, h, :]).then_inc(sem("s3_mm"), 1)

            def l3_pair(u, par, hp, s, t):
                h = 2 * hp + s // 2
                if t == 0 and not (isinstance(u, int) and u * 4 + s < 2):
                    eng.wait_ge(sem("exp3"), u * 4 + (s - 1))
                last = mm(PP[1 + s % 2][:, t, :], ka[par][:, h, tile_cols(2 * (s % 2) + t)], qa[par][:, h, :])
                if t:
                    last.then_inc(sem("st3"), 1)

            def l3_values(u, par, hp, k):
                if k == 0:
                    eng.wait_ge(sem("exp3"), u * 4 + 4)
                    eng.wait_ge(sem("vg"), (u // 2 if isinstance(u, int) else l3_it["values"]) + 1)
                    if not (isinstance(u, int) and u == 0):
                        eng.wait_ge(sem("os3"), u)
                for e in range(2):
                    for h in range(2):
                        strip = PAD * (2 * e + h)
                        last = mm(bank(6)[strip:strip + PAD, hp * 2 * P:(hp + 1) * 2 * P]
                                  .rearrange("p (w q) -> p w q", w=2),
                                  vg[par][:, k, 2 * hp + h, :],
                                  p3[:, hp, h, k, :].rearrange("p (w e q) -> p e w q", e=2, w=2)[:, e, :, :],
                                  k == 0, k == NB - 1)
                if k == NB - 1:
                    last.then_inc(sem("pv3_mm"), 1)

            def l3_turn_max(u):
                eng.wait_ge(sem("ms3"), u + 1)
                pe.transpose(bank(7)[:, 2 * P:2 * P + P // 2].bitcast(BF16), ms3[:, :, :].rearrange("p i n -> p (i n)"),
                             identb[:, :]).then_inc(sem("m3_tr"), 1)

            def l3_tokens(u, hp):
                eng.wait_ge(sem("os3"), u + 1)
                if not (isinstance(u, int) and u >= UNITS - 3):
                    eng.wait_ge(sem("mT3"), u + 4)
                else:
                    eng.wait_ge(sem("otok3"), u)
                for w in range(2):
                    last = pe.transpose(bank(7)[:, tile_cols(w)], os3[:, hp, tile_cols(w)], ident)
                last.then_inc(sem("ot3_mm"), 1)

            def l3_slot(u, par, hp, ready, own=True, ahead=True, turn=True, values=True, tokens=True):
                if own:
                    eng.wait_ge(sem(f"ld_m{par}{hp}"), 16 * ready)
                if ahead:
                    eng.wait_ge(sem(f"ld_q{1 - par}{hp}"), 32 * (ready + par))
                for s in range(4):
                    for t in range(2):
                        if own:
                            l3_pair(u, par, hp, s, t)
                        if ahead:
                            l3_score(u + 2, 1 - par, hp, 2 * s + t)
                    if s == 1 and turn:
                        l3_turn_max(u + 1)
                    if values:
                        l3_values(u - 1, par if hp else 1 - par, 1 - hp, s)
                    if s == 2 and tokens:
                        l3_tokens(u - 2, hp)

            eng.wait_ge(sem("identb"), 1)
            eng.wait_ge(sem("consts"), 4)
            eng.wait_ge(sem("ld_q00"), 32)
            for j in range(8):
                l3_score(0, 0, 0, j)
            eng.wait_ge(sem("ld_q01"), 32)
            for j in range(8):
                if j == 4:
                    l3_turn_max(0)
                l3_score(1, 0, 1, j)
            l3_slot(0, 0, 0, 1, values=False, tokens=False)
            l3_slot(1, 0, 1, 1, tokens=False)
            l3_it = {}
            with eng.Fori(0, NIT // 2 - 1) as pair:
                for j in range(4):
                    u, par = pair * 4 + (2 + j), 1 - j // 2
                    l3_it["values"] = pair * 2 + (1 + j) // 2
                    l3_slot(u, par, j % 2, pair + (1 + j // 2))
            l3_slot(UNITS - 2, 1, 0, NIT // 2, ahead=False)
            l3_slot(UNITS - 1, 1, 1, NIT // 2, ahead=False, turn=False)
            l3_slot(UNITS, 0, 0, 0, own=False, ahead=False, turn=False)
            l3_tokens(UNITS - 1, 1)
            eng.wait_ge(sem("max3"), 8 * UNITS)
            eng.wait_ge(sem("exp3"), 4 * UNITS)
            freed.clear()
            out_proj(1, lambda b, wt: o3[:, wt, b * NG3:(b + 1) * NG3, :].rearrange("p g f -> p (g f)"), lambda b: W("wao"))

            norm_turn(5, 0)
            for b in range(B):
                eng.wait_ge(sem("hT"), 2 * 5 + b + 1)
                for c in range(4):
                    if b == 0 and c == 2:
                        norm_turn(5, 1)
                    k = 4 * b + c
                    claim(eng, 2 * (k % 2), "gT", 16 + k + 1)
                    claim(eng, 2 * (k % 2) + 1, "sg3", k + 1)
                    mm(bank(2 * (k % 2) + 1), W("wfc")[:, tile_cols(4 + c)], hT[:, half(b)]).then_inc(sem("fc_mm"), 1)
                    mm(bank(2 * (k % 2)), W("wfc")[:, tile_cols(c)], hT[:, half(b)]).then_inc(sem("fc_mm"), 1)
            mlp_down(2, lambda b, c: W("wfo")[:, tile_cols(c)])

        @block.scalar
        def _(eng):
            eng.dma_start(xT[:, :], xt_in).then_inc(sem("ld_xT"), 16)
            eng.dma_start(rows_in, rows).then_inc(sem("ld_rows"), 16)
            eng.dma_start(adj[1][:, :], adj_in[1]).then_inc(sem("ld_adj1"), 16)
            eng.dma_start(tiles["w1"][:, :], w1).then_inc(sem("ld_w1"), 16)

            def ident_act(o, i, bias=None, scale=None):
                kw = {}
                if bias is not None:
                    kw["bias"] = bias
                if scale is not None:
                    kw["scale"] = scale
                return act.activation(o, i, ACT.Identity, **kw)

            eng.wait_ge(sem("ld_w0"), 16)
            act.activation(silu_c[:, :], W("cond"), ACT.Silu).then_inc(sem("silu_c"), 1)
            act.activation(col[:, 0:1], W("log_step"), ACT.Exp).then_inc(sem("dt"), 1)
            eng.wait_ge(sem("rho_in"), 1)
            act.activation(col[:, 2:3], col[:, 1:2], ACT.Exp).then_inc(sem("rho"), 1)
            eng.wait_ge(sem("qrow_mm"), 1)
            act.copy(qrow[:, :], bank(5)[0:1, 0:2 * P]).then_inc(sem("qrow"), 1)

            def rows_evac(j):
                lo, hi = 512 * j, min(512 * (j + 1), sum(ROWS.values()))
                eng.wait_ge(sem("rows_mm"), j + 1)
                act.copy(tiles["rw"][:, lo:hi], bank((4, 7, 0, 1)[j])[:, 0:hi - lo]).then_inc(sem("rows"), 1)

            rows_evac(0)
            for b in range(B):
                eng.wait_ge(sem("sf_mm"), b + 1)
                ident_act(sfT[:, half(b)], bank(b), W("bself")).then_inc(sem("sfT"), 1)
            for b in range(B):
                for d in range(2):
                    n = 2 * b + d
                    eng.wait_ge(sem("qh_mm"), n + 1)
                    ident_act(qhT[d][:, half(b)], bank(2 + n), W("bq0")[:, d:d + 1]).then_inc(sem("qhT"), 1)
            for j in range(1, NROWS):
                rows_evac(j)
            eng.wait_ge(sem("ld_adj1"), 16)
            act.copy(adj_w[1][:, :, :].rearrange("p n l -> p (n l)"), adj[1][:, :]).then_inc(sem("adj_f"), 1)
            eng.wait_ge(sem("turns"), 1)
            act.activation(ei[:, :], tA[:, :], ACT.Sin, scale=TWO_PI).then_inc(sem("rot"), 1)
            eng.wait_ge(sem("turns"), 2)
            act.activation(er[:, :], tB[:, :], ACT.Sin, scale=-TWO_PI, bias=W("halfpi")).then_inc(sem("rot"), 1)

            def l0_exp(g):
                eng.wait_ge(sem("sub0"), g + 1)
                act.activation(w0p[:, g % 4, :, :], w0p[:, g % 4, :, :], ACT.Exp).then_inc(sem("exp0"), 1)

            def l0_evac(g):
                b, d, h = g // 4, (g // 2) % 2, g % 2
                dst = w0T[2 * b + d]
                cols = slice(2 * h * P, 2 * h * P + 2 * P)
                pr = PP[2 + g % 2]
                eng.wait_ge(sem("w0_tr"), g + 1)
                act.copy(dst[:, 0:2, cols].rearrange("r c (t q) -> r t c q", t=2),
                         pr[0:RC, :, 0:2 * P].rearrange("r t (c q) -> r t c q", c=2)).then_inc(sem("w0T"), 1)
                act.copy(dst[0:RLAST, 2, cols].rearrange("r (t q) -> r t q", t=2),
                         pr[0:RLAST, :, 2 * P:3 * P]).then_inc(sem("w0T"), 1)

            def x0_evac(b):
                eng.wait_ge(sem("l0_back"), b + 1)
                act.copy(X[:, btiles(b), :].rearrange("p w f -> p (w f)"), bank(1 + 2 * b)).then_inc(sem("x0"), 1)

            for k in range(8 + 2):
                if k == 2:
                    eng.wait_ge(sem("modc"), 1)
                    act.activation(sgt[:, :], modc[:, 11, :], ACT.Silu).then_inc(sem("sgt"), 1)
                if k < 8:
                    l0_exp(k)
                if k >= 2:
                    l0_evac(k - 2)
            for b in range(B):
                x0_evac(b)

            def norm_evac(n, b):
                eng.wait_ge(sem("norm_tr"), 2 * n + b + 1)
                if n == 0:
                    eng.wait_ge(sem("scl"), 1)
                ident_act(hT[:, half(b)], bank(4 + b), shf[:, n, b:b + 1], scl[:, n, b:b + 1]).then_inc(sem("hT"), 1)

            def mlp_act(n, bias):
                for k in range(8):
                    b, c = k // 4, k % 4
                    if k in (0, 2):
                        norm_evac(3 if n else 1, k // 2)
                    eng.wait_ge(sem("up_mm"), 8 * n + k + 1)
                    act.activation(gT[:, c, half(b)], bank(k % 4), ACT.Gelu_apprx_tanh, bias=bias[:, c:c + 1])\
                       .then_inc(sem("gT"), 1)

            def oT_evac(n):
                for b in range(B):
                    eng.wait_ge(sem("oT_mm"), 2 * n + b + 1)
                    act.copy(oT[:, half(b)], bank(b)).then_inc(sem("oT"), 1)

            def l1_qkT(b):
                for j, dst in enumerate((qT1, kT1)):
                    eng.wait_ge(sem("qkT_mm"), 2 * b + j + 1)
                    act.copy(dst[:, half(b)], bank(6 + j)).then_inc(sem("qkT1"), 1)

            for b in range(B):
                norm_evac(0, b)
            l1_qkT(0)
            for k in range(NT + 2):
                if k == 2:
                    l1_qkT(1)
                w = k - 1
                if 0 <= w < NT:
                    eng.wait_ge(sem("p1_tr"), w + 1)
                    if w >= 2:
                        eng.wait_ge(sem("pv1_mm"), w - 1)
                    act.copy(pT1[:, w % 2, :, :].rearrange("p h q -> p (h q)"),
                             PP[2][:, :, :].rearrange("p a q -> p (a q)")).then_inc(sem("pT1"), 1)
                w = k
                if w < NT:
                    eng.wait_ge(sem("sub1"), w + 1)
                    act.activation(p1[:, w % 2, :, :], p1[:, w % 2, :, :], ACT.Exp, scale=float(D1) ** -0.5)\
                       .then_inc(sem("exp1"), 1)
                w = k - 2
                if 0 <= w < NT:
                    eng.wait_ge(sem("pv1_mm"), w + 1)
                    if w >= 2:
                        eng.wait_ge(sem("ot1_mm"), w - 1)
                    act.copy(os1[:, w % 2, :, :].rearrange("p a q -> p (a q)"), bank(6)[:, 0:2 * P])\
                       .then_inc(sem("os1"), 1)
            oT_evac(0)
            mlp_act(0, W("bff1_1"))

            eng.wait_ge(sem("bbar_tr"), 1)
            act.copy(bbT[:, :], bank(0)[:, 0:P]).then_inc(sem("bbT"), 1)
            for b in range(B):
                norm_evac(2, b)
            mlp_act(1, W("bff1_2"))

            for b in range(B):
                norm_evac(4, b)
            for n in range(2 * B):
                eng.wait_ge(sem("qkT3_mm"), n + 1)
                act.copy(split[:, n, 0, :], bank(n)).then_inc(sem("split1"), 1)
                eng.wait_ge(sem("res3"), n + 1)
                act.copy(split[:, n, 1, :], res3[:, n, :]).then_inc(sem("split2"), 1)

            def l3_exp(u, hp, s):
                eng.wait_ge(sem("st3"), u * 4 + s + 1)
                if s == 0 and not (isinstance(u, int) and u < 2):
                    eng.wait_ge(sem("pv3_mm"), u - 1)
                act.activation(p3[:, hp, s // 2, 2 * (s % 2):2 * (s % 2) + 2, :], PP[1 + s % 2][:, :, :], ACT.Exp,
                               scale=float(D3) ** -0.5).then_inc(sem("exp3"), 1)

            def l3_mT(u, hp):
                eng.wait_ge(sem("m3_tr"), u + 1)
                act.copy(mT3[:, hp, :], bank(7)[0:3 * 2 * NB, 2 * P:2 * P + P // 2].bitcast(BF16))\
                    .then_inc(sem("mT3"), 1)

            def l3_out(u, hp):
                eng.wait_ge(sem("pv3_mm"), u + 1)
                if isinstance(u, int) and u >= 2:
                    eng.wait_ge(sem("ot3_mm"), u - 1)
                act.copy(os3[:, hp, :], bank(6)[:, hp * 2 * P:(hp + 1) * 2 * P]).then_inc(sem("os3"), 1)

            def l3_slot(u, hp, turn=True, values=True):
                for s in range(4):
                    l3_exp(u, hp, s)
                    if s == 1 and turn:
                        l3_mT(u + 1, 1 - hp)
                if values:
                    l3_out(u - 1, 1 - hp)

            l3_mT(0, 0)
            l3_slot(0, 0, values=False)
            l3_slot(1, 1)
            with eng.Fori(1, NIT - 1) as it:
                l3_slot(it * 2, 0)
                l3_slot(it * 2 + 1, 1)
            l3_slot(UNITS - 2, 0)
            l3_slot(UNITS - 1, 1, turn=False)
            l3_out(UNITS - 1, 1)
            oT_evac(1)
            for k in range(8):
                c = k % 4
                if k in (0, 2):
                    norm_evac(5, k // 2)
                eng.wait_ge(sem("fc_mm"), 2 * k + 1)
                if k >= 2:
                    eng.wait_ge(sem("gT"), 16 + k - 1)
                act.activation(sg3[:, k % 2, :], bank(2 * (k % 2) + 1), ACT.Silu, bias=W("bfc")[:, 4 + c:5 + c])\
                   .then_inc(sem("sg3"), 1)

        @block.gpsimd
        def _(eng):
            def tt(o, a, b, op):
                return pool.tensor_tensor(o, a, b, op)

            pool.memset(ones[:, :], 1.0).then_inc(sem("consts"), 1)
            pool.memset(mhalf[:, :], -0.5).then_inc(sem("consts"), 1)
            pool.memset(zeros[:, :], 0.0).then_inc(sem("consts"), 1)
            pool.memset(ms3[:, 3:, :], 0.0).then_inc(sem("consts"), 1)
            eng.wait_ge(sem("ld_w0"), 16)
            tt(steps[:, :].rearrange("p (a c) -> p a c", c=16), W("steps_hi").unsqueeze(2).to_broadcast([P, T // 16, 16]),
               W("steps_lo").unsqueeze(1).to_broadcast([P, T // 16, 16]), ALU.add).then_inc(sem("steps"), 1)
            pool.tensor_copy(bc_cond[:, :, :], W("cond").unsqueeze(2).to_broadcast([P, B, P])).then_inc(sem("bcast"), 1)
            eng.wait_ge(sem("silu_c"), 1)
            pool.tensor_copy(bc_silu[:, :, :], silu_c[:, :].unsqueeze(2).to_broadcast([P, B, P])).then_inc(sem("bcast"), 1)
            for b in range(B):
                eng.wait_ge(sem("sfT"), b + 1)
                pool.tensor_copy(kvrep[b][:, :, :],
                                 sfT[:, b * T:b * T + M0].unsqueeze(1).to_broadcast([P, NC0 * HC, M0]))\
                    .then_inc(sem("kvrep"), 1)

            eng.wait_ge(sem("adj_f"), 1)
            tt(adj_w[1][:, :, :], adj_w[1][:, :, :], W("wbias0").unsqueeze(1).to_broadcast([P, NT * M0, L]), ALU.mult)\
                .then_inc(sem("mprod1"), 1)

            def l0_tiles(src, g):
                b, d, h = g // 4, (g // 2) % 2, g % 2
                i = b * NB + 2 * h
                return src[:, d, i * M0:(i + 2) * M0].rearrange("p (t m) -> p t m", t=2).unsqueeze(2)\
                    .to_broadcast([P, 2, H0, M0])

            def l0_view(g):
                return w0p[:, g % 4, :, :].rearrange("p t (h m) -> p t h m", m=M0)

            def l0_bias(g):
                eng.wait_ge(sem("s0_m"), g + 1)
                eng.wait_ge(sem("mtb"), (g // 2) % 2 + 1)
                tt(l0_view(g), l0_view(g), l0_tiles(mtb, g), ALU.add).then_inc(sem("add0"), 1)

            def l0_norm(g):
                eng.wait_ge(sem("rs0"), g + 1)
                v = w0p[:, g % 4, :, :].rearrange("p t (h m) -> p (t h) m", m=M0)
                tt(v, v, rs0[:, g % 4, :].unsqueeze(2).to_broadcast([P, 2 * H0, M0]), ALU.mult)\
                    .then_inc(sem("w0n"), 1)

            for k in range(8 + 2):
                if k < 8:
                    l0_bias(k)
                if k >= 2:
                    l0_norm(k - 2)

            pool.memset(v1[:, :, :, D1:PAD], 0.0).then_inc(sem("ones_v"), 1)
            eng.wait_ge(sem("ones_v"), 1)
            pool.memset(v1[:, :, :, D1:D1 + 1], 1.0).then_inc(sem("ones_v"), 1)

            eng.wait_ge(sem("ld_w1"), 16)
            eng.wait_ge(sem("ld_w2"), 16)
            eng.wait_ge(sem("rows"), NROWS)
            eng.wait_ge(sem("gate"), B)

            def gcols(b, j, n=None):
                g = gate[:, b, j * P:(j + 1) * P]
                return g if n is None else g.unsqueeze(1).to_broadcast([P, n, P])

            for b in range(B):
                tt(wout1g[:, b, :], W("wout1"), gcols(b, 0), ALU.mult).then_inc(sem("gated_w"), 1)
            for b in range(B):
                tt(bres[:, 0, b, :], W("rout1"), gcols(b, 0), ALU.mult).then_inc(sem("gated_b"), 1)

            def residual(n, bias):
                use = {0: 0, 1: 1, 2: 3, 3: 4, 4: 5}[n]
                for b in range(B):
                    if use == 0:
                        eng.wait_ge(sem("x0"), b + 1)
                    else:
                        eng.wait_ge(sem("xr"), 2 * (use - 1) + b + 1)
                    tt(Xb[:, btiles(b), :], X[:, btiles(b), :], bias(b).unsqueeze(1).to_broadcast([P, NB, P]), ALU.add)\
                        .then_inc(sem("xb"), 1)

            def norm_pow(n):
                for b in range(B):
                    eng.wait_ge(sem("var"), 2 * n + b + 1)
                    if n == 0 and b == 0:
                        eng.wait_ge(sem("consts"), 2)
                    tt(rstd[:, btiles(b)], var[:, btiles(b)], mhalf[:, btiles(b)], ALU.pow).then_inc(sem("rstd"), 1)

            norm_pow(0)
            eng.wait_ge(sem("gated_b"), 2)
            residual(0, lambda b: bres[:, 0, b, :])
            for w in range(NT):
                eng.wait_ge(sem("qkT1"), 2 * (w // NB + 1))
                if w >= 2:
                    eng.wait_ge(sem("s1_mm"), w - 1)
                tt(kb1[:, w % 2, :, :], kT1[:, tile_cols(w)].unsqueeze(1).to_broadcast([P, H1, P]),
                   W("kmask1").unsqueeze(2).to_broadcast([P, H1, P]), ALU.mult).then_inc(sem("kb1"), 1)
            for b in range(B):
                tt(wff2g[0][:, b, :, :], W("wff2_1").rearrange("p (c f) -> p c f", c=4), gcols(b, 1, 4), ALU.mult)\
                    .then_inc(sem("gated_w"), 1)
            for b in range(B):
                tt(bres[:, 1, b, :], W("rff2_1"), gcols(b, 1), ALU.mult).then_inc(sem("gated_b"), 1)
            norm_pow(1)
            eng.wait_ge(sem("gated_b"), 4)
            residual(1, lambda b: bres[:, 1, b, :])
            for b in range(B):
                tt(wff2g[1][:, b, :, :], W("wff2_2").rearrange("p (c f) -> p c f", c=4), gcols(b, 3, 4), ALU.mult)\
                    .then_inc(sem("gated_w"), 1)
            for b in range(B):
                tt(bres[:, 2, b, :], W("rff2_2"), gcols(b, 3), ALU.mult).then_inc(sem("gated_b"), 1)
            pool.memset(v3[:, :, :, :, D3:PAD], 0.0).then_inc(sem("ones_v"), 1)
            eng.wait_ge(sem("ones_v"), 3)
            pool.memset(v3[:, :, :, :, D3:D3 + 1], 1.0).then_inc(sem("ones_v"), 1)
            eng.wait_ge(sem("ld_w3"), 16)
            for name, wide in (("cos3", cos3), ("sin3", sin3)):
                pool.tensor_copy(wide[:, :, :, :], W(name).rearrange("p (w c) -> p w c", w=NB).unsqueeze(2)
                                 .to_broadcast([P, NB, 2 * NG3, D3])).then_inc(sem("wide3"), 1)
            norm_pow(2)
            norm_pow(3)
            eng.wait_ge(sem("gated_b"), 6)
            residual(2, lambda b: bres[:, 2, b, :])
            eng.wait_ge(sem("xb"), 6)
            for j in range(2):
                pool.memset(qa[j][64:P, :, :], 0.0).then_inc(sem("zero3"), 1)
                pool.memset(ka[j][64:P, :, :], 0.0).then_inc(sem("zero3a"), 1)
            eng.wait_ge(sem("zero3a"), 2)
            for j in range(2):
                pool.memset(ka[j][AUG:AUG + 3, :, :], 1.0).then_inc(sem("zero3"), 1)
            eng.wait_ge(sem("zero3"), 4)
            pool.tensor_copy(identb[:, :], ident).then_inc(sem("identb"), 1)
            norm_pow(4)
            residual(3, lambda b: W("rao"))

            for n in range(2 * B):
                eng.wait_ge(sem("split2"), n + 1)
                tt(split[:, n, 2, :], res3[:, n, :], split[:, n, 1, :], ALU.subtract).then_inc(sem("split3"), 1)

            def values(it, par):
                if not (isinstance(it, int) and it < 2):
                    eng.wait_ge(sem("pv3_mm"), it * 2 - 2)
                pool.tensor_copy(vg[par][:, :, :, :].rearrange("p w h c -> p (w h c)"),
                                 v3[:, :, :, :, :].rearrange("p i w h c -> p (i w h c)")[:, bass.ds(it * 512, 512)])\
                    .then_inc(sem("vg"), 1)

            def l3_split_max(u, hp):
                eng.wait_ge(sem("max3"), u * 8 + 8)
                if not (isinstance(u, int) and u == 0):
                    eng.wait_ge(sem("m3_tr"), u)
                tt(ms3[:, 0, :], nm3[:, hp, :], zeros[:, :], ALU.add).then_inc(sem("ms3_t"), 1)
                eng.wait_ge(sem("ms3_t"), u * 3 + 1)
                tt(nr3[:, :], nm3[:, hp, :], ms3[:, 0, :], ALU.subtract).then_inc(sem("ms3_t"), 1)
                eng.wait_ge(sem("ms3_t"), u * 3 + 2)
                tt(ms3[:, 1, :], nr3[:, :], zeros[:, :], ALU.add).then_inc(sem("ms3_t"), 1)
                eng.wait_ge(sem("ms3_t"), u * 3 + 3)
                tt(ms3[:, 2, :], nr3[:, :], ms3[:, 1, :], ALU.subtract).then_inc(sem("ms3"), 1)

            eng.wait_ge(sem("vv"), 2 * NT)
            eng.wait_ge(sem("ones_v"), 4)
            values(0, 0)
            values(1, 1)
            eng.wait_ge(sem("consts"), 3)
            for u in range(4):
                l3_split_max(u, u % 2)
            with eng.Fori(1, NIT // 2) as pair:
                for j in range(2):
                    l3_split_max(pair * 4 + 2 * j, 0)
                    values(pair * 2 + j, j)
                    l3_split_max(pair * 4 + (2 * j + 1), 1)
            norm_pow(5)
            residual(4, lambda b: W("rfo"))

        @block.vector
        def _(eng):
            def tt(o, a, b, op):
                return dve.tensor_tensor(o, a, b, op)

            ssm_done = [0]

            def did(ins):
                ssm_done[0] += 1
                ins.then_inc(sem("ssm_step"), 1)
                eng.wait_ge(sem("ssm_step"), ssm_done[0])

            def c(j):
                return col[:, j:j + 1]

            def ts(o, i, s1, s2, op0, op1=None):
                return dve.tensor_scalar(o, i, s1, s2, op0) if op1 is None else dve.tensor_scalar(o, i, s1, s2, op0, op1)

            def stt(o, i, s, j, op0, op1):
                return dve.scalar_tensor_tensor(out=o, in0=i, scalar=s, in1=j, op0=op0, op1=op1)

            def ssm_angles():
                eng.wait_ge(sem("ld_w0"), 16)
                eng.wait_ge(sem("dt"), 1)
                tt(c(1), W("lam_re"), c(0), ALU.mult).then_inc(sem("rho_in"), 1)
                did(tt(c(3), W("lam_im"), c(0), ALU.mult))
                did(ts(c(4), c(3), 1.0 / TWO_PI, ROUND, ALU.mult, ALU.add))
                did(ts(c(4), c(4), -ROUND, None, ALU.add))
                did(stt(c(5), c(4), -TURN[0], c(3), ALU.mult, ALU.add))
                did(stt(c(5), c(4), -TURN[1], c(5), ALU.mult, ALU.add))
                did(stt(c(5), c(4), -TURN[2], c(5), ALU.mult, ALU.add))
                did(ts(c(6), c(5), 1.0 / TWO_PI, None, ALU.mult))
                did(ts(c(7), c(6), ROUND12, ROUND12, ALU.add, ALU.subtract))
                did(tt(c(8), c(6), c(7), ALU.subtract))
                t = steps[:, :]
                eng.wait_ge(sem("steps"), 1)
                did(ts(tA[:, :], t, c(7), None, ALU.mult))
                did(ts(tB[:, :], tA[:, :], ROUND, ROUND, ALU.add, ALU.subtract))
                did(tt(tA[:, :], tA[:, :], tB[:, :], ALU.subtract))
                did(stt(tA[:, :], t, c(8), tA[:, :], ALU.mult, ALU.add))
                did(ts(tB[:, :], tA[:, :], ROUND, ROUND, ALU.add, ALU.subtract))
                did(tt(tA[:, :], tA[:, :], tB[:, :], ALU.subtract))
                ts(tA[:, :], tA[:, :], 0.4999999, -0.4999999, ALU.min, ALU.max).then_inc(sem("turns"), 1)
                eng.wait_ge(sem("turns"), 1)
                stt(tB[:, :], tA[:, :], -1.0, tA[:, :], ALU.mult, ALU.max).then_inc(sem("turns"), 1)

            def ssm_inputs():
                eng.wait_ge(sem("ld_w2"), 16)
                lre, lim = W("lam_re"), W("lam_im")
                eng.wait_ge(sem("rho"), 1)
                eng.wait_ge(sem("rot"), 2)
                did(ts(c(9), er[:, 1:2], c(2), -1.0, ALU.mult, ALU.add))
                did(tt(c(10), ei[:, 1:2], c(2), ALU.mult))
                did(tt(c(11), lre, lre, ALU.mult))
                did(stt(c(12), lim, lim, c(11), ALU.mult, ALU.add))
                did(dve.reciprocal(c(13), c(12)))
                did(tt(c(14), c(9), lre, ALU.mult))
                did(stt(c(15), c(10), lim, c(14), ALU.mult, ALU.add))
                did(tt(c(16), c(15), c(13), ALU.mult))
                did(tt(c(17), c(9), lim, ALU.mult))
                did(stt(c(18), c(10), lre, c(17), ALU.mult, ALU.subtract))
                did(tt(c(19), c(18), c(13), ALU.mult))
                did(tt(c(20), c(16), W("sa"), ALU.mult))
                did(tt(c(21), c(19), W("sb"), ALU.mult))
                did(ts(bbar[:, :], W("bx"), c(20), None, ALU.mult))
                stt(bbar[:, :], W("by"), c(21), bbar[:, :], ALU.mult, ALU.add).then_inc(sem("bbar"), 1)
                for b in range(B):
                    g = gate[:, b, 2 * P:3 * P]
                    stt(cga[:, b, :], W("cta"), W("sign1")[:, b:b + 1], g, ALU.mult, ALU.mult).then_inc(sem("cg"), 1)
                    stt(cgb[:, b, :], W("ctb"), W("sign2")[:, b:b + 1], g, ALU.mult, ALU.mult).then_inc(sem("cg"), 1)
                    stt(dg[:, b, :], ident, W("dcol"), g, ALU.mult, ALU.mult).then_inc(sem("cg"), 1)

            def l0_blocks():
                tt(bout_sum[:, :], W("bout0")[:, 0:1], W("bout0")[:, 1:2], ALU.add).then_inc(sem("bout_sum"), 1)
                eng.wait_ge(sem("kh_mm"), 4)
                for n in range(4):
                    d = n % 2
                    dve.scalar_tensor_tensor(
                        out=kblk[n][:, :, :], in0=bank(6)[:, 32 * n:32 * n + M0].unsqueeze(1).to_broadcast([P, H0, M0]),
                        scalar=W("bk0")[:, d:d + 1], in1=W("kmask0").unsqueeze(2).to_broadcast([P, H0, M0]),
                        op0=ALU.add, op1=ALU.mult).then_inc(sem("kblk"), 1)

            for b in range(B):
                eng.wait_ge(sem("rowsum"), b + 1)
                dve.tensor_scalar(keep[:, half(b)], bank(6 + b)[0:1, :], 0.0, None, ALU.not_equal)\
                   .then_inc(sem("keep"), 1)
            ssm_angles()
            for d in range(2):
                a = adj[d][:, :].rearrange("p (n l) -> p n l", l=L)
                eng.wait_ge(sem(f"ld_adj{d}"), 16)
                dve.tensor_reduce(msum[:, d, :], a, X_AXIS, ALU.add).then_inc(sem("msum"), 1)
                eng.wait_ge(sem("msum"), d + 1)
                dve.tensor_scalar(mask[:, d, :], msum[:, d, :], 0.0, None, ALU.is_gt).then_inc(sem("mask"), 1)
                eng.wait_ge(sem("mask"), d + 1)
                dve.tensor_scalar(mpen[:, d, :], mask[:, d, :], -1.0, -NEG, ALU.add, ALU.mult).then_inc(sem("mpen"), 1)
            for d in range(2):
                if d == 0:
                    eng.wait_ge(sem("rows"), 1)
                    tt(adj_w[0][:, :, :], adj[0][:, :].rearrange("p (n l) -> p n l", l=L),
                       W("wbias0").unsqueeze(1).to_broadcast([P, NT * M0, L]), ALU.mult).then_inc(sem("mprod0"), 1)
                eng.wait_ge(sem(f"mprod{d}"), 1)
                dve.tensor_reduce(mbias[:, d, :], adj_w[d][:, :, :], X_AXIS, ALU.add).then_inc(sem("mbias"), 1)
                eng.wait_ge(sem("mbias"), d + 1)
                eng.wait_ge(sem("mpen"), d + 1)
                dve.scalar_tensor_tensor(out=mtb[:, d, :], in0=mbias[:, d, :], scalar=W("bbias0"), in1=mpen[:, d, :],
                                         op0=ALU.add, op1=ALU.add).then_inc(sem("mtb"), 1)
                if d == 0:
                    l0_blocks()
            def l0_value_blocks():
                for n in range(4):
                    eng.wait_ge(sem("vf_mm"), n + 1)
                    tt(vblk[n][:, :, :].rearrange("r c (h e) -> r (c h) e", h=H0),
                       bank(4 + n)[0:RC, 0:NC0 * P].rearrange("r (k e) -> r k e", e=P // H0),
                       W("vmask0")[0:RC, :].unsqueeze(2).to_broadcast([RC, NC0 * H0, P // H0]), ALU.mult)\
                        .then_inc(sem("vblk"), 1)

            def l0_tiles(src, g):
                b, d, h = g // 4, (g // 2) % 2, g % 2
                i = b * NB + 2 * h
                return src[:, d, i * M0:(i + 2) * M0].rearrange("p (t m) -> p t m", t=2).unsqueeze(2)\
                    .to_broadcast([P, 2, H0, M0])

            def flat(g):
                return w0p[:, g % 4, :, :].rearrange("p t (h m) -> p (t h) m", m=M0)

            def l0_mask(g):
                eng.wait_ge(sem("s0_mm"), g + 1)
                if g >= 4:
                    eng.wait_ge(sem("w0_tr"), g - 3)
                tt(w0p[:, g % 4, :, :].rearrange("p t (h m) -> p t h m", m=M0),
                   PP[g % 2][:, :, 0:H0 * M0].rearrange("p t (h m) -> p t h m", m=M0),
                   l0_tiles(mask, g), ALU.mult).then_inc(sem("s0_m"), 1)

            def l0_max(g):
                eng.wait_ge(sem("add0"), g + 1)
                dve.tensor_reduce(mx0[:, g % 4, :], flat(g), X_AXIS, ALU.max).then_inc(sem("mx0"), 1)
                eng.wait_ge(sem("mx0"), g + 1)
                tt(flat(g), flat(g), mx0[:, g % 4, :].unsqueeze(2).to_broadcast([P, 2 * H0, M0]), ALU.subtract)\
                    .then_inc(sem("sub0"), 1)

            def l0_sum(g):
                eng.wait_ge(sem("exp0"), g + 1)
                dve.tensor_reduce(sm0[:, g % 4, :], flat(g), X_AXIS, ALU.add).then_inc(sem("sm0"), 1)
                eng.wait_ge(sem("sm0"), g + 1)
                dve.reciprocal(rs0[:, g % 4, :], sm0[:, g % 4, :]).then_inc(sem("rs0"), 1)

            def l0_final(b):
                k = 2 * b
                eng.wait_ge(sem("o0_mm"), b + 1)
                eng.wait_ge(sem("bout_sum"), 1)
                dve.scalar_tensor_tensor(out=l0sum[:, b, :], in0=bank(k), scalar=bout_sum[:, :], in1=sfT[:, half(b)],
                                         op0=ALU.add, op1=ALU.add).then_inc(sem("l0sum"), 1)
                eng.wait_ge(sem("l0sum"), b + 1)
                dve.scalar_tensor_tensor(out=xoT[:, half(b)], in0=l0sum[:, b, :], scalar=0.0, in1=xT[:, half(b)],
                                         op0=ALU.max, op1=ALU.add).then_inc(sem("l0x"), 1)

            mod_done = [0]

            def mod_did(ins):
                mod_done[0] += 1
                ins.then_inc(sem("mod_step"), 1)
                eng.wait_ge(sem("mod_step"), mod_done[0])

            def modulation():
                eng.wait_ge(sem("mod_mm"), 1)
                eng.wait_ge(sem("rows"), NROWS)
                tt(modc[:, :, :], bank(4)[:, 0:24].rearrange("p (j b) -> p j b", b=B),
                   W("bmod").unsqueeze(2).to_broadcast([P, 12, B]), ALU.add).then_inc(sem("modc"), 1)
                eng.wait_ge(sem("sgt"), 1)
                eng.wait_ge(sem("modc"), 1)
                tt(tpe[:, :], modc[:, 10, :], sgt[:, :], ALU.mult).then_inc(sem("tpe"), 1)
                for b in range(B):
                    eng.wait_ge(sem("gate_mm"), b + 1)
                    tt(gate[:, b, :], bank(5 + b), W("rgate"), ALU.add).then_inc(sem("gate"), 1)
                eng.wait_ge(sem("modd_mm"), 1)
                tt(modd[:, :, :], bank(7)[:, 0:8].rearrange("p (j b) -> p j b", b=B),
                   W("bmodd").unsqueeze(2).to_broadcast([P, 4, B]), ALU.add).then_inc(sem("modd"), 1)

            def norm_factors():
                eng.wait_ge(sem("modd"), 1)
                mod_did(dve.tensor_scalar(modp[:, :, :], modc[:, :, :], 1.0, None, ALU.add))
                mod_did(dve.tensor_scalar(modq[:, :, :], modd[:, :, :], 1.0, None, ALU.add))
                mod_did(dve.tensor_scalar(scl[:, 0, :], modp[:, 1, :], W("s1a"), None, ALU.mult))
                mod_did(dve.tensor_scalar(scl[:, 1, :], modp[:, 3, :], W("s1b"), None, ALU.mult))
                mod_did(dve.tensor_copy(scl[:, 2, :], modp[:, 5, :]))
                mod_did(tt(scl[:, 3, :], modp[:, 8, :], modp[:, 7, :], ALU.mult))
                mod_did(dve.tensor_scalar(scl[:, 4, :], modq[:, 1, :], W("g3a"), None, ALU.mult))
                mod_did(dve.tensor_scalar(scl[:, 5, :], modq[:, 3, :], W("g3b"), None, ALU.mult))
                mod_did(dve.tensor_copy(shf[:, 0, :], modc[:, 0, :]))
                mod_did(dve.tensor_copy(shf[:, 1, :], modc[:, 2, :]))
                mod_did(dve.tensor_copy(shf[:, 2, :], modc[:, 4, :]))
                mod_did(tt(shtmp[:, :], modc[:, 9, :], modp[:, 7, :], ALU.mult))
                mod_did(tt(shf[:, 3, :], shtmp[:, :], modc[:, 6, :], ALU.add))
                mod_did(dve.tensor_copy(shf[:, 4, :], modd[:, 0, :]))
                dve.tensor_copy(shf[:, 5, :], modd[:, 2, :]).then_inc(sem("scl"), 1)

            for k in range(8 + 2):
                if k < 8:
                    l0_mask(k)
                if k == 3:
                    modulation()
                    l0_value_blocks()
                if 1 <= k <= 8:
                    l0_max(k - 1)
                if k >= 2:
                    l0_sum(k - 2)
            l0_final(0)
            norm_factors()
            l0_final(1)

            def norm_stats(n, b, centred):
                if n == 0:
                    eng.wait_ge(sem("x0"), b + 1)
                else:
                    eng.wait_ge(sem("xr"), 2 * (n - 1) + b + 1)
                for w in range(NB):
                    i = b * NB + w
                    dve.bn_stats(st[:, i, :], X[:, i, :]).then_inc(sem("stats"), 1)
                eng.wait_ge(sem("stats"), NT * n + NB * (b + 1))
                for w in range(NB):
                    i = b * NB + w
                    dve.bn_aggr(mv[:, i, :], st[:, i, :]).then_inc(sem("aggr"), 1)
                eng.wait_ge(sem("aggr"), NT * n + NB * (b + 1))
                bt = btiles(b)
                eps = 1e-5 if n < 4 else 1.1920928955078125e-07
                if centred:
                    dve.tensor_scalar(var[:, bt], mv[:, bt, 1], eps, None, ALU.add).then_inc(sem("var"), 1)
                else:
                    tt(msq[:, bt], mv[:, bt, 0], mv[:, bt, 0], ALU.mult).then_inc(sem("msq"), 1)
                    eng.wait_ge(sem("msq"), 2 * {0: 0, 1: 1, 4: 2, 5: 3}[n] + b + 1)
                    dve.scalar_tensor_tensor(out=var[:, bt], in0=msq[:, bt], scalar=eps, in1=mv[:, bt, 1],
                                             op0=ALU.add, op1=ALU.add).then_inc(sem("var"), 1)

            def norm_apply(n, b, centred):
                eng.wait_ge(sem("rstd"), 2 * n + b + 1)
                if n:
                    eng.wait_ge(sem("norm_tr"), 2 * (n - 1) + b + 1)
                for w in range(NB):
                    i = b * NB + w
                    if centred:
                        ins = dve.tensor_scalar(xn[:, i, :], X[:, i, :], mv[:, i, 0:1], rstd[:, i:i + 1],
                                                ALU.subtract, ALU.mult)
                    else:
                        ins = dve.tensor_scalar(xn[:, i, :], X[:, i, :], rstd[:, i:i + 1], None, ALU.mult)
                    ins.then_inc(sem("xn"), 1)

            def add_residual(u, done, src, b):
                base = X if u == 2 else Xb
                eng.wait_ge(sem(done[0]), done[1] + b + 1)
                if u != 2:
                    eng.wait_ge(sem("xb"), 2 * {0: 0, 1: 1, 3: 2, 4: 3, 5: 4}[u] + b + 1)
                else:
                    eng.wait_ge(sem("xn"), NT * 3)
                tt(X[:, btiles(b), :].rearrange("p w f -> p (w f)"), bank(src + b),
                   base[:, btiles(b), :].rearrange("p w f -> p (w f)"), ALU.add).then_inc(sem("xr"), 1)

            def residual_norm(u, done, src, centred):
                add_residual(u, done, src, 0)
                norm_stats(u + 1, 0, centred)
                add_residual(u, done, src, 1)
                norm_apply(u + 1, 0, centred)
                norm_stats(u + 1, 1, centred)
                norm_apply(u + 1, 1, centred)

            norm_stats(0, 0, False)
            norm_stats(0, 1, False)
            norm_apply(0, 0, False)
            norm_apply(0, 1, False)

            def l1_qkv(b):
                for i in range(b * NB, (b + 1) * NB):
                    eng.wait_ge(sem("qkv_mm"), i + 1)
                    tt(qk[:, i, :], bank(qkv_bank(i))[:, 0:2 * P], W("rqkv1")[:, 0:2 * P], ALU.add).then_inc(sem("qk"), 1)
                    tt(v1[:, i, :, 0:D1], bank(qkv_bank(i))[:, 2 * P:3 * P].rearrange("p (h c) -> p h c", h=H1),
                       W("rqkv1")[:, 2 * P:3 * P].rearrange("p (h c) -> p h c", h=H1), ALU.add).then_inc(sem("vv"), 1)

            def l1_rope(b):
                eng.wait_ge(sem("qk"), NB * (b + 1))
                v = qk[:, btiles(b), :].rearrange("p w (h c) -> p (w h) c", c=D1)
                r1 = rt1[:, btiles(b), :].rearrange("p w (h c) -> p (w h) c", c=D1)
                r2 = rt2[:, btiles(b), :].rearrange("p w (h c) -> p (w h) c", c=D1)
                n, hd = NB * 2 * H1, D1 // 2
                tt(r1, v, W("cos1").unsqueeze(1).to_broadcast([P, n, D1]), ALU.mult).then_inc(sem("rope_t"), 1)
                tt(r2[:, :, 0:hd], v[:, :, hd:D1], W("sin1")[:, 0:hd].unsqueeze(1).to_broadcast([P, n, hd]), ALU.mult)\
                    .then_inc(sem("rope_t"), 1)
                tt(r2[:, :, hd:D1], v[:, :, 0:hd], W("sin1")[:, hd:D1].unsqueeze(1).to_broadcast([P, n, hd]), ALU.mult)\
                    .then_inc(sem("rope_t"), 1)
                eng.wait_ge(sem("rope_t"), 3 * (b + 1))
                tt(v, r1, r2, ALU.add).then_inc(sem("rope"), 1)

            for b in range(B):
                l1_qkv(b)
                l1_rope(b)
            for k in range(NT + 3):
                w = k
                if w < NT:
                    eng.wait_ge(sem("s1_mm"), w + 1)
                    s = PP[w % 2][:, :, :].rearrange("p a (h k) -> p (a h) k", k=P)
                    dve.tensor_reduce(mx1[:, w % 2, :], s, X_AXIS, ALU.max).then_inc(sem("mx1"), 1)
                    eng.wait_ge(sem("mx1"), w + 1)
                    if w >= 2:
                        eng.wait_ge(sem("p1_tr"), w - 1)
                    tt(p1[:, w % 2, :, :], s, mx1[:, w % 2, :].unsqueeze(2).to_broadcast([P, H1, P]), ALU.subtract)\
                        .then_inc(sem("sub1"), 1)
                w = k - 3
                if 0 <= w < NT:
                    eng.wait_ge(sem("ot1_mm"), w + 1)
                    o = bank(7)[:, 0:2 * P].rearrange("p (h c) -> p h c", c=PAD)
                    dve.reciprocal(rc1[:, w % 2, :], o[:, :, D1]).then_inc(sem("rc1"), 1)
                    eng.wait_ge(sem("rc1"), w + 1)
                    tt(otok[:, w, :].rearrange("p (h c) -> p h c", c=D1), o[:, :, 0:D1],
                       rc1[:, w % 2, :].unsqueeze(2).to_broadcast([P, H1, D1]), ALU.mult).then_inc(sem("otok1"), 1)
            residual_norm(0, ("proj_mm", 0), 2, False)
            ssm_inputs()

            residual_norm(1, ("down_mm", 0), 6, True)
            eng.wait_ge(sem("u_mm"), 1)
            eng.wait_ge(sem("rot"), 2)
            tt(ua[:, :], bank(2), er[:, :], ALU.mult).then_inc(sem("rotin"), 1)
            tt(ub[:, :], bank(3), ei[:, :], ALU.mult).then_inc(sem("rotin"), 1)
            eng.wait_ge(sem("rotin"), 2)
            tt(uw[:, :], ua[:, :], ub[:, :], ALU.add).then_inc(sem("scan_in"), 1)
            eng.wait_ge(sem("scan_in"), 1)
            eng.wait_ge(sem("rho"), 1)
            dve.tensor_tensor_scan(xs[:, :], col[:, 2:3].to_broadcast([P, T]), uw[:, :], 0.0, ALU.mult, ALU.add)\
               .then_inc(sem("scan"), 1)
            eng.wait_ge(sem("scan"), 1)
            tt(uw[:, :], xs[:, :], er[:, :], ALU.mult).then_inc(sem("rotout"), 1)
            tt(uw2[:, :], xs[:, :], ei[:, :], ALU.mult).then_inc(sem("rotout"), 1)
            residual_norm(2, ("y_mm", 0), 6, True)

            residual_norm(3, ("down_mm", 2), 6, False)

            def l3_qkv(b):
                for w in range(NB):
                    i = b * NB + w
                    eng.wait_ge(sem("qkv_mm"), NT + i + 1)
                    tt(qk[:, i, :], bank(qkv_bank(i))[:, 0:2 * P], W("rqkv3")[:, 0:2 * P], ALU.add).then_inc(sem("qk"), 1)
                    tt(v3[:, btiles(b), w, :, 0:D3],
                       bank(qkv_bank(i))[:, 2 * P:3 * P].rearrange("p (g h c) -> p g h c", g=NG3, h=G3),
                       W("rqkv3")[:, 2 * P:3 * P].rearrange("p (g h c) -> p g h c", g=NG3, h=G3), ALU.add)\
                        .then_inc(sem("vv"), 1)

            def l3_rope(b):
                eng.wait_ge(sem("qk"), NT + NB * (b + 1))
                eng.wait_ge(sem("wide3"), 2)
                v = qk[:, btiles(b), :].rearrange("p w (r c) -> p (w r) c", c=G3)
                r1 = rt1[:, btiles(b), :].rearrange("p w (r c) -> p (w r) c", c=G3)
                r2 = rt2[:, btiles(b), :].rearrange("p w (r c) -> p (w r) c", c=G3)
                n = NB * 2 * NG3 * D3
                cos, sin = (t[:, :, :, :].rearrange("p w g c -> p (w g c)") for t in (cos3, sin3))
                tt(r1, v, cos.unsqueeze(2).to_broadcast([P, n, G3]), ALU.mult).then_inc(sem("rope_t3"), 1)
                for e in range(2):
                    tt(r2[:, e:n:2, :], v[:, 1 - e:n:2, :], sin[:, e:n:2].unsqueeze(2).to_broadcast([P, n // 2, G3]),
                       ALU.mult).then_inc(sem("rope_t3"), 1)
                eng.wait_ge(sem("rope_t3"), 3 * (b + 1))
                tt(v, r1, r2, ALU.add).then_inc(sem("rope3"), 1)

            def l3_rests(n):
                eng.wait_ge(sem("split1"), n + 1)
                tt(res3[:, n, :], bank(n), split[:, n, 0, :], ALU.subtract).then_inc(sem("res3"), 1)

            l3_qkv(0)
            l3_rope(0)
            l3_qkv(1)
            l3_rests(0)
            l3_rests(1)
            l3_rope(1)
            l3_rests(2)
            l3_rests(3)

            def l3_maxima(u, hp, j):
                eng.wait_ge(sem("s3_mm"), u * 8 + j + 1)
                dve.tensor_reduce(nm3[:, hp, j:j + 1], bank(j % 2), X_AXIS, ALU.max, negate=True)\
                    .then_inc(sem("max3"), 1)

            def l3_tokens(u):
                eng.wait_ge(sem("ot3_mm"), u + 1)
                o = bank(7)[:, 0:2 * P].rearrange("p (w h c) -> p w h c", w=NB, h=2)
                dve.reciprocal(rc3[:, :, :], o[:, :, :, D3]).then_inc(sem("rc3"), 1)
                eng.wait_ge(sem("rc3"), u + 1)
                tt(o3[:, :, :, :].rearrange("p w i f -> p w (i f)")[:, :, bass.ds(u * (2 * D3), 2 * D3)]
                   .rearrange("p w (h c) -> p w h c", h=2),
                   o[:, :, :, 0:D3], rc3[:, :, :].unsqueeze(3).to_broadcast([P, NB, 2, D3]), ALU.mult)\
                    .then_inc(sem("otok3"), 1)

            def l3_slot(u, hp, ahead=True, tokens=True):
                if ahead:
                    for j in range(8):
                        if j == 6 and tokens:
                            l3_tokens(u - 2)
                        l3_maxima(u + 2, hp, j)
                else:
                    l3_tokens(u - 2)

            for u in range(2):
                for j in range(8):
                    l3_maxima(u, u, j)
            l3_slot(0, 0, tokens=False)
            l3_slot(1, 1, tokens=False)
            with eng.Fori(1, NIT - 1) as it:
                l3_slot(it * 2, 0)
                l3_slot(it * 2 + 1, 1)
            for u in range(UNITS - 2, UNITS + 2):
                l3_slot(u, u % 2, ahead=False)
            residual_norm(4, ("proj_mm", 2), 2, False)
            for k in range(8):
                b, c = k // 4, k % 4
                eng.wait_ge(sem("fc_mm"), 2 * k + 2)
                eng.wait_ge(sem("sg3"), k + 1)
                dve.scalar_tensor_tensor(out=gT[:, c, half(b)], in0=bank(2 * (k % 2)), scalar=W("bfc")[:, c:c + 1],
                                         in1=sg3[:, k % 2, :], op0=ALU.add, op1=ALU.mult).then_inc(sem("gT"), 1)
            for b in range(B):
                add_residual(5, ("down_mm", 4), 6, b)


def _pack(spec, parts):
    import numpy as np
    cols = []
    for name, width in spec.items():
        a = parts[name]
        a = np.asarray(a, np.float32).reshape(a.shape[0], -1)
        assert a.shape[1] == width, name
        if a.shape[0] < P:
            a = np.concatenate([a, np.zeros((P - a.shape[0], width), np.float32)])
        cols.append(a)
    return np.ascontiguousarray(np.concatenate(cols, 1))


def _rope_angles(n, dim):
    import numpy as np
    inv = np.float32(1.0) / np.float32(10000.0) ** (np.arange(0, dim, 2, dtype=np.float32) / np.float32(dim))
    return np.arange(n, dtype=np.float32)[:, None] * inv[None, :].astype(np.float32)


def _layout(inp):
    import numpy as np
    f = {k: np.asarray(v) for k, v in inp.items()}
    z = {}

    def chunks(w, ids):
        return np.concatenate([w[:, P * j:P * (j + 1)] for j in ids], 1)

    def rows_to_cols(v, ids=None):
        v = v.reshape(-1, P)
        return (v if ids is None else v[list(ids)]).T

    def stacked(w):
        return w.reshape(4, P, P).transpose(1, 0, 2)

    p = np.arange(P)
    z["ident"] = np.eye(P)
    ws = f["L0_cond_W_self"]
    z["wsv"], z["wsq"] = ws[:, :D].T, ws[:, D:].T
    z["wq"] = f["L0_cond_Wq"].transpose(2, 0, 1)
    z["wk"] = f["L0_cond_Wk"].transpose(2, 0, 1)
    z["wo"] = f["L0_cond_Wout"].reshape(2, P, D).transpose(2, 0, 1)
    z["kmask0"] = (p[:, None] // 8 == np.arange(H0)) * np.float32(1 / np.sqrt(8))
    r = np.arange(RC)
    z["vmask0"] = np.stack([HC * c + r[:, None] // M0 == np.arange(H0) for c in range(NC0)], 1)
    z["bself"] = rows_to_cols(f["L0_cond_b_self"])
    z["bq0"], z["bk0"], z["bout0"] = f["L0_cond_bq"].T, f["L0_cond_bk"].T, f["L0_cond_bout"].T
    z["cond"] = f["cond_1024"].T

    ada, bada = f["L1_cond_W_ada"], f["L1_cond_b_ada"]
    wm, bm = f["L2_cond_Wm"], f["L2_cond_bm"]
    wc, bc = f["L2_cond_Wc"], f["L2_cond_bc"]
    z["wcol1"], z["wgate1"] = chunks(ada, (0, 1, 3, 4)), chunks(ada, (2, 5))
    z["wt1"] = f["L3_cond_w_t1"]
    z["wqkv1"], z["wout1"], z["wff1_1"] = f["L1_cond_W_qkv"], f["L1_cond_W_out"], f["L1_cond_W_ff1"]
    z["wff2_1"] = stacked(f["L1_cond_W_ff2"])
    z["kmask1"] = p[:, None] // D1 == np.arange(H1)
    ang = _rope_angles(P, D1)
    z["cos1"] = np.repeat(np.cos(ang), 2, 1)
    z["sin1"] = np.repeat(np.sin(ang), 2, 1) * np.where(np.arange(D1) < D1 // 2, -1.0, 1.0)
    z["bff1_1"] = rows_to_cols(f["L1_cond_b_ff1"])
    z["bmod"] = np.concatenate([rows_to_cols(bada, (0, 1, 3, 4)), rows_to_cols(bm, (0, 1, 3, 4)),
                                rows_to_cols(bc), rows_to_cols(f["L3_cond_b_t1"])], 1)
    z["bmodd"] = rows_to_cols(f["L3_cond_b_t2"])
    z["s1a"], z["s1b"] = rows_to_cols(f["L1_cond_scale1"]), rows_to_cols(f["L1_cond_scale2"])
    z["g3a"], z["g3b"] = rows_to_cols(f["L3_cond_g1"]), rows_to_cols(f["L3_cond_g2"])

    z["wcol2"] = np.concatenate([chunks(wm, (0, 1, 3, 4)), wc], 1)
    z["wgate2"] = chunks(wm, (2, 5))
    z["wff1_2"], z["wff2_2"] = f["L2_cond_W1"], stacked(f["L2_cond_W2"])
    bre, bim, cre, cim = (f["L2_cond_" + n] for n in ("B_re", "B_im", "C_re", "C_im"))
    z["bx"] = np.concatenate([bre, bim, bim, bre])
    z["by"] = np.concatenate([bim, bre, bre, bim])
    z["cta"] = np.concatenate([cre.T, cim.T] * 2)
    z["ctb"] = np.concatenate([cim.T, cre.T] * 2)
    z["steps_hi"] = np.tile(16 * np.arange(T // 16), (P, 1))
    z["steps_lo"] = np.tile(np.arange(16), (P, 1))
    for n in ("lam_re", "lam_im", "log_step"):
        src = f["L2_cond_" + {"lam_re": "Lam_re", "lam_im": "Lam_im", "log_step": "log_step"}[n]]
        z[n] = np.tile(src, 4)[:, None]
    q = p // 32
    z["sa"] = np.where(q == 3, -1.0, 1.0)[:, None]
    z["sb"] = np.where(q == 0, -1.0, 1.0)[:, None]
    own = (p[:, None] // 64 == np.arange(B)[None, :])
    z["sign1"] = own * np.where(q % 2 == 0, 2.0, -2.0)[:, None]
    z["sign2"] = own * -2.0
    z["dcol"] = rows_to_cols(f["L2_cond_D_diag"])
    z["bff1_2"] = rows_to_cols(f["L2_cond_b1"])
    z["halfpi"] = np.full((P, 1), np.pi / 2)

    hd, g, c = np.meshgrid(np.arange(D3), np.arange(NG3), np.arange(G3), indexing="ij")
    perm = np.empty(P, int)
    perm[(g * 32 + hd * G3 + c).ravel()] = ((g * G3 + c) * D3 + hd).ravel()
    wqkv, bqkv = f["L3_cond_w_qkv"], f["L3_cond_b_qkv"]
    order = np.concatenate([perm, P + perm, 2 * P + np.arange(P)])
    z["wcol3"], z["wqkv3"], z["wao"] = f["L3_cond_w_t2"], wqkv[:, order], f["L3_cond_w_ao"]
    z["wfc"], z["wfo"] = f["L3_cond_w_fc"], stacked(f["L3_cond_w_fo"])
    ang = _rope_angles(T, D3).reshape(NB, P, D3 // 2).transpose(1, 0, 2)
    sign = np.where(np.arange(D3) % 2 == 0, -1.0, 1.0)
    z["cos3"] = np.repeat(np.cos(ang), 2, 2)
    z["sin3"] = np.repeat(np.sin(ang), 2, 2) * sign
    z["bfc"] = rows_to_cols(f["L3_cond_b_fc"])

    z["wbias0"], z["bbias0"] = f["L0_cond_w_bias"][None], f["L0_cond_b_bias"].reshape(1, 1)
    z["rgate"] = np.concatenate([bada.reshape(6, P)[[2, 5]].ravel(), bm.reshape(6, P)[[2, 5]].ravel()])[None]
    z["rqkv1"], z["rout1"], z["rff2_1"] = (f["L1_cond_" + n][None] for n in ("b_qkv", "b_out", "b_ff2"))
    z["rff2_2"] = f["L2_cond_b2"][None]
    z["rqkv3"], z["rao"], z["rfo"] = bqkv[order][None], f["L3_cond_b_ao"][None], f["L3_cond_b_fo"][None]

    adj = f["mask_BxSxSx11_ik0"]
    adj = [adj[:, :, :M0, :], adj[:, :M0, :, :].transpose(0, 2, 1, 3)]
    adj = np.stack([a.reshape(NT, P, M0 * L).transpose(1, 0, 2).reshape(P, NT * M0 * L) for a in adj])
    return {
        "w0": _pack(W0, z), "wm": _pack(WM, z), "w1": _pack(W1, z), "w2": _pack(W2, z), "w3": _pack(W3, z),
        "rows": np.concatenate([z[n].reshape(1, -1) for n in ROWS], 1).astype(np.float32),
        "xt": np.ascontiguousarray(f["x"].reshape(B * T, D).T),
        "adj": np.ascontiguousarray(adj),
    }


def kernel(**inputs):
    import numpy as np
    import concourse.bacc as bacc
    from concourse.bass_utils import run_bass_kernel_spmd

    nc = bacc.Bacc("TRN2", target_bir_lowering=False, num_devices=1)
    arrays = _layout(inputs)
    args = [nc.dram_tensor(n, arrays[n].shape, mybir.dt.from_np(arrays[n].dtype), kind="ExternalInput").ap()
            for n in ("w0", "wm", "w1", "w2", "w3", "rows", "xt", "adj")]
    out = nc.dram_tensor("out", (P, B * T), F32, kind="ExternalOutput").ap()
    q_scr = nc.dram_tensor("q_scr", (NIT, 3, 32, T), BF16, kind="Internal").ap()
    k_scr = nc.dram_tensor("k_scr", (NIT, 5, 32, T), BF16, kind="Internal").ap()
    build_program(nc, *args, out, q_scr, k_scr)
    r = run_bass_kernel_spmd(nc, [arrays], core_ids=[0])
    y = np.asarray(r.results[0]["out"]).reshape(P, NT, D)
    return np.ascontiguousarray(y.transpose(1, 0, 2)).reshape(B, T, D)
```

```python
from contextlib import ExitStack

import concourse.bass as bass
from concourse import mybir

F32 = mybir.dt.float32
BF16 = mybir.dt.bfloat16
I32 = mybir.dt.int32
ALU = mybir.AluOpType
ACT = mybir.ActivationFunctionType
X_AXIS = mybir.AxisListType.X

P = 128
B, T, D = 2, 512, 128
NB = T // P
NT = B * NB
L, M0 = 11, 20
H0, H1, H3 = 16, 8, 16
HC = 6
NC0 = 3
RC = HC * M0
RLAST = H0 * M0 - 2 * RC
D1 = D // H1
D3 = D // H3
PAD = 32
G3 = 4
NG3 = H3 // G3
NIT = B * NG3
UNITS = 2 * NIT
NROW = 9 * D3
AUG = 96
NEG = -9000000000000000.0
ROUND = 1.5 * 2.0 ** 23
ROUND12 = 1.5 * 2.0 ** 11
TWO_PI = 6.283185307179586
TURN = (6.28125, 0.0019350051879882812, 3.0199159819e-07)

W0 = dict(ident=P, wsv=P, wsq=P, wq=2 * P, wk=2 * P, wo=2 * P, kmask0=H0, vmask0=NC0 * H0,
          bself=1, bq0=2, bk0=2, bout0=2, cond=2, steps_hi=T // 16, steps_lo=16,
          lam_re=1, lam_im=1, log_step=1, sa=1, sb=1, sign1=2, sign2=2, dcol=1, halfpi=1)
WM = dict(wcol1=4 * P, wgate1=2 * P, wcol2=6 * P, wgate2=2 * P, wt1=2 * P, wcol3=4 * P,
          bmod=12, bmodd=4, s1a=1, s1b=1, g3a=1, g3b=1)
W1 = dict(wqkv1=3 * P, wout1=P, wff1_1=4 * P, wff2_1=4 * P, kmask1=H1, cos1=D1, sin1=D1, bff1_1=4)
W2 = dict(wff1_2=4 * P, wff2_2=4 * P, bx=P, by=P, cta=P, ctb=P, bff1_2=4)
W3 = dict(wqkv3=3 * P, wao=P, wfc=8 * P, wfo=4 * P, cos3=NB * D3, sin3=NB * D3, bfc=8)
NROWS = 4
ROWS = dict(wbias0=L, bbias0=1, rgate=4 * P, rqkv1=3 * P, rout1=P, rff2_1=P, rff2_2=P, rqkv3=3 * P,
            rao=P, rfo=P)


def build_program(nc, w0, wm, w1, w2, w3, rows, xt_in, adj_in, out, q_scr, k_scr):
    with ExitStack() as ctx:
        sems = {}

        def sem(name):
            if name not in sems:
                sems[name] = ctx.enter_context(nc.semaphore(name))
            return sems[name]

        def sb(name, shape, dt=F32):
            return ctx.enter_context(nc.sbuf_tensor(name, shape, dt))

        def arena(name, words):
            return [sb(name, [P, words]), 0]

        def carve(a, shape, dt=F32):
            n = 1
            for k in shape[1:]:
                n *= k
            words = n if dt in (F32, I32) else n // 2
            v = a[0][0:shape[0], a[1]:a[1] + words]
            a[1] += words
            if dt is not F32:
                v = v.bitcast(dt)
            names = "abcd"[:len(shape) - 1]
            if len(names) > 1:
                v = v.rearrange(f"p ({' '.join(names)}) -> p {' '.join(names)}",
                                **{c: k for c, k in zip(names, shape[1:])})
            return v

        packed = {}
        tiles = {}
        for tag, spec in (("w0", W0), ("wm", WM), ("w1", W1), ("w2", W2), ("w3", W3), ("rw", ROWS)):
            n = sum(spec.values())
            tiles[tag] = sb(tag + "_sb", [P, n])
            at = 0
            for name, width in spec.items():
                packed[name] = tiles[tag][:, at:at + width]
                at += width

        def W(name):
            return packed[name]

        ident = W("ident")
        attn = arena("attn", 23 * 1024)
        early = arena("early", 4 * 1024)
        mlp = arena("mlp", 4 * B * T)
        gT = carve(mlp, [P, 4, B * T])
        mlp[1] = 0
        rows_in = carve(mlp, [1, sum(ROWS.values())])

        adj = [carve(attn, [P, NT * M0 * L], I32) for d in range(2)]
        adj_w = [carve(attn, [P, NT * M0, L]), carve(mlp, [P, NT * M0, L])]
        msum = carve(attn, [P, 2, NT * M0])
        mbias = carve(attn, [P, 2, NT * M0])
        mpen = carve(attn, [P, 2, NT * M0])
        mtb = carve(attn, [P, 2, NT * M0])
        qhT = [carve(attn, [P, B * T]) for d in range(2)]
        kblk = [carve(attn, [P, H0, M0]) for j in range(4)]
        kvrep = [carve(attn, [P, NC0 * HC, M0]) for b in range(B)]
        vblk = [carve(attn, [RC, NC0, P]) for j in range(4)]
        w0p = carve(attn, [P, 4, 2, H0 * M0])
        w0T = [carve(attn, [RC, NC0, T]) for j in range(4)]
        l0sum = carve(attn, [P, B, T])
        xoT = carve(attn, [P, B * T])
        xT = carve(early, [P, B * T])
        sfT = carve(early, [P, B * T])
        keep = carve(early, [1, B * T])
        qrow = carve(early, [1, B * P])
        bc_cond = carve(early, [P, B, P])
        bc_silu = carve(early, [P, B, P])
        col = sb("col", [P, 26])
        er, ei = sb("er", [P, T]), sb("ei", [P, T])
        ones = sb("ones", [P, P])
        mx0 = sb("mx0", [P, 4, 2 * H0])
        sm0 = sb("sm0", [P, 4, 2 * H0])
        rs0 = sb("rs0", [P, 4, 2 * H0])
        bout_sum = sb("bout_sum", [P, 1])

        silu_c = sb("silu_c", [P, B])
        modc = sb("modc", [P, 12, B])
        modp = sb("modp", [P, 12, B])
        modd = sb("modd", [P, 4, B])
        modq = sb("modq", [P, 4, B])
        sgt = sb("sgt", [P, B])
        tpe = sb("tpe", [P, B])
        scl = sb("scl", [P, 6, B])
        shf = sb("shf", [P, 6, B])
        shtmp = sb("shtmp", [P, B])
        gate = sb("gate", [P, B, 4 * P])
        wout1g = sb("wout1g", [P, B, P])
        wff2g = [sb(f"wff2g{n}", [P, B, 4, P]) for n in range(2)]
        bres = sb("bres", [P, 3, B, P])

        X = sb("X", [P, NT, P])
        Xb = sb("Xb", [P, NT, P])
        st = sb("st", [P, NT, 6])
        mv = sb("mv", [P, NT, 2])
        msq = sb("msq", [P, NT])
        var = sb("var", [P, NT])
        rstd = sb("rstd", [P, NT])
        mhalf = sb("mhalf", [P, NT])
        xn = sb("xn", [P, NT, P])
        early[1] = 0
        qk = carve(early, [P, NT, 2 * P])
        hT = carve(early, [P, B * T])
        oT = carve(early, [P, B * T])

        attn[1] = 0
        v1 = carve(attn, [P, NT, H1, PAD])
        qT1 = carve(attn, [P, B * T])
        kT1 = carve(attn, [P, B * T])
        kb1 = carve(attn, [P, 2, H1, P])
        p1 = carve(attn, [P, 2, H1, P])
        pT1 = carve(attn, [P, 2, H1, P])
        os1 = carve(attn, [P, 2, 2, P])
        otok = carve(attn, [P, NT, P])
        mx1 = sb("mx1", [P, 2, H1])
        rc1 = sb("rc1", [P, 2, H1])

        attn[1] = 0
        v3 = carve(attn, [P, NIT, NB, G3, PAD])
        qa = [carve(attn, [P, G3, T], BF16) for j in range(2)]
        ka = [carve(attn, [P, G3, T], BF16) for j in range(2)]
        split = carve(attn, [P, 2 * B, 3, T], BF16)
        res3 = carve(attn, [P, 2 * B, T])
        tail = attn[1]
        p3 = carve(attn, [P, 2, 2, NB, T])
        o3 = carve(attn, [P, NB, NIT, G3 * D3])
        mlp[1] = 0
        vg = [carve(mlp, [P, NB, G3, PAD]) for j in range(2)]
        os3 = carve(mlp, [P, 2, T // 2])
        nm3 = sb("nm3", [P, 2, 2 * NB])
        zeros = sb("zeros", [P, 2 * NB])
        nr3 = sb("nr3", [P, 2 * NB])
        ms3 = sb("ms3", [P, P // (2 * NB), 2 * NB], BF16)
        mT3 = sb("mT3", [3 * 2 * NB, 2, P], BF16)
        identb = sb("identb", [P, P], BF16)
        rc3 = sb("rc3", [P, NB, 2])

        attn[1] = tail
        rt1 = carve(attn, [P, NT, 2 * P])
        rt2 = carve(attn, [P, NT, 2 * P])
        cos3 = carve(attn, [P, NB, 2 * NG3, D3])
        sin3 = carve(attn, [P, NB, 2 * NG3, D3])
        tA, tB, steps = (carve(attn, [P, T]) for j in range(3))
        ua = carve(attn, [P, T])
        ub = carve(attn, [P, T])
        uw = carve(attn, [P, T])
        uw2 = carve(attn, [P, T])
        xs = carve(attn, [P, T])
        bbar = carve(attn, [P, P])
        bbT = carve(attn, [P, P])
        cga = carve(attn, [P, B, P])
        cgb = carve(attn, [P, B, P])
        dg = carve(attn, [P, B, P])
        attn[1] = tail
        sg3 = carve(attn, [P, 2, T])

        PP = [ctx.enter_context(nc.psum_tensor(f"pp{j}", [P, 2, 512], F32)) for j in range(4)]

        def bank(k):
            return PP[k // 2][:, k % 2, :]

        block = ctx.enter_context(nc.Block())
        pe, dve, act, pool = nc.tensor, nc.vector, nc.scalar, nc.gpsimd

        def qkv_bank(i):
            return (6 + i) % 8

        def tile_cols(i):
            return slice(i * P, (i + 1) * P)

        def half(b):
            return slice(b * T, (b + 1) * T)

        def btiles(b):
            return slice(b * NB, (b + 1) * NB)

        @block.sync
        def _(sp):
            sp.dma_start(tiles["w0"][:, :], w0).then_inc(sem("ld_w0"), 16)
            sp.dma_start(adj[0][:, :], adj_in[0]).then_inc(sem("ld_adj0"), 16)
            sp.dma_start(tiles["wm"][:, :], wm).then_inc(sem("ld_wm"), 16)
            sp.dma_start(tiles["w2"][:, :], w2).then_inc(sem("ld_w2"), 16)
            sp.dma_start(tiles["w3"][:, :], w3).then_inc(sem("ld_w3"), 16)

            def store(b):
                for part in range(3):
                    for n, scr, places in ((2 * b, q_scr, (part,)), (2 * b + 1, k_scr, (part, part + 3))):
                        sp.wait_ge(sem(f"split{part + 1}"), n + 1)
                        for place in places:
                            if place < scr.shape[1]:
                                sp.dma_start(scr[b * NG3:(b + 1) * NG3, place, :, :], split[:, n, part, :])\
                                  .then_inc(sem(f"st_qk{b}"), 16)

            def load(u, par, hp):
                step_q = q_scr.rearrange("n i (d c) t -> (n i d) (c t)", c=G3)
                step_k = k_scr.rearrange("n i (d c) t -> (n i d) (c t)", c=G3)
                half_row = slice(hp * 2 * T, (hp + 1) * 2 * T)
                heads = slice(2 * hp, 2 * hp + 2)
                it = (u - hp) // 2 if isinstance(u, int) else u
                qs = step_q[bass.ds(it * (3 * D3), 3 * D3), half_row]
                ks = step_k[bass.ds(it * (5 * D3), 3 * D3), half_row]
                row = G3 * T
                sp.dma_start(qa[par][0:NROW, heads, :].rearrange("p c t -> p (c t)"),
                             qs.unsqueeze(0).to_broadcast([3, 3 * D3, 2 * T])).then_inc(sem(f"ld_q{par}{hp}"), 16)
                sp.dma_start(ka[par][0:NROW, heads, :].rearrange("p c t -> p (c t)"),
                             bass.AP(ks.tensor, ks.offset, [[D3 * row, 3], [row, 3 * D3], [1, 2 * T]]))\
                  .then_inc(sem(f"ld_q{par}{hp}"), 16)

            def maxima(u, par, hp):
                sp.wait_ge(sem("mT3"), u + 1)
                sp.dma_start(qa[par][AUG:AUG + 3, 2 * hp:2 * hp + 2, :].rearrange("p c t -> p (c t)"), mT3[:, hp, :])\
                  .then_inc(sem(f"ld_m{par}{hp}"), 16)

            sp.wait_ge(sem("zero3"), 4)
            store(0)
            sp.wait_ge(sem("st_qk0"), 16 * 8)
            for u in range(4):
                load(u, u // 2, u % 2)
            store(1)
            maxima(0, 0, 0)
            maxima(1, 0, 1)

            def slot(u, it, par, hp):
                sp.wait_ge(sem("st3"), u * 4 + 4)
                load(it + 2, par, hp)
                maxima(u + 2, 1 - par, hp)

            sp.wait_ge(sem("st_qk1"), 16 * 8)
            with sp.Fori(0, NIT // 2 - 1) as pair:
                for j in range(4):
                    slot(pair * 4 + j, pair * 2 + j // 2, j // 2, j % 2)
            maxima(UNITS - 2, 1, 0)
            maxima(UNITS - 1, 1, 1)

            for b in range(B):
                sp.wait_ge(sem("xr"), 2 * 5 + b + 1)
                sp.dma_start(out[:, b * T:(b + 1) * T], X[:, btiles(b), :].rearrange("p w f -> p (w f)"))\
                  .then_inc(sem("st_out"), 16)
            sp.wait_ge(sem("st_out"), 32)

        def third_part(tt, eng, n):
            eng.wait_ge(sem("split2"), n + 1)
            tt(split[:, n, 2, :], res3[:, n, :], split[:, n, 1, :], ALU.subtract).then_inc(sem("split3"), 1)

        freed = {}

        def claim(eng, k, name, value):
            if k in freed:
                eng.wait_ge(sem(freed[k][0]), freed[k][1])
            freed[k] = (name, value)

        @block.tensor
        def _(eng):
            def mm(o, l, r, start=True, stop=True):
                return pe.matmul(o, l, r, start=start, stop=stop)

            def bias_rows(j, k):
                lo, hi = 512 * j, min(512 * (j + 1), sum(ROWS.values()))
                claim(eng, k, "rows", j + 1)
                mm(bank(k)[:, 0:hi - lo], ones[0:1, :], rows_in[:, lo:hi]).then_inc(sem("rows_mm"), 1)

            eng.wait_ge(sem("ld_xT"), 16)
            eng.wait_ge(sem("consts"), 1)
            for b in range(B):
                claim(eng, 6 + b, "keep", b + 1)
                mm(bank(6 + b)[0:1, :], ones[:, 0:1], xT[:, half(b)]).then_inc(sem("rowsum"), 1)
            eng.wait_ge(sem("ld_w0"), 16)
            claim(eng, 5, "qrow", 1)
            for b in range(B):
                last = mm(bank(5)[0:1, b * P:(b + 1) * P], W("cond")[:, b:b + 1], W("wsq"))
            last.then_inc(sem("qrow_mm"), 1)
            eng.wait_ge(sem("ld_rows"), 16)
            bias_rows(0, 4)
            for b in range(B):
                claim(eng, b, "sfT", b + 1)
                mm(bank(b), W("wsv"), xT[:, half(b)], True, False)
                eng.wait_ge(sem("keep"), b + 1)
                eng.wait_ge(sem("qrow"), 1)
                mm(bank(b), qrow[:, b * P:(b + 1) * P], keep[:, half(b)], False, True).then_inc(sem("sf_mm"), 1)
            for b in range(B):
                eng.wait_ge(sem("sfT"), b + 1)
                for d in range(2):
                    n = 2 * b + d
                    claim(eng, 2 + n, "qhT", n + 1)
                    mm(bank(2 + n), W("wq")[:, tile_cols(d)], sfT[:, half(b)]).then_inc(sem("qh_mm"), 1)
            claim(eng, 6, "kblk", 4)
            for b in range(B):
                for d in range(2):
                    n = 2 * b + d
                    mm(bank(6)[:, 32 * n:32 * n + M0], W("wk")[:, tile_cols(d)], sfT[:, b * T:b * T + M0])\
                        .then_inc(sem("kh_mm"), 1)
            for j in range(1, NROWS):
                bias_rows(j, (7, 0, 1)[j - 1])
            for b in range(B):
                eng.wait_ge(sem("kvrep"), b + 1)
                for d in range(2):
                    n = 2 * b + d
                    claim(eng, 4 + n, "vblk", n + 1)
                    for c in range(NC0):
                        last = mm(bank(4 + n)[0:RC, c * P:(c + 1) * P],
                                  kvrep[b][:, HC * c:HC * c + HC, :].rearrange("p h m -> p (h m)"),
                                  W("wo")[:, tile_cols(d)])
                    last.then_inc(sem("vf_mm"), 1)

            def l0_scores(g):
                b, d, h = g // 4, (g // 2) % 2, g % 2
                pr = PP[g % 2]
                claim(eng, 2 * (g % 2), "s0_m", g + 1)
                claim(eng, 2 * (g % 2) + 1, "s0_m", g + 1)
                eng.wait_ge(sem("kblk"), 2 * b + d + 1)
                eng.wait_ge(sem("qhT"), 2 * b + d + 1)
                for t in range(2):
                    i = b * NB + 2 * h + t
                    last = mm(pr[:, t, 0:H0 * M0], qhT[d][:, tile_cols(i)],
                              kblk[2 * b + d][:, :, :].rearrange("p h m -> p (h m)"))
                last.then_inc(sem("s0_mm"), 1)

            def l0_turn(g):
                claim(eng, 4, "w0T", 2 * g + 2)
                claim(eng, 5, "w0T", 2 * g + 2)
                eng.wait_ge(sem("w0n"), g + 1)
                for t in range(2):
                    for c in range(NC0):
                        n = RC if c < 2 else RLAST
                        last = pe.transpose(PP[2][0:n, t, c * P:(c + 1) * P],
                                            w0p[:, g % 4, t, c * RC:c * RC + n], ident)
                last.then_inc(sem("w0_tr"), 1)

            def l0_out(b, d):
                k = 6 + b
                if d == 0:
                    claim(eng, k, "l0sum", b + 1)
                eng.wait_ge(sem("w0T"), 8 * b + 4 * d + 4)
                eng.wait_ge(sem("vblk"), 2 * b + d + 1)
                for c in range(NC0):
                    n = RC if c < 2 else RLAST
                    last = mm(bank(k), vblk[2 * b + d][0:n, c, :], w0T[2 * b + d][0:n, c, :],
                              d == 0 and c == 0, d == 1 and c == NC0 - 1)
                if d:
                    last.then_inc(sem("o0_mm"), 1)

            def l0_back(b):
                claim(eng, b, "x0", b + 1)
                eng.wait_ge(sem("l0x"), b + 1)
                for w in range(NB):
                    last = pe.transpose(bank(b)[:, tile_cols(w)], xoT[:, tile_cols(b * NB + w)], ident)
                last.then_inc(sem("l0_back"), 1)

            for g in range(4):
                l0_scores(g)

            claim(eng, 4, "modc", 1)
            eng.wait_ge(sem("ld_wm"), 16)
            eng.wait_ge(sem("silu_c"), 1)
            eng.wait_ge(sem("bcast"), 2)
            cond = W("cond")
            for j in range(12):
                lhs, rhs = ((W("wcol1"), silu_c[:, :]) if j < 4 else
                            (W("wcol2"), cond) if j < 10 else (W("wt1"), cond))
                at = j if j < 4 else j - 4 if j < 10 else j - 10
                last = mm(bank(4)[:, 2 * j:2 * j + 2], lhs[:, tile_cols(at)], rhs)
            last.then_inc(sem("mod_mm"), 1)
            for b in range(B):
                claim(eng, 5 + b, "gate", b + 1)
                mm(bank(5 + b)[:, 0:2 * P], bc_silu[:, b, :], W("wgate1"))
                mm(bank(5 + b)[:, 2 * P:4 * P], bc_cond[:, b, :], W("wgate2")).then_inc(sem("gate_mm"), 1)
            claim(eng, 7, "modd", 1)
            eng.wait_ge(sem("tpe"), 1)
            for j in range(4):
                last = mm(bank(7)[:, 2 * j:2 * j + 2], W("wcol3")[:, tile_cols(j)], tpe[:, :])
            last.then_inc(sem("modd_mm"), 1)

            for g in range(8):
                if g + 4 < 8:
                    l0_scores(g + 4)
                if g == 6:
                    l0_out(1, 0)
                l0_turn(g)
                if g == 3:
                    l0_out(0, 0)
                if g == 4:
                    l0_out(0, 1)
                if g == 6:
                    l0_back(0)
            l0_out(1, 1)

            def l3_qkT(b):
                for j in range(2):
                    n = 2 * b + j
                    claim(eng, n, "res3", n + 1)
                    eng.wait_ge(sem("rope3"), b + 1)
                    for wt in range(NB):
                        last = pe.transpose(bank(n)[:, tile_cols(wt)], qk[:, b * NB + wt, j * P:(j + 1) * P], ident)
                    last.then_inc(sem("qkT3_mm"), 1)

            def norm_turn(n, b):
                claim(eng, 4 + b, "hT", 2 * n + b + 1)
                eng.wait_ge(sem("xn"), NT * n + NB * (b + 1))
                for w in range(NB):
                    last = pe.transpose(bank(4 + b)[:, tile_cols(w)], xn[:, b * NB + w, :], ident)
                last.then_inc(sem("norm_tr"), 1)

            def mlp_down(n, w, b):
                claim(eng, 6 + b, "xr", 2 * {0: 1, 1: 3, 2: 5}[n] + b + 1)
                eng.wait_ge(sem("gT"), 8 * n + 4 * b + 4)
                for wt in range(NB):
                    for c in range(4):
                        last = mm(bank(6 + b)[:, tile_cols(wt)], gT[:, c, tile_cols(b * NB + wt)], w(b, c),
                                  c == 0, c == 3)
                last.then_inc(sem("down_mm"), 1)

            def mlp(n, w_up, w_down):
                m = 3 if n else 1
                if n:
                    norm_turn(m, 0)
                for k in range(8):
                    b, c = k // 4, k % 4
                    if k == 0 and n == 0:
                        o_proj(0, 1, 7, wout1g[:, 1, :])
                    if k == (2 if n else 3):
                        norm_turn(m, 1)
                    if k == 6:
                        eng.wait_ge(sem("gated_w"), 4 + 2 * n)
                        mlp_down(n, w_down, 0)
                    eng.wait_ge(sem("hT"), 2 * m + b + 1)
                    claim(eng, k % 4, "gT", 8 * n + k + 1)
                    mm(bank(k % 4), w_up[:, tile_cols(c)], hT[:, half(b)]).then_inc(sem("up_mm"), 1)
                mlp_down(n, w_down, 1)

            def qkv(n, w, b):
                for i in range(b * NB, (b + 1) * NB):
                    if i % NB == 0:
                        norm_turn(4 if n else 0, b)
                    if n == 0 and i == 0:
                        l0_back(1)
                    if i == 6:
                        (l3_qkT if n else l1_qkT)(0)
                    claim(eng, qkv_bank(i), "vv", NT * n + i + 1)
                    eng.wait_ge(sem("hT"), 2 * (4 if n else 0) + b + 1)
                    mm(bank(qkv_bank(i))[:, 0:3 * P], hT[:, tile_cols(i)], w).then_inc(sem("qkv_mm"), 1)

            def l1_qkT(b):
                eng.wait_ge(sem("rope"), b + 1)
                for j in range(2):
                    claim(eng, 6 + j, "qkT1", 2 * b + j + 1)
                    for wt in range(NB):
                        last = pe.transpose(bank(6 + j)[:, tile_cols(wt)], qk[:, b * NB + wt, j * P:(j + 1) * P], ident)
                    last.then_inc(sem("qkT_mm"), 1)

            for b in range(B):
                qkv(0, W("wqkv1"), b)

            def l1_scores(w):
                claim(eng, 2 * (w % 2), "sub1", w + 1)
                claim(eng, 2 * (w % 2) + 1, "sub1", w + 1)
                eng.wait_ge(sem("kb1"), w + 1)
                for j in range(2):
                    last = mm(PP[w % 2][:, j, :], qT1[:, tile_cols(w)],
                              kb1[:, w % 2, 4 * j:4 * j + 4, :].rearrange("p h k -> p (h k)"))
                last.then_inc(sem("s1_mm"), 1)

            def l1_turn(w):
                claim(eng, 4, "pT1", w + 1)
                claim(eng, 5, "pT1", w + 1)
                eng.wait_ge(sem("exp1"), w + 1)
                for h in range(H1):
                    last = pe.transpose(PP[2][:, h // 4, tile_cols(h % 4)], p1[:, w % 2, h, :], ident)
                last.then_inc(sem("p1_tr"), 1)

            def l1_values(w):
                claim(eng, 6, "os1", w + 1)
                eng.wait_ge(sem("pT1"), w + 1)
                eng.wait_ge(sem("vv"), w + 1)
                eng.wait_ge(sem("ones_v"), 2)
                for h in range(H1):
                    g = h % 4
                    last = mm(bank(6)[PAD * g:PAD * g + PAD, tile_cols(h // 4)], v1[:, w, h, :], pT1[:, w % 2, h, :])
                last.then_inc(sem("pv1_mm"), 1)

            def l1_tokens(w):
                claim(eng, 7, "otok1", w + 1)
                eng.wait_ge(sem("os1"), w + 1)
                for j in range(2):
                    last = pe.transpose(bank(7)[:, tile_cols(j)], os1[:, w % 2, j, :], ident)
                last.then_inc(sem("ot1_mm"), 1)

            def o_turn(n, b, k, src):
                claim(eng, k, "oT", 2 * n + b + 1)
                eng.wait_ge(sem("otok1" if n == 0 else "otok3"), (NB if n == 0 else NIT) * (b + 1))
                for wt in range(NB):
                    last = pe.transpose(bank(k)[:, tile_cols(wt)], src(wt), ident)
                last.then_inc(sem("oT_mm"), 1)

            def o_proj(n, b, k, w):
                claim(eng, k, "xr", 2 * (4 if n else 0) + b + 1)
                eng.wait_ge(sem("oT"), 2 * n + b + 1)
                for wt in range(NB):
                    last = mm(bank(k)[:, tile_cols(wt)], oT[:, tile_cols(b * NB + wt)], w)
                last.then_inc(sem("proj_mm"), 1)

            for k in range(NT + 4):
                if k < NT:
                    l1_scores(k)
                if k == 2:
                    l1_qkT(1)
                if 0 <= k - 2 < NT:
                    l1_turn(k - 2)
                if 0 <= k - 3 < NT:
                    l1_values(k - 3)
                if k == NT:
                    o_turn(0, 0, 0, lambda wt: otok[:, wt, :])
                if 0 <= k - 4 < NT:
                    l1_tokens(k - 4)
                if k == NT + 1:
                    eng.wait_ge(sem("gated_w"), 2)
                    o_proj(0, 0, 2, wout1g[:, 0, :])
            o_turn(0, 1, 1, lambda wt: otok[:, NB + wt, :])
            norm_turn(1, 0)

            mlp(0, W("wff1_1"), lambda b, c: wff2g[0][:, b, c, :])

            claim(eng, 0, "bbT", 1)
            eng.wait_ge(sem("bbar"), 1)
            pe.transpose(bank(0)[:, 0:P], bbar[:, :], ident).then_inc(sem("bbar_tr"), 1)
            eng.wait_ge(sem("bbT"), 1)
            claim(eng, 2, "rotin", 1)
            claim(eng, 3, "rotin", 2)
            for b in range(B):
                norm_turn(2, b)
                eng.wait_ge(sem("hT"), 2 * 2 + b + 1)
                for j in range(2):
                    last = mm(bank(2 + j)[64 * b:64 * b + 64, :], bbT[:, 64 * j:64 * j + 64], hT[:, half(b)])
            last.then_inc(sem("u_mm"), 1)
            eng.wait_ge(sem("cg"), 3 * B)
            for b in range(B):
                claim(eng, 6 + b, "xr", 2 * 2 + b + 1)
                for wt in range(NB):
                    mm(bank(6 + b)[:, tile_cols(wt)], hT[:, tile_cols(b * NB + wt)], dg[:, b, :], wt == 0, False)
            eng.wait_ge(sem("rotout"), 2)
            for b in range(B):
                for wt in range(NB):
                    o = bank(6 + b)[:, tile_cols(wt)]
                    mm(o, uw[:, tile_cols(wt)], cga[:, b, :], False, False)
                    last = mm(o, uw2[:, tile_cols(wt)], cgb[:, b, :], False, wt == NB - 1)
                last.then_inc(sem("y_mm"), 1)
            mlp(1, W("wff1_2"), lambda b, c: wff2g[1][:, b, c, :])

            for b in range(B):
                qkv(1, W("wqkv3"), b)
            l3_qkT(1)
            eng.wait_ge(sem("res3"), 2)
            eng.wait_ge(sem("vv"), 2 * NT)
            eng.wait_ge(sem("hT"), 2 * 4 + 2)

            def l3_score(u, par, hp, j):
                h, w = 2 * hp + j // NB, j % NB
                if not (isinstance(u, int) and u * 8 + j < 2):
                    eng.wait_ge(sem("max3"), u * 8 + (j - 1))
                mm(bank(j % 2), qa[par][0:AUG, h, tile_cols(w)], ka[par][0:AUG, h, :]).then_inc(sem("s3_mm"), 1)

            def l3_pair(u, par, hp, s, t):
                h = 2 * hp + s // 2
                if t == 0 and not (isinstance(u, int) and u * 4 + s < 2):
                    eng.wait_ge(sem("exp3"), u * 4 + (s - 1))
                last = mm(PP[1 + s % 2][:, t, :], ka[par][:, h, tile_cols(2 * (s % 2) + t)], qa[par][:, h, :])
                if t:
                    last.then_inc(sem("st3"), 1)

            def l3_values(u, par, hp, k):
                if k == 0:
                    eng.wait_ge(sem("exp3"), u * 4 + 4)
                    eng.wait_ge(sem("vg"), (u // 2 if isinstance(u, int) else l3_it["values"]) + 1)
                    if not (isinstance(u, int) and u == 0):
                        eng.wait_ge(sem("os3"), u)
                for e in range(2):
                    for h in range(2):
                        strip = PAD * (2 * e + h)
                        last = mm(bank(6)[strip:strip + PAD, hp * 2 * P:(hp + 1) * 2 * P]
                                  .rearrange("p (w q) -> p w q", w=2),
                                  vg[par][:, k, 2 * hp + h, :],
                                  p3[:, hp, h, k, :].rearrange("p (w e q) -> p e w q", e=2, w=2)[:, e, :, :],
                                  k == 0, k == NB - 1)
                if k == NB - 1:
                    last.then_inc(sem("pv3_mm"), 1)

            def l3_turn_max(u):
                eng.wait_ge(sem("ms3"), u + 1)
                pe.transpose(bank(7)[:, 2 * P:2 * P + P // 2].bitcast(BF16), ms3[:, :, :].rearrange("p i n -> p (i n)"),
                             identb[:, :]).then_inc(sem("m3_tr"), 1)

            def l3_tokens(u, hp):
                eng.wait_ge(sem("os3"), u + 1)
                if not (isinstance(u, int) and u >= UNITS - 3):
                    eng.wait_ge(sem("mT3"), u + 4)
                else:
                    eng.wait_ge(sem("otok3"), u)
                for w in range(2):
                    last = pe.transpose(bank(7)[:, tile_cols(w)], os3[:, hp, tile_cols(w)], ident)
                last.then_inc(sem("ot3_mm"), 1)

            def l3_slot(u, par, hp, ready, own=True, ahead=True, turn=True, values=True, tokens=True):
                if own:
                    eng.wait_ge(sem(f"ld_m{par}{hp}"), 16 * ready)
                if ahead:
                    eng.wait_ge(sem(f"ld_q{1 - par}{hp}"), 32 * (ready + par))
                for s in range(4):
                    for t in range(2):
                        if own:
                            l3_pair(u, par, hp, s, t)
                        if ahead:
                            l3_score(u + 2, 1 - par, hp, 2 * s + t)
                    if s == 1 and turn:
                        l3_turn_max(u + 1)
                    if values:
                        l3_values(u - 1, par if hp else 1 - par, 1 - hp, s)
                    if s == 2 and tokens:
                        l3_tokens(u - 2, hp)

            eng.wait_ge(sem("identb"), 1)
            eng.wait_ge(sem("consts"), 4)
            eng.wait_ge(sem("ld_q00"), 32)
            for j in range(8):
                l3_score(0, 0, 0, j)
            eng.wait_ge(sem("ld_q01"), 32)
            for j in range(8):
                if j == 4:
                    l3_turn_max(0)
                l3_score(1, 0, 1, j)
            eng.wait_ge(sem("res3"), 4)
            l3_slot(0, 0, 0, 1, values=False, tokens=False)
            l3_slot(1, 0, 1, 1, tokens=False)
            l3_it = {}
            with eng.Fori(0, NIT // 2 - 1) as pair:
                for j in range(4):
                    u, par = pair * 4 + (2 + j), 1 - j // 2
                    l3_it["values"] = pair * 2 + (1 + j) // 2
                    l3_slot(u, par, j % 2, pair + (1 + j // 2))

            def o3_tile(b):
                return lambda wt: o3[:, wt, b * NG3:(b + 1) * NG3, :].rearrange("p g f -> p (g f)")

            freed.clear()
            l3_slot(UNITS - 2, 1, 0, NIT // 2, ahead=False)
            eng.wait_ge(sem("max3"), 8 * UNITS)
            o_turn(1, 0, 0, o3_tile(0))
            l3_slot(UNITS - 1, 1, 1, NIT // 2, ahead=False, turn=False)
            o_proj(1, 0, 1, W("wao"))
            l3_slot(UNITS, 0, 0, 0, own=False, ahead=False, turn=False)
            l3_tokens(UNITS - 1, 1)
            o_turn(1, 1, 6, o3_tile(1))
            eng.wait_ge(sem("exp3"), 4 * UNITS)
            norm_turn(5, 0)
            o_proj(1, 1, 7, W("wao"))

            for k in range(8):
                b, c = k // 4, k % 4
                if k == 3:
                    norm_turn(5, 1)
                eng.wait_ge(sem("hT"), 2 * 5 + b + 1)
                claim(eng, 2 * (k % 2), "gT", 16 + k + 1)
                claim(eng, 2 * (k % 2) + 1, "sg3", k + 1)
                mm(bank(2 * (k % 2) + 1), W("wfc")[:, tile_cols(4 + c)], hT[:, half(b)]).then_inc(sem("fc_mm"), 1)
                mm(bank(2 * (k % 2)), W("wfc")[:, tile_cols(c)], hT[:, half(b)]).then_inc(sem("fc_mm"), 1)
            for b in range(B):
                mlp_down(2, lambda b, c: W("wfo")[:, tile_cols(c)], b)

        @block.scalar
        def _(eng):
            eng.dma_start(xT[:, :], xt_in).then_inc(sem("ld_xT"), 16)
            eng.dma_start(rows_in, rows).then_inc(sem("ld_rows"), 16)
            eng.dma_start(adj[1][:, :], adj_in[1]).then_inc(sem("ld_adj1"), 16)
            eng.dma_start(tiles["w1"][:, :], w1).then_inc(sem("ld_w1"), 16)

            def ident_act(o, i, bias=None, scale=None):
                kw = {}
                if bias is not None:
                    kw["bias"] = bias
                if scale is not None:
                    kw["scale"] = scale
                return act.activation(o, i, ACT.Identity, **kw)

            eng.wait_ge(sem("ld_w0"), 16)
            act.activation(silu_c[:, :], W("cond"), ACT.Silu).then_inc(sem("silu_c"), 1)
            act.activation(col[:, 0:1], W("log_step"), ACT.Exp).then_inc(sem("dt"), 1)
            eng.wait_ge(sem("rho_in"), 1)
            act.activation(col[:, 2:3], col[:, 1:2], ACT.Exp).then_inc(sem("rho"), 1)
            eng.wait_ge(sem("turn1"), 1)
            act.activation(col[:, 24:25], col[:, 22:23], ACT.Sin, scale=TWO_PI).then_inc(sem("rot1"), 1)
            act.activation(col[:, 25:26], col[:, 23:24], ACT.Sin, scale=-TWO_PI, bias=W("halfpi")).then_inc(sem("rot1"), 1)
            eng.wait_ge(sem("qrow_mm"), 1)
            act.copy(qrow[:, :], bank(5)[0:1, 0:2 * P]).then_inc(sem("qrow"), 1)

            def rows_evac(j):
                lo, hi = 512 * j, min(512 * (j + 1), sum(ROWS.values()))
                eng.wait_ge(sem("rows_mm"), j + 1)
                act.copy(tiles["rw"][:, lo:hi], bank((4, 7, 0, 1)[j])[:, 0:hi - lo]).then_inc(sem("rows"), 1)

            rows_evac(0)
            for b in range(B):
                eng.wait_ge(sem("sf_mm"), b + 1)
                ident_act(sfT[:, half(b)], bank(b), W("bself")).then_inc(sem("sfT"), 1)
            for b in range(B):
                for d in range(2):
                    n = 2 * b + d
                    eng.wait_ge(sem("qh_mm"), n + 1)
                    ident_act(qhT[d][:, half(b)], bank(2 + n), W("bq0")[:, d:d + 1]).then_inc(sem("qhT"), 1)
            for j in range(1, NROWS):
                rows_evac(j)
            eng.wait_ge(sem("ld_adj1"), 16)
            act.copy(adj_w[1][:, :, :].rearrange("p n l -> p (n l)"), adj[1][:, :]).then_inc(sem("adj_f"), 1)

            def l0_exp(g):
                eng.wait_ge(sem("sub0"), g + 1)
                act.activation(w0p[:, g % 4, :, :], w0p[:, g % 4, :, :], ACT.Exp).then_inc(sem("exp0"), 1)

            def l0_evac(g):
                b, d, h = g // 4, (g // 2) % 2, g % 2
                dst = w0T[2 * b + d]
                cols = slice(2 * h * P, 2 * h * P + 2 * P)
                pr = PP[2]
                eng.wait_ge(sem("w0_tr"), g + 1)
                act.copy(dst[:, 0:2, cols].rearrange("r c (t q) -> r t c q", t=2),
                         pr[0:RC, :, 0:2 * P].rearrange("r t (c q) -> r t c q", c=2)).then_inc(sem("w0T"), 1)
                act.copy(dst[0:RLAST, 2, cols].rearrange("r (t q) -> r t q", t=2),
                         pr[0:RLAST, :, 2 * P:3 * P]).then_inc(sem("w0T"), 1)

            def x0_evac(b):
                eng.wait_ge(sem("l0_back"), b + 1)
                act.copy(X[:, btiles(b), :].rearrange("p w f -> p (w f)"), bank(b)).then_inc(sem("x0"), 1)

            for k in range(8 + 2):
                if k == 2:
                    eng.wait_ge(sem("modc"), 1)
                    act.activation(sgt[:, :], modc[:, 11, :], ACT.Silu).then_inc(sem("sgt"), 1)
                if k < 8:
                    l0_exp(k)
                if k >= 2:
                    l0_evac(k - 2)
                if k - 2 == 6:
                    x0_evac(0)

            def norm_evac(n, b):
                eng.wait_ge(sem("norm_tr"), 2 * n + b + 1)
                if n == 0:
                    eng.wait_ge(sem("scl"), 1)
                ident_act(hT[:, half(b)], bank(4 + b), shf[:, n, b:b + 1], scl[:, n, b:b + 1]).then_inc(sem("hT"), 1)

            def mlp_act(n, bias):
                for k in range(8):
                    b, c = k // 4, k % 4
                    if n and k == 0:
                        norm_evac(3, 0)
                    if k == (2 if n else 3):
                        norm_evac(3 if n else 1, 1)
                    eng.wait_ge(sem("up_mm"), 8 * n + k + 1)
                    act.activation(gT[:, c, half(b)], bank(k % 4), ACT.Gelu_apprx_tanh, bias=bias[:, c:c + 1])\
                       .then_inc(sem("gT"), 1)

            def oT_evac(n, b, k):
                eng.wait_ge(sem("oT_mm"), 2 * n + b + 1)
                act.copy(oT[:, half(b)], bank(k)).then_inc(sem("oT"), 1)

            def l1_qkT(b):
                for j, dst in enumerate((qT1, kT1)):
                    eng.wait_ge(sem("qkT_mm"), 2 * b + j + 1)
                    act.copy(dst[:, half(b)], bank(6 + j)).then_inc(sem("qkT1"), 1)

            norm_evac(0, 0)
            x0_evac(1)
            norm_evac(0, 1)
            l1_qkT(0)
            for k in range(NT + 2):
                if k == 2:
                    l1_qkT(1)
                w = k
                if w < NT:
                    eng.wait_ge(sem("sub1"), w + 1)
                    act.activation(p1[:, w % 2, :, :], p1[:, w % 2, :, :], ACT.Exp, scale=float(D1) ** -0.5)\
                       .then_inc(sem("exp1"), 1)
                w = k - 1
                if 0 <= w < NT:
                    eng.wait_ge(sem("p1_tr"), w + 1)
                    if w >= 2:
                        eng.wait_ge(sem("pv1_mm"), w - 1)
                    act.copy(pT1[:, w % 2, :, :].rearrange("p h q -> p (h q)"),
                             PP[2][:, :, :].rearrange("p a q -> p (a q)")).then_inc(sem("pT1"), 1)
                w = k - 2
                if 0 <= w < NT:
                    eng.wait_ge(sem("pv1_mm"), w + 1)
                    if w >= 2:
                        eng.wait_ge(sem("ot1_mm"), w - 1)
                    act.copy(os1[:, w % 2, :, :].rearrange("p a q -> p (a q)"), bank(6)[:, 0:2 * P])\
                       .then_inc(sem("os1"), 1)
                if k == NT - 1:
                    oT_evac(0, 0, 0)
            oT_evac(0, 1, 1)
            norm_evac(1, 0)
            mlp_act(0, W("bff1_1"))

            eng.wait_ge(sem("turns"), 1)
            act.activation(ei[:, :], tA[:, :], ACT.Sin, scale=TWO_PI).then_inc(sem("rot"), 1)
            eng.wait_ge(sem("turns"), 2)
            act.activation(er[:, :], tB[:, :], ACT.Sin, scale=-TWO_PI, bias=W("halfpi")).then_inc(sem("rot"), 1)
            eng.wait_ge(sem("bbar_tr"), 1)
            act.copy(bbT[:, :], bank(0)[:, 0:P]).then_inc(sem("bbT"), 1)
            for b in range(B):
                norm_evac(2, b)
            mlp_act(1, W("bff1_2"))

            for b in range(B):
                norm_evac(4, b)
            for b in range(B):
                for n in range(2 * b, 2 * b + 2):
                    eng.wait_ge(sem("qkT3_mm"), n + 1)
                    act.copy(split[:, n, 0, :], bank(n)).then_inc(sem("split1"), 1)
                for n in range(2 * b, 2 * b + 2):
                    eng.wait_ge(sem("res3"), n + 1)
                    act.copy(split[:, n, 1, :], res3[:, n, :]).then_inc(sem("split2"), 1)

            def l3_exp(u, hp, s):
                eng.wait_ge(sem("st3"), u * 4 + s + 1)
                if s == 0 and not (isinstance(u, int) and u < 2):
                    eng.wait_ge(sem("pv3_mm"), u - 1)
                act.activation(p3[:, hp, s // 2, 2 * (s % 2):2 * (s % 2) + 2, :], PP[1 + s % 2][:, :, :], ACT.Exp,
                               scale=float(D3) ** -0.5).then_inc(sem("exp3"), 1)

            def l3_mT(u, hp):
                eng.wait_ge(sem("m3_tr"), u + 1)
                act.copy(mT3[:, hp, :], bank(7)[0:3 * 2 * NB, 2 * P:2 * P + P // 2].bitcast(BF16))\
                    .then_inc(sem("mT3"), 1)

            def l3_out(u, hp):
                eng.wait_ge(sem("pv3_mm"), u + 1)
                if isinstance(u, int) and u >= 2:
                    eng.wait_ge(sem("ot3_mm"), u - 1)
                act.copy(os3[:, hp, :], bank(6)[:, hp * 2 * P:(hp + 1) * 2 * P]).then_inc(sem("os3"), 1)

            def l3_slot(u, hp, turn=True, values=True):
                for s in range(4):
                    l3_exp(u, hp, s)
                    if s == 1 and turn:
                        l3_mT(u + 1, 1 - hp)
                if values:
                    l3_out(u - 1, 1 - hp)

            l3_mT(0, 0)
            l3_slot(0, 0, values=False)
            l3_slot(1, 1)
            with eng.Fori(1, NIT - 1) as it:
                l3_slot(it * 2, 0)
                l3_slot(it * 2 + 1, 1)
            l3_slot(UNITS - 2, 0)
            oT_evac(1, 0, 0)
            l3_slot(UNITS - 1, 1, turn=False)
            l3_out(UNITS - 1, 1)
            oT_evac(1, 1, 6)
            norm_evac(5, 0)
            for k in range(8):
                c = k % 4
                if k == 3:
                    norm_evac(5, 1)
                eng.wait_ge(sem("fc_mm"), 2 * k + 1)
                if k >= 2:
                    eng.wait_ge(sem("gT"), 16 + k - 1)
                act.activation(sg3[:, k % 2, :], bank(2 * (k % 2) + 1), ACT.Silu, bias=W("bfc")[:, 4 + c:5 + c])\
                   .then_inc(sem("sg3"), 1)

        @block.gpsimd
        def _(eng):
            def tt(o, a, b, op):
                return pool.tensor_tensor(o, a, b, op)

            pool.memset(ones[:, :], 1.0).then_inc(sem("consts"), 1)
            pool.memset(mhalf[:, :], -0.5).then_inc(sem("consts"), 1)
            pool.memset(zeros[:, :], 0.0).then_inc(sem("consts"), 1)
            pool.memset(ms3[:, 3:, :], 0.0).then_inc(sem("consts"), 1)
            eng.wait_ge(sem("ld_w0"), 16)
            pool.tensor_copy(bc_cond[:, :, :], W("cond").unsqueeze(2).to_broadcast([P, B, P])).then_inc(sem("bcast"), 1)
            eng.wait_ge(sem("silu_c"), 1)
            pool.tensor_copy(bc_silu[:, :, :], silu_c[:, :].unsqueeze(2).to_broadcast([P, B, P])).then_inc(sem("bcast"), 1)
            for b in range(B):
                eng.wait_ge(sem("sfT"), b + 1)
                pool.tensor_copy(kvrep[b][:, :, :],
                                 sfT[:, b * T:b * T + M0].unsqueeze(1).to_broadcast([P, NC0 * HC, M0]))\
                    .then_inc(sem("kvrep"), 1)

            eng.wait_ge(sem("adj_f"), 1)
            tt(adj_w[1][:, :, :], adj_w[1][:, :, :], W("wbias0").unsqueeze(1).to_broadcast([P, NT * M0, L]), ALU.mult)\
                .then_inc(sem("mprod1"), 1)

            def l0_sub(g):
                eng.wait_ge(sem("mx0"), g + 1)
                v = w0p[:, g % 4, :, :].rearrange("p t (h m) -> p (t h) m", m=M0)
                tt(v, v, mx0[:, g % 4, :].unsqueeze(2).to_broadcast([P, 2 * H0, M0]), ALU.subtract)\
                    .then_inc(sem("sub0"), 1)

            def l0_norm(g):
                eng.wait_ge(sem("rs0"), g + 1)
                v = w0p[:, g % 4, :, :].rearrange("p t (h m) -> p (t h) m", m=M0)
                tt(v, v, rs0[:, g % 4, :].unsqueeze(2).to_broadcast([P, 2 * H0, M0]), ALU.mult)\
                    .then_inc(sem("w0n"), 1)

            for k in range(8 + 1):
                if k < 8:
                    l0_sub(k)
                if k >= 1:
                    l0_norm(k - 1)

            pool.memset(v1[:, :, :, D1:PAD], 0.0).then_inc(sem("ones_v"), 1)
            eng.wait_ge(sem("ones_v"), 1)
            pool.memset(v1[:, :, :, D1:D1 + 1], 1.0).then_inc(sem("ones_v"), 1)

            eng.wait_ge(sem("ld_w1"), 16)
            eng.wait_ge(sem("ld_w2"), 16)
            eng.wait_ge(sem("rows"), NROWS)
            eng.wait_ge(sem("gate"), B)

            def gcols(b, j, n=None):
                g = gate[:, b, j * P:(j + 1) * P]
                return g if n is None else g.unsqueeze(1).to_broadcast([P, n, P])

            for b in range(B):
                tt(wout1g[:, b, :], W("wout1"), gcols(b, 0), ALU.mult).then_inc(sem("gated_w"), 1)
            for b in range(B):
                tt(bres[:, 0, b, :], W("rout1"), gcols(b, 0), ALU.mult).then_inc(sem("gated_b"), 1)

            def residual(n, bias):
                use = {0: 0, 1: 1, 2: 3, 3: 4, 4: 5}[n]
                for b in range(B):
                    if use == 0:
                        eng.wait_ge(sem("x0"), b + 1)
                    else:
                        eng.wait_ge(sem("xr"), 2 * (use - 1) + b + 1)
                    tt(Xb[:, btiles(b), :], X[:, btiles(b), :], bias(b).unsqueeze(1).to_broadcast([P, NB, P]), ALU.add)\
                        .then_inc(sem("xb"), 1)

            def norm_pow(n):
                for b in range(B):
                    eng.wait_ge(sem("var"), 2 * n + b + 1)
                    if n == 0 and b == 0:
                        eng.wait_ge(sem("consts"), 2)
                    tt(rstd[:, btiles(b)], var[:, btiles(b)], mhalf[:, btiles(b)], ALU.pow).then_inc(sem("rstd"), 1)

            norm_pow(0)
            eng.wait_ge(sem("gated_b"), 2)
            residual(0, lambda b: bres[:, 0, b, :])
            tt(steps[:, :].rearrange("p (a c) -> p a c", c=16), W("steps_hi").unsqueeze(2).to_broadcast([P, T // 16, 16]),
               W("steps_lo").unsqueeze(1).to_broadcast([P, T // 16, 16]), ALU.add).then_inc(sem("steps"), 1)

            for w in range(NT):
                eng.wait_ge(sem("qkT1"), 2 * (w // NB + 1))
                if w >= 2:
                    eng.wait_ge(sem("s1_mm"), w - 1)
                tt(kb1[:, w % 2, :, :], kT1[:, tile_cols(w)].unsqueeze(1).to_broadcast([P, H1, P]),
                   W("kmask1").unsqueeze(2).to_broadcast([P, H1, P]), ALU.mult).then_inc(sem("kb1"), 1)
            for b in range(B):
                tt(wff2g[0][:, b, :, :], W("wff2_1").rearrange("p (c f) -> p c f", c=4), gcols(b, 1, 4), ALU.mult)\
                    .then_inc(sem("gated_w"), 1)
            for b in range(B):
                tt(bres[:, 1, b, :], W("rff2_1"), gcols(b, 1), ALU.mult).then_inc(sem("gated_b"), 1)
            norm_pow(1)
            eng.wait_ge(sem("gated_b"), 4)
            residual(1, lambda b: bres[:, 1, b, :])
            for b in range(B):
                tt(wff2g[1][:, b, :, :], W("wff2_2").rearrange("p (c f) -> p c f", c=4), gcols(b, 3, 4), ALU.mult)\
                    .then_inc(sem("gated_w"), 1)
            for b in range(B):
                tt(bres[:, 2, b, :], W("rff2_2"), gcols(b, 3), ALU.mult).then_inc(sem("gated_b"), 1)
            pool.memset(v3[:, :, :, :, D3:PAD], 0.0).then_inc(sem("ones_v"), 1)
            eng.wait_ge(sem("ones_v"), 3)
            pool.memset(v3[:, :, :, :, D3:D3 + 1], 1.0).then_inc(sem("ones_v"), 1)
            eng.wait_ge(sem("ld_w3"), 16)
            for name, wide in (("cos3", cos3), ("sin3", sin3)):
                pool.tensor_copy(wide[:, :, :, :], W(name).rearrange("p (w c) -> p w c", w=NB).unsqueeze(2)
                                 .to_broadcast([P, NB, 2 * NG3, D3])).then_inc(sem("wide3"), 1)
            norm_pow(2)
            norm_pow(3)
            eng.wait_ge(sem("gated_b"), 6)
            residual(2, lambda b: bres[:, 2, b, :])
            eng.wait_ge(sem("xb"), 6)
            for j in range(2):
                pool.memset(qa[j][64:P, :, :], 0.0).then_inc(sem("zero3"), 1)
                pool.memset(ka[j][64:P, :, :], 0.0).then_inc(sem("zero3a"), 1)
            eng.wait_ge(sem("zero3a"), 2)
            for j in range(2):
                pool.memset(ka[j][AUG:AUG + 3, :, :], 1.0).then_inc(sem("zero3"), 1)
            eng.wait_ge(sem("zero3"), 4)
            pool.tensor_copy(identb[:, :], ident).then_inc(sem("identb"), 1)
            norm_pow(4)
            residual(3, lambda b: W("rao"))

            def values(it, par):
                if not (isinstance(it, int) and it < 2):
                    eng.wait_ge(sem("pv3_mm"), it * 2 - 2)
                pool.tensor_copy(vg[par][:, :, :, :].rearrange("p w h c -> p (w h c)"),
                                 v3[:, :, :, :, :].rearrange("p i w h c -> p (i w h c)")[:, bass.ds(it * 512, 512)])\
                    .then_inc(sem("vg"), 1)

            def l3_split_max(u, hp):
                eng.wait_ge(sem("max3"), u * 8 + 8)
                if not (isinstance(u, int) and u == 0):
                    eng.wait_ge(sem("m3_tr"), u)
                tt(ms3[:, 0, :], nm3[:, hp, :], zeros[:, :], ALU.add).then_inc(sem("ms3_t"), 1)
                eng.wait_ge(sem("ms3_t"), u * 3 + 1)
                tt(nr3[:, :], nm3[:, hp, :], ms3[:, 0, :], ALU.subtract).then_inc(sem("ms3_t"), 1)
                eng.wait_ge(sem("ms3_t"), u * 3 + 2)
                tt(ms3[:, 1, :], nr3[:, :], zeros[:, :], ALU.add).then_inc(sem("ms3_t"), 1)
                eng.wait_ge(sem("ms3_t"), u * 3 + 3)
                tt(ms3[:, 2, :], nr3[:, :], ms3[:, 1, :], ALU.subtract).then_inc(sem("ms3"), 1)

            eng.wait_ge(sem("vv"), 2 * NT)
            eng.wait_ge(sem("ones_v"), 4)
            values(0, 0)
            values(1, 1)
            for n in range(2, 2 * B):
                third_part(tt, eng, n)
            eng.wait_ge(sem("consts"), 3)
            for u in range(4):
                l3_split_max(u, u % 2)
            with eng.Fori(1, NIT // 2) as pair:
                for j in range(2):
                    l3_split_max(pair * 4 + 2 * j, 0)
                    values(pair * 2 + j, j)
                    l3_split_max(pair * 4 + (2 * j + 1), 1)
            norm_pow(5)
            residual(4, lambda b: W("rfo"))

        @block.vector
        def _(eng):
            def tt(o, a, b, op):
                return dve.tensor_tensor(o, a, b, op)

            ssm_done = [0]

            def did(ins):
                ssm_done[0] += 1
                ins.then_inc(sem("ssm_step"), 1)
                eng.wait_ge(sem("ssm_step"), ssm_done[0])

            def c(j):
                return col[:, j:j + 1]

            def ts(o, i, s1, s2, op0, op1=None):
                return dve.tensor_scalar(o, i, s1, s2, op0) if op1 is None else dve.tensor_scalar(o, i, s1, s2, op0, op1)

            def stt(o, i, s, j, op0, op1):
                return dve.scalar_tensor_tensor(out=o, in0=i, scalar=s, in1=j, op0=op0, op1=op1)

            def ssm_angles(part):
                t = steps[:, :]
                if part == 0:
                    did(tt(c(3), W("lam_im"), c(0), ALU.mult))
                    did(ts(c(4), c(3), 1.0 / TWO_PI, ROUND, ALU.mult, ALU.add))
                    did(ts(c(4), c(4), -ROUND, None, ALU.add))
                    did(stt(c(5), c(4), -TURN[0], c(3), ALU.mult, ALU.add))
                elif part == 1:
                    did(stt(c(5), c(4), -TURN[1], c(5), ALU.mult, ALU.add))
                    did(stt(c(5), c(4), -TURN[2], c(5), ALU.mult, ALU.add))
                    did(ts(c(6), c(5), 1.0 / TWO_PI, None, ALU.mult))
                    did(ts(c(22), c(6), 0.4999999, -0.4999999, ALU.min, ALU.max))
                    stt(c(23), c(22), -1.0, c(22), ALU.mult, ALU.max).then_inc(sem("turn1"), 1)
                    did(ts(c(7), c(6), ROUND12, ROUND12, ALU.add, ALU.subtract))
                elif part == 2:
                    did(tt(c(8), c(6), c(7), ALU.subtract))
                    eng.wait_ge(sem("steps"), 1)
                    did(ts(tA[:, :], t, c(7), None, ALU.mult))
                elif part == 3:
                    did(ts(tB[:, :], tA[:, :], ROUND, ROUND, ALU.add, ALU.subtract))
                    did(tt(tA[:, :], tA[:, :], tB[:, :], ALU.subtract))
                elif part == 4:
                    did(stt(tA[:, :], t, c(8), tA[:, :], ALU.mult, ALU.add))
                elif part == 5:
                    did(ts(tB[:, :], tA[:, :], ROUND, ROUND, ALU.add, ALU.subtract))
                    did(tt(tA[:, :], tA[:, :], tB[:, :], ALU.subtract))
                elif part == 6:
                    ts(tA[:, :], tA[:, :], 0.4999999, -0.4999999, ALU.min, ALU.max).then_inc(sem("turns"), 1)
                    eng.wait_ge(sem("turns"), 1)
                    stt(tB[:, :], tA[:, :], -1.0, tA[:, :], ALU.mult, ALU.max).then_inc(sem("turns"), 1)

            def ssm_inputs():
                eng.wait_ge(sem("ld_w2"), 16)
                lre, lim = W("lam_re"), W("lam_im")
                eng.wait_ge(sem("rho"), 1)
                eng.wait_ge(sem("rot1"), 2)
                did(ts(c(9), c(25), c(2), -1.0, ALU.mult, ALU.add))
                did(tt(c(10), c(24), c(2), ALU.mult))
                did(tt(c(11), lre, lre, ALU.mult))
                did(stt(c(12), lim, lim, c(11), ALU.mult, ALU.add))
                did(dve.reciprocal(c(13), c(12)))
                did(tt(c(14), c(9), lre, ALU.mult))
                did(stt(c(15), c(10), lim, c(14), ALU.mult, ALU.add))
                did(tt(c(16), c(15), c(13), ALU.mult))
                did(tt(c(17), c(9), lim, ALU.mult))
                did(stt(c(18), c(10), lre, c(17), ALU.mult, ALU.subtract))
                did(tt(c(19), c(18), c(13), ALU.mult))
                did(tt(c(20), c(16), W("sa"), ALU.mult))
                did(tt(c(21), c(19), W("sb"), ALU.mult))
                did(ts(bbar[:, :], W("bx"), c(20), None, ALU.mult))
                stt(bbar[:, :], W("by"), c(21), bbar[:, :], ALU.mult, ALU.add).then_inc(sem("bbar"), 1)
                for b in range(B):
                    g = gate[:, b, 2 * P:3 * P]
                    stt(cga[:, b, :], W("cta"), W("sign1")[:, b:b + 1], g, ALU.mult, ALU.mult).then_inc(sem("cg"), 1)
                    stt(cgb[:, b, :], W("ctb"), W("sign2")[:, b:b + 1], g, ALU.mult, ALU.mult).then_inc(sem("cg"), 1)
                    stt(dg[:, b, :], ident, W("dcol"), g, ALU.mult, ALU.mult).then_inc(sem("cg"), 1)

            def l0_blocks():
                tt(bout_sum[:, :], W("bout0")[:, 0:1], W("bout0")[:, 1:2], ALU.add).then_inc(sem("bout_sum"), 1)
                eng.wait_ge(sem("kh_mm"), 4)
                for n in range(4):
                    d = n % 2
                    dve.scalar_tensor_tensor(
                        out=kblk[n][:, :, :], in0=bank(6)[:, 32 * n:32 * n + M0].unsqueeze(1).to_broadcast([P, H0, M0]),
                        scalar=W("bk0")[:, d:d + 1], in1=W("kmask0").unsqueeze(2).to_broadcast([P, H0, M0]),
                        op0=ALU.add, op1=ALU.mult).then_inc(sem("kblk"), 1)

            def l0_value_blocks():
                for n in range(4):
                    eng.wait_ge(sem("vf_mm"), n + 1)
                    tt(vblk[n][:, :, :].rearrange("r c (h e) -> r (c h) e", h=H0),
                       bank(4 + n)[0:RC, 0:NC0 * P].rearrange("r (k e) -> r k e", e=P // H0),
                       W("vmask0")[0:RC, :].unsqueeze(2).to_broadcast([RC, NC0 * H0, P // H0]), ALU.mult)\
                        .then_inc(sem("vblk"), 1)

            def l0_tiles(src, g):
                b, d, h = g // 4, (g // 2) % 2, g % 2
                i = b * NB + 2 * h
                return src[:, d, i * M0:(i + 2) * M0].rearrange("p (t m) -> p t m", t=2).unsqueeze(2)\
                    .to_broadcast([P, 2, H0, M0])

            def flat(g):
                return w0p[:, g % 4, :, :].rearrange("p t (h m) -> p (t h) m", m=M0)

            def l0_bias(g):
                eng.wait_ge(sem("s0_mm"), g + 1)
                eng.wait_ge(sem("mtb"), (g // 2) % 2 + 1)
                if g >= 4:
                    eng.wait_ge(sem("w0_tr"), g - 3)
                tt(w0p[:, g % 4, :, :].rearrange("p t (h m) -> p t h m", m=M0),
                   PP[g % 2][:, :, 0:H0 * M0].rearrange("p t (h m) -> p t h m", m=M0),
                   l0_tiles(mtb, g), ALU.add).then_inc(sem("s0_m"), 1)

            def l0_max(g):
                eng.wait_ge(sem("s0_m"), g + 1)
                dve.tensor_reduce(mx0[:, g % 4, :], flat(g), X_AXIS, ALU.max).then_inc(sem("mx0"), 1)

            def l0_sum(g):
                eng.wait_ge(sem("exp0"), g + 1)
                dve.tensor_reduce(sm0[:, g % 4, :], flat(g), X_AXIS, ALU.add).then_inc(sem("sm0"), 1)
                eng.wait_ge(sem("sm0"), g + 1)
                dve.reciprocal(rs0[:, g % 4, :], sm0[:, g % 4, :]).then_inc(sem("rs0"), 1)

            def l0_final(b):
                k = 6 + b
                eng.wait_ge(sem("o0_mm"), b + 1)
                eng.wait_ge(sem("bout_sum"), 1)
                dve.scalar_tensor_tensor(out=l0sum[:, b, :], in0=bank(k), scalar=bout_sum[:, :], in1=sfT[:, half(b)],
                                         op0=ALU.add, op1=ALU.add).then_inc(sem("l0sum"), 1)
                eng.wait_ge(sem("l0sum"), b + 1)
                dve.scalar_tensor_tensor(out=xoT[:, half(b)], in0=l0sum[:, b, :], scalar=0.0, in1=xT[:, half(b)],
                                         op0=ALU.max, op1=ALU.add).then_inc(sem("l0x"), 1)

            eng.wait_ge(sem("ld_w0"), 16)
            eng.wait_ge(sem("dt"), 1)
            tt(c(1), W("lam_re"), c(0), ALU.mult).then_inc(sem("rho_in"), 1)
            for b in range(B):
                ssm_angles(b)
                eng.wait_ge(sem("rowsum"), b + 1)
                dve.tensor_scalar(keep[:, half(b)], bank(6 + b)[0:1, :], 0.0, None, ALU.not_equal)\
                   .then_inc(sem("keep"), 1)
            for d in range(2):
                a = adj[d][:, :].rearrange("p (n l) -> p n l", l=L)
                eng.wait_ge(sem(f"ld_adj{d}"), 16)
                dve.tensor_reduce(msum[:, d, :], a, X_AXIS, ALU.add).then_inc(sem("msum"), 1)
                eng.wait_ge(sem("msum"), d + 1)
                dve.tensor_scalar(mpen[:, d, :], msum[:, d, :], 0.0, NEG, ALU.is_le, ALU.mult).then_inc(sem("mpen"), 1)
            for d in range(2):
                if d == 0:
                    eng.wait_ge(sem("rows"), 1)
                    tt(adj_w[0][:, :, :], adj[0][:, :].rearrange("p (n l) -> p n l", l=L),
                       W("wbias0").unsqueeze(1).to_broadcast([P, NT * M0, L]), ALU.mult).then_inc(sem("mprod0"), 1)
                eng.wait_ge(sem(f"mprod{d}"), 1)
                dve.tensor_reduce(mbias[:, d, :], adj_w[d][:, :, :], X_AXIS, ALU.add).then_inc(sem("mbias"), 1)
                eng.wait_ge(sem("mbias"), d + 1)
                eng.wait_ge(sem("mpen"), d + 1)
                dve.scalar_tensor_tensor(out=mtb[:, d, :], in0=mbias[:, d, :], scalar=W("bbias0"), in1=mpen[:, d, :],
                                         op0=ALU.add, op1=ALU.add).then_inc(sem("mtb"), 1)
                if d == 0:
                    l0_blocks()
                    l0_value_blocks()
                    for g in range(2):
                        l0_bias(g)
                        l0_max(g)
            mod_done = [0]

            def mod_did(ins):
                mod_done[0] += 1
                ins.then_inc(sem("mod_step"), 1)
                eng.wait_ge(sem("mod_step"), mod_done[0])

            def modulation():
                eng.wait_ge(sem("mod_mm"), 1)
                eng.wait_ge(sem("rows"), NROWS)
                tt(modc[:, :, :], bank(4)[:, 0:24].rearrange("p (j b) -> p j b", b=B),
                   W("bmod").unsqueeze(2).to_broadcast([P, 12, B]), ALU.add).then_inc(sem("modc"), 1)
                eng.wait_ge(sem("sgt"), 1)
                eng.wait_ge(sem("modc"), 1)
                tt(tpe[:, :], modc[:, 10, :], sgt[:, :], ALU.mult).then_inc(sem("tpe"), 1)
                for b in range(B):
                    eng.wait_ge(sem("gate_mm"), b + 1)
                    tt(gate[:, b, :], bank(5 + b), W("rgate"), ALU.add).then_inc(sem("gate"), 1)
                eng.wait_ge(sem("modd_mm"), 1)
                tt(modd[:, :, :], bank(7)[:, 0:8].rearrange("p (j b) -> p j b", b=B),
                   W("bmodd").unsqueeze(2).to_broadcast([P, 4, B]), ALU.add).then_inc(sem("modd"), 1)

            def norm_factors():
                eng.wait_ge(sem("modd"), 1)
                mod_did(dve.tensor_scalar(modp[:, :, :], modc[:, :, :], 1.0, None, ALU.add))
                mod_did(dve.tensor_scalar(modq[:, :, :], modd[:, :, :], 1.0, None, ALU.add))
                mod_did(dve.tensor_scalar(scl[:, 0, :], modp[:, 1, :], W("s1a"), None, ALU.mult))
                mod_did(dve.tensor_scalar(scl[:, 1, :], modp[:, 3, :], W("s1b"), None, ALU.mult))
                mod_did(dve.tensor_copy(scl[:, 2, :], modp[:, 5, :]))
                mod_did(tt(scl[:, 3, :], modp[:, 8, :], modp[:, 7, :], ALU.mult))
                mod_did(dve.tensor_scalar(scl[:, 4, :], modq[:, 1, :], W("g3a"), None, ALU.mult))
                mod_did(dve.tensor_scalar(scl[:, 5, :], modq[:, 3, :], W("g3b"), None, ALU.mult))
                mod_did(dve.tensor_copy(shf[:, 0, :], modc[:, 0, :]))
                mod_did(dve.tensor_copy(shf[:, 1, :], modc[:, 2, :]))
                mod_did(dve.tensor_copy(shf[:, 2, :], modc[:, 4, :]))
                mod_did(tt(shtmp[:, :], modc[:, 9, :], modp[:, 7, :], ALU.mult))
                mod_did(tt(shf[:, 3, :], shtmp[:, :], modc[:, 6, :], ALU.add))
                mod_did(dve.tensor_copy(shf[:, 4, :], modd[:, 0, :]))
                dve.tensor_copy(shf[:, 5, :], modd[:, 2, :]).then_inc(sem("scl"), 1)

            for k in range(8 + 2):
                if 2 <= k < 8:
                    l0_bias(k)
                if k == 3:
                    modulation()
                if 3 <= k <= 8:
                    l0_max(k - 1)
                if k == 8:
                    l0_final(0)
                if k >= 2:
                    l0_sum(k - 2)
            norm_factors()

            def norm_stats(n, b, centred):
                if n == 0:
                    eng.wait_ge(sem("x0"), b + 1)
                else:
                    eng.wait_ge(sem("xr"), 2 * (n - 1) + b + 1)
                for w in range(NB):
                    i = b * NB + w
                    dve.bn_stats(st[:, i, :], X[:, i, :]).then_inc(sem("stats"), 1)
                eng.wait_ge(sem("stats"), NT * n + NB * (b + 1))
                for w in range(NB):
                    i = b * NB + w
                    dve.bn_aggr(mv[:, i, :], st[:, i, :]).then_inc(sem("aggr"), 1)
                eng.wait_ge(sem("aggr"), NT * n + NB * (b + 1))
                bt = btiles(b)
                eps = 1e-5 if n < 4 else 1.1920928955078125e-07
                if centred:
                    dve.tensor_scalar(var[:, bt], mv[:, bt, 1], eps, None, ALU.add).then_inc(sem("var"), 1)
                else:
                    tt(msq[:, bt], mv[:, bt, 0], mv[:, bt, 0], ALU.mult).then_inc(sem("msq"), 1)
                    eng.wait_ge(sem("msq"), 2 * {0: 0, 1: 1, 4: 2, 5: 3}[n] + b + 1)
                    dve.scalar_tensor_tensor(out=var[:, bt], in0=msq[:, bt], scalar=eps, in1=mv[:, bt, 1],
                                             op0=ALU.add, op1=ALU.add).then_inc(sem("var"), 1)

            def norm_apply(n, b, centred):
                eng.wait_ge(sem("rstd"), 2 * n + b + 1)
                if n:
                    eng.wait_ge(sem("norm_tr"), 2 * (n - 1) + b + 1)
                for w in range(NB):
                    i = b * NB + w
                    if centred:
                        ins = dve.tensor_scalar(xn[:, i, :], X[:, i, :], mv[:, i, 0:1], rstd[:, i:i + 1],
                                                ALU.subtract, ALU.mult)
                    else:
                        ins = dve.tensor_scalar(xn[:, i, :], X[:, i, :], rstd[:, i:i + 1], None, ALU.mult)
                    ins.then_inc(sem("xn"), 1)

            def add_residual(u, done, k, b):
                base = X if u == 2 else Xb
                eng.wait_ge(sem(done[0]), done[1] + b + 1)
                if u != 2:
                    eng.wait_ge(sem("xb"), 2 * {0: 0, 1: 1, 3: 2, 4: 3, 5: 4}[u] + b + 1)
                else:
                    eng.wait_ge(sem("xn"), NT * 3)
                tt(X[:, btiles(b), :].rearrange("p w f -> p (w f)"), bank(k),
                   base[:, btiles(b), :].rearrange("p w f -> p (w f)"), ALU.add).then_inc(sem("xr"), 1)

            def residual_norm(u, done, k, centred, together=False):
                add_residual(u, done, k, 0)
                norm_stats(u + 1, 0, centred)
                if together:
                    add_residual(u, done, k + 1, 1)
                norm_apply(u + 1, 0, centred)
                if not together:
                    add_residual(u, done, k + 1, 1)
                norm_stats(u + 1, 1, centred)
                norm_apply(u + 1, 1, centred)

            def l1_qkv(b):
                for i in range(b * NB, (b + 1) * NB):
                    eng.wait_ge(sem("qkv_mm"), i + 1)
                    tt(qk[:, i, :], bank(qkv_bank(i))[:, 0:2 * P], W("rqkv1")[:, 0:2 * P], ALU.add).then_inc(sem("qk"), 1)
                    tt(v1[:, i, :, 0:D1], bank(qkv_bank(i))[:, 2 * P:3 * P].rearrange("p (h c) -> p h c", h=H1),
                       W("rqkv1")[:, 2 * P:3 * P].rearrange("p (h c) -> p h c", h=H1), ALU.add).then_inc(sem("vv"), 1)

            def l1_rope_products(b):
                eng.wait_ge(sem("qk"), NB * (b + 1))
                v = qk[:, btiles(b), :].rearrange("p w (h c) -> p (w h) c", c=D1)
                r1 = rt1[:, btiles(b), :].rearrange("p w (h c) -> p (w h) c", c=D1)
                r2 = rt2[:, btiles(b), :].rearrange("p w (h c) -> p (w h) c", c=D1)
                n, hd = NB * 2 * H1, D1 // 2
                tt(r1, v, W("cos1").unsqueeze(1).to_broadcast([P, n, D1]), ALU.mult).then_inc(sem("rope_t"), 1)
                tt(r2[:, :, 0:hd], v[:, :, hd:D1], W("sin1")[:, 0:hd].unsqueeze(1).to_broadcast([P, n, hd]), ALU.mult)\
                    .then_inc(sem("rope_t"), 1)
                tt(r2[:, :, hd:D1], v[:, :, 0:hd], W("sin1")[:, hd:D1].unsqueeze(1).to_broadcast([P, n, hd]), ALU.mult)\
                    .then_inc(sem("rope_t"), 1)

            def l1_rope_sum(b):
                eng.wait_ge(sem("rope_t"), 3 * (b + 1))
                tt(qk[:, btiles(b), :], rt1[:, btiles(b), :], rt2[:, btiles(b), :], ALU.add).then_inc(sem("rope"), 1)

            norm_stats(0, 0, False)
            norm_apply(0, 0, False)
            l0_final(1)
            norm_stats(0, 1, False)
            l1_qkv(0)
            norm_apply(0, 1, False)
            l1_rope_products(0)
            l1_rope_sum(0)
            l1_qkv(1)
            l1_rope_products(1)
            for k in range(NT + 4):
                w = k
                if w < NT:
                    eng.wait_ge(sem("s1_mm"), w + 1)
                    s = PP[w % 2][:, :, :].rearrange("p a (h k) -> p (a h) k", k=P)
                    dve.tensor_reduce(mx1[:, w % 2, :], s, X_AXIS, ALU.max).then_inc(sem("mx1"), 1)
                    eng.wait_ge(sem("mx1"), w + 1)
                    if w >= 2:
                        eng.wait_ge(sem("p1_tr"), w - 1)
                    tt(p1[:, w % 2, :, :], s, mx1[:, w % 2, :].unsqueeze(2).to_broadcast([P, H1, P]), ALU.subtract)\
                        .then_inc(sem("sub1"), 1)
                if k == 0:
                    l1_rope_sum(1)
                if 5 <= k < 10:
                    ssm_angles(k - 3)
                w = k - 4
                if 0 <= w < NT:
                    eng.wait_ge(sem("ot1_mm"), w + 1)
                    o = bank(7)[:, 0:2 * P].rearrange("p (h c) -> p h c", c=PAD)
                    dve.reciprocal(rc1[:, w % 2, :], o[:, :, D1]).then_inc(sem("rc1"), 1)
                    eng.wait_ge(sem("rc1"), w + 1)
                    tt(otok[:, w, :].rearrange("p (h c) -> p h c", c=D1), o[:, :, 0:D1],
                       rc1[:, w % 2, :].unsqueeze(2).to_broadcast([P, H1, D1]), ALU.mult).then_inc(sem("otok1"), 1)
                if k == NT + 1:
                    add_residual(0, ("proj_mm", 0), 2, 0)
                if k == NT + 2:
                    norm_stats(1, 0, False)
                if k == NT + 3:
                    norm_apply(1, 0, False)
            add_residual(0, ("proj_mm", 0), 7, 1)
            norm_stats(1, 1, False)
            norm_apply(1, 1, False)
            ssm_inputs()

            residual_norm(1, ("down_mm", 0), 6, True)
            eng.wait_ge(sem("u_mm"), 1)
            eng.wait_ge(sem("rot"), 2)
            tt(ua[:, :], bank(2), er[:, :], ALU.mult).then_inc(sem("rotin"), 1)
            tt(ub[:, :], bank(3), ei[:, :], ALU.mult).then_inc(sem("rotin"), 1)
            eng.wait_ge(sem("rotin"), 2)
            tt(uw[:, :], ua[:, :], ub[:, :], ALU.add).then_inc(sem("scan_in"), 1)
            eng.wait_ge(sem("scan_in"), 1)
            eng.wait_ge(sem("rho"), 1)
            dve.tensor_tensor_scan(xs[:, :], col[:, 2:3].to_broadcast([P, T]), uw[:, :], 0.0, ALU.mult, ALU.add)\
               .then_inc(sem("scan"), 1)
            eng.wait_ge(sem("scan"), 1)
            tt(uw[:, :], xs[:, :], er[:, :], ALU.mult).then_inc(sem("rotout"), 1)
            tt(uw2[:, :], xs[:, :], ei[:, :], ALU.mult).then_inc(sem("rotout"), 1)
            residual_norm(2, ("y_mm", 0), 6, True, together=True)

            def l3_qkv(b, tiles=range(NB)):
                for w in tiles:
                    i = b * NB + w
                    eng.wait_ge(sem("qkv_mm"), NT + i + 1)
                    tt(qk[:, i, :], bank(qkv_bank(i))[:, 0:2 * P], W("rqkv3")[:, 0:2 * P], ALU.add).then_inc(sem("qk"), 1)
                    tt(v3[:, btiles(b), w, :, 0:D3],
                       bank(qkv_bank(i))[:, 2 * P:3 * P].rearrange("p (g h c) -> p g h c", g=NG3, h=G3),
                       W("rqkv3")[:, 2 * P:3 * P].rearrange("p (g h c) -> p g h c", g=NG3, h=G3), ALU.add)\
                        .then_inc(sem("vv"), 1)

            def l3_rope(b):
                eng.wait_ge(sem("qk"), NT + NB * (b + 1))
                eng.wait_ge(sem("wide3"), 2)
                v = qk[:, btiles(b), :].rearrange("p w (r c) -> p (w r) c", c=G3)
                r1 = rt1[:, btiles(b), :].rearrange("p w (r c) -> p (w r) c", c=G3)
                r2 = rt2[:, btiles(b), :].rearrange("p w (r c) -> p (w r) c", c=G3)
                n = NB * 2 * NG3 * D3
                cos, sin = (t[:, :, :, :].rearrange("p w g c -> p (w g c)") for t in (cos3, sin3))
                tt(r1, v, cos.unsqueeze(2).to_broadcast([P, n, G3]), ALU.mult).then_inc(sem("rope_t3"), 1)
                for e in range(2):
                    tt(r2[:, e:n:2, :], v[:, 1 - e:n:2, :], sin[:, e:n:2].unsqueeze(2).to_broadcast([P, n // 2, G3]),
                       ALU.mult).then_inc(sem("rope_t3"), 1)
                eng.wait_ge(sem("rope_t3"), 3 * (b + 1))
                tt(v, r1, r2, ALU.add).then_inc(sem("rope3"), 1)

            def l3_rests(n):
                eng.wait_ge(sem("split1"), n + 1)
                tt(res3[:, n, :], bank(n), split[:, n, 0, :], ALU.subtract).then_inc(sem("res3"), 1)

            for b in range(B):
                add_residual(3, ("down_mm", 2), 6 + b, b)
                norm_stats(4, b, False)
                if b == 0:
                    norm_apply(4, 0, False)
            l3_qkv(0)
            norm_apply(4, 1, False)
            l3_rope(0)
            l3_qkv(1, range(0, 2))
            l3_rests(0)
            l3_rests(1)
            l3_qkv(1, range(2, 3))
            for n in range(2):
                third_part(tt, eng, n)
            l3_qkv(1, range(3, NB))
            l3_rope(1)
            l3_rests(2)
            l3_rests(3)

            def l3_maxima(u, hp, j):
                eng.wait_ge(sem("s3_mm"), u * 8 + j + 1)
                dve.tensor_reduce(nm3[:, hp, j:j + 1], bank(j % 2), X_AXIS, ALU.max, negate=True)\
                    .then_inc(sem("max3"), 1)

            def l3_tokens(u):
                eng.wait_ge(sem("ot3_mm"), u + 1)
                o = bank(7)[:, 0:2 * P].rearrange("p (w h c) -> p w h c", w=NB, h=2)
                dve.reciprocal(rc3[:, :, :], o[:, :, :, D3]).then_inc(sem("rc3"), 1)
                eng.wait_ge(sem("rc3"), u + 1)
                tt(o3[:, :, :, :].rearrange("p w i f -> p w (i f)")[:, :, bass.ds(u * (2 * D3), 2 * D3)]
                   .rearrange("p w (h c) -> p w h c", h=2),
                   o[:, :, :, 0:D3], rc3[:, :, :].unsqueeze(3).to_broadcast([P, NB, 2, D3]), ALU.mult)\
                    .then_inc(sem("otok3"), 1)

            def l3_slot(u, hp, ahead=True, tokens=True):
                if ahead:
                    for j in range(8):
                        if j == 6 and tokens:
                            l3_tokens(u - 2)
                        l3_maxima(u + 2, hp, j)
                else:
                    l3_tokens(u - 2)

            for u in range(2):
                for j in range(8):
                    l3_maxima(u, u, j)
            l3_slot(0, 0, tokens=False)
            l3_slot(1, 1, tokens=False)
            with eng.Fori(1, NIT - 1) as it:
                l3_slot(it * 2, 0)
                l3_slot(it * 2 + 1, 1)
            l3_slot(UNITS - 2, 0, ahead=False)
            l3_slot(UNITS - 1, 1, ahead=False)
            add_residual(4, ("proj_mm", 2), 1, 0)
            norm_stats(5, 0, False)
            l3_slot(UNITS, 0, ahead=False)
            l3_slot(UNITS + 1, 1, ahead=False)
            norm_apply(5, 0, False)
            add_residual(4, ("proj_mm", 2), 7, 1)
            norm_stats(5, 1, False)
            for k in range(8):
                b, c = k // 4, k % 4
                if k == 1:
                    norm_apply(5, 1, False)
                eng.wait_ge(sem("fc_mm"), 2 * k + 2)
                eng.wait_ge(sem("sg3"), k + 1)
                dve.scalar_tensor_tensor(out=gT[:, c, half(b)], in0=bank(2 * (k % 2)), scalar=W("bfc")[:, c:c + 1],
                                         in1=sg3[:, k % 2, :], op0=ALU.add, op1=ALU.mult).then_inc(sem("gT"), 1)
            for b in range(B):
                add_residual(5, ("down_mm", 4), 6 + b, b)


def _pack(spec, parts):
    import numpy as np
    cols = []
    for name, width in spec.items():
        a = parts[name]
        a = np.asarray(a, np.float32).reshape(a.shape[0], -1)
        assert a.shape[1] == width, name
        if a.shape[0] < P:
            a = np.concatenate([a, np.zeros((P - a.shape[0], width), np.float32)])
        cols.append(a)
    return np.ascontiguousarray(np.concatenate(cols, 1))


def _rope_angles(n, dim):
    import numpy as np
    inv = np.float32(1.0) / np.float32(10000.0) ** (np.arange(0, dim, 2, dtype=np.float32) / np.float32(dim))
    return np.arange(n, dtype=np.float32)[:, None] * inv[None, :].astype(np.float32)


def _layout(inp):
    import numpy as np
    f = {k: np.asarray(v) for k, v in inp.items()}
    z = {}

    def chunks(w, ids):
        return np.concatenate([w[:, P * j:P * (j + 1)] for j in ids], 1)

    def rows_to_cols(v, ids=None):
        v = v.reshape(-1, P)
        return (v if ids is None else v[list(ids)]).T

    def stacked(w):
        return w.reshape(4, P, P).transpose(1, 0, 2)

    p = np.arange(P)
    z["ident"] = np.eye(P)
    ws = f["L0_cond_W_self"]
    z["wsv"], z["wsq"] = ws[:, :D].T, ws[:, D:].T
    z["wq"] = f["L0_cond_Wq"].transpose(2, 0, 1)
    z["wk"] = f["L0_cond_Wk"].transpose(2, 0, 1)
    z["wo"] = f["L0_cond_Wout"].reshape(2, P, D).transpose(2, 0, 1)
    z["kmask0"] = (p[:, None] // 8 == np.arange(H0)) * np.float32(1 / np.sqrt(8))
    r = np.arange(RC)
    z["vmask0"] = np.stack([HC * c + r[:, None] // M0 == np.arange(H0) for c in range(NC0)], 1)
    z["bself"] = rows_to_cols(f["L0_cond_b_self"])
    z["bq0"], z["bk0"], z["bout0"] = f["L0_cond_bq"].T, f["L0_cond_bk"].T, f["L0_cond_bout"].T
    z["cond"] = f["cond_1024"].T

    ada, bada = f["L1_cond_W_ada"], f["L1_cond_b_ada"]
    wm, bm = f["L2_cond_Wm"], f["L2_cond_bm"]
    wc, bc = f["L2_cond_Wc"], f["L2_cond_bc"]
    z["wcol1"], z["wgate1"] = chunks(ada, (0, 1, 3, 4)), chunks(ada, (2, 5))
    z["wt1"] = f["L3_cond_w_t1"]
    z["wqkv1"], z["wout1"], z["wff1_1"] = f["L1_cond_W_qkv"], f["L1_cond_W_out"], f["L1_cond_W_ff1"]
    z["wff2_1"] = stacked(f["L1_cond_W_ff2"])
    z["kmask1"] = p[:, None] // D1 == np.arange(H1)
    ang = _rope_angles(P, D1)
    z["cos1"] = np.repeat(np.cos(ang), 2, 1)
    z["sin1"] = np.repeat(np.sin(ang), 2, 1) * np.where(np.arange(D1) < D1 // 2, -1.0, 1.0)
    z["bff1_1"] = rows_to_cols(f["L1_cond_b_ff1"])
    z["bmod"] = np.concatenate([rows_to_cols(bada, (0, 1, 3, 4)), rows_to_cols(bm, (0, 1, 3, 4)),
                                rows_to_cols(bc), rows_to_cols(f["L3_cond_b_t1"])], 1)
    z["bmodd"] = rows_to_cols(f["L3_cond_b_t2"])
    z["s1a"], z["s1b"] = rows_to_cols(f["L1_cond_scale1"]), rows_to_cols(f["L1_cond_scale2"])
    z["g3a"], z["g3b"] = rows_to_cols(f["L3_cond_g1"]), rows_to_cols(f["L3_cond_g2"])

    z["wcol2"] = np.concatenate([chunks(wm, (0, 1, 3, 4)), wc], 1)
    z["wgate2"] = chunks(wm, (2, 5))
    z["wff1_2"], z["wff2_2"] = f["L2_cond_W1"], stacked(f["L2_cond_W2"])
    bre, bim, cre, cim = (f["L2_cond_" + n] for n in ("B_re", "B_im", "C_re", "C_im"))
    z["bx"] = np.concatenate([bre, bim, bim, bre])
    z["by"] = np.concatenate([bim, bre, bre, bim])
    z["cta"] = np.concatenate([cre.T, cim.T] * 2)
    z["ctb"] = np.concatenate([cim.T, cre.T] * 2)
    z["steps_hi"] = np.tile(16 * np.arange(T // 16), (P, 1))
    z["steps_lo"] = np.tile(np.arange(16), (P, 1))
    for n in ("lam_re", "lam_im", "log_step"):
        src = f["L2_cond_" + {"lam_re": "Lam_re", "lam_im": "Lam_im", "log_step": "log_step"}[n]]
        z[n] = np.tile(src, 4)[:, None]
    q = p // 32
    z["sa"] = np.where(q == 3, -1.0, 1.0)[:, None]
    z["sb"] = np.where(q == 0, -1.0, 1.0)[:, None]
    own = (p[:, None] // 64 == np.arange(B)[None, :])
    z["sign1"] = own * np.where(q % 2 == 0, 2.0, -2.0)[:, None]
    z["sign2"] = own * -2.0
    z["dcol"] = rows_to_cols(f["L2_cond_D_diag"])
    z["bff1_2"] = rows_to_cols(f["L2_cond_b1"])
    z["halfpi"] = np.full((P, 1), np.pi / 2)

    hd, g, c = np.meshgrid(np.arange(D3), np.arange(NG3), np.arange(G3), indexing="ij")
    perm = np.empty(P, int)
    perm[(g * 32 + hd * G3 + c).ravel()] = ((g * G3 + c) * D3 + hd).ravel()
    wqkv, bqkv = f["L3_cond_w_qkv"], f["L3_cond_b_qkv"]
    order = np.concatenate([perm, P + perm, 2 * P + np.arange(P)])
    z["wcol3"], z["wqkv3"], z["wao"] = f["L3_cond_w_t2"], wqkv[:, order], f["L3_cond_w_ao"]
    z["wfc"], z["wfo"] = f["L3_cond_w_fc"], stacked(f["L3_cond_w_fo"])
    ang = _rope_angles(T, D3).reshape(NB, P, D3 // 2).transpose(1, 0, 2)
    sign = np.where(np.arange(D3) % 2 == 0, -1.0, 1.0)
    z["cos3"] = np.repeat(np.cos(ang), 2, 2)
    z["sin3"] = np.repeat(np.sin(ang), 2, 2) * sign
    z["bfc"] = rows_to_cols(f["L3_cond_b_fc"])

    z["wbias0"], z["bbias0"] = f["L0_cond_w_bias"][None], f["L0_cond_b_bias"].reshape(1, 1)
    z["rgate"] = np.concatenate([bada.reshape(6, P)[[2, 5]].ravel(), bm.reshape(6, P)[[2, 5]].ravel()])[None]
    z["rqkv1"], z["rout1"], z["rff2_1"] = (f["L1_cond_" + n][None] for n in ("b_qkv", "b_out", "b_ff2"))
    z["rff2_2"] = f["L2_cond_b2"][None]
    z["rqkv3"], z["rao"], z["rfo"] = bqkv[order][None], f["L3_cond_b_ao"][None], f["L3_cond_b_fo"][None]

    adj = f["mask_BxSxSx11_ik0"]
    adj = [adj[:, :, :M0, :], adj[:, :M0, :, :].transpose(0, 2, 1, 3)]
    adj = np.stack([a.reshape(NT, P, M0 * L).transpose(1, 0, 2).reshape(P, NT * M0 * L) for a in adj])
    return {
        "w0": _pack(W0, z), "wm": _pack(WM, z), "w1": _pack(W1, z), "w2": _pack(W2, z), "w3": _pack(W3, z),
        "rows": np.concatenate([z[n].reshape(1, -1) for n in ROWS], 1).astype(np.float32),
        "xt": np.ascontiguousarray(f["x"].reshape(B * T, D).T),
        "adj": np.ascontiguousarray(adj),
    }


def kernel(**inputs):
    import numpy as np
    import concourse.bacc as bacc
    from concourse.bass_utils import run_bass_kernel_spmd

    nc = bacc.Bacc("TRN2", target_bir_lowering=False, num_devices=1)
    arrays = _layout(inputs)
    args = [nc.dram_tensor(n, arrays[n].shape, mybir.dt.from_np(arrays[n].dtype), kind="ExternalInput").ap()
            for n in ("w0", "wm", "w1", "w2", "w3", "rows", "xt", "adj")]
    out = nc.dram_tensor("out", (P, B * T), F32, kind="ExternalOutput").ap()
    q_scr = nc.dram_tensor("q_scr", (NIT, 3, 32, T), BF16, kind="Internal").ap()
    k_scr = nc.dram_tensor("k_scr", (NIT, 5, 32, T), BF16, kind="Internal").ap()
    build_program(nc, *args, out, q_scr, k_scr)
    r = run_bass_kernel_spmd(nc, [arrays], core_ids=[0])
    y = np.asarray(r.results[0]["out"]).reshape(P, NT, D)
    return np.ascontiguousarray(y.transpose(1, 0, 2)).reshape(B, T, D)
```
